# Optimizing a Trainium2 kernel written in Bass

```python
import numpy as np
import jax
import jax.numpy as jnp

def _softmax(x, axis=-1):
    return jax.nn.softmax(x, axis=axis)

def _gelu(x):
    return jax.nn.gelu(x, approximate=True)

def _silu(x):
    return jax.nn.silu(x)

def _sigmoid(x):
    return jax.nn.sigmoid(x)

def _layernorm(x, axis=-1, eps=1e-05):
    m = jnp.mean(x, axis=axis, keepdims=True)
    v = jnp.var(x, axis=axis, keepdims=True)
    return (x - m) / jnp.sqrt(v + eps)

def _scatter_add(tgt, idx, src, axis=0):
    return tgt.at[idx].add(src)

def _segment_sum(src, seg, n):
    return jax.ops.segment_sum(src, seg, n)
kernel_name = 'mk_macaron_d1_jaxref_r4_de105f'

def setup_inputs(seed: int=0):
    np.random.seed(seed)
    _w = jnp.asarray

    def _L0_attn_setup():
        import math
        import jax, jax.numpy as jnp
        import numpy as np
        H = 32
        NOPE = 64
        ROPE = 64
        VD = 128
        QHD = NOPE + ROPE
        KVR = 64
        EPS = 1e-06

        def _yarn_cos_sin(seq_len, dim=ROPE, base=10000.0, factor=128.0, beta_fast=32.0, beta_slow=1.0, orig_max=2048, mscale=1.0, mscale_all_dim=1.0):

            def corr_dim(r):
                return dim * math.log(orig_max / (r * 2 * math.pi)) / (2 * math.log(base))
            low = max(math.floor(corr_dim(beta_fast)), 0)
            high = min(math.ceil(corr_dim(beta_slow)), dim - 1)
            hi = high + 0.001 if low == high else float(high)
            ramp = np.clip((np.arange(dim // 2, dtype=np.float32) - low) / (hi - low), 0.0, 1.0)
            inv_freq_mask = 1.0 - ramp
            freq_extra = 1.0 / base ** (np.arange(0, dim, 2, dtype=np.float32) / dim)
            freq_inter = freq_extra / factor
            inv_freq = freq_inter * (1.0 - inv_freq_mask) + freq_extra * inv_freq_mask
            t = np.arange(seq_len, dtype=np.float32)
            freqs = np.outer(t, inv_freq)
            emb = np.concatenate([freqs, freqs], axis=-1)

            def gm(s, m):
                return 1.0 if s <= 1 else 0.1 * m * math.log(s) + 1.0
            ms = gm(factor, mscale) / gm(factor, mscale_all_dim)
            return (jnp.asarray(np.cos(emb) * ms), jnp.asarray(np.sin(emb) * ms))

        def _rmsnorm(x, w, eps=EPS):
            var = jnp.mean(jnp.square(x), axis=-1, keepdims=True)
            return x * jax.lax.rsqrt(var + eps) * w

        def _deinterleave(x):
            d = x.shape[-1]
            x = x.reshape(*x.shape[:-1], d // 2, 2)
            return jnp.concatenate([x[..., 0], x[..., 1]], axis=-1)

        def _rotate_half(x):
            d = x.shape[-1] // 2
            return jnp.concatenate([-x[..., d:], x[..., :d]], axis=-1)

        def _apply_rope(x, cos, sin):
            return x * cos + _rotate_half(x) * sin
        key = jax.random.key(seed)
        ks = jax.random.split(key, 6)
        B, S, D = (1, 512, 1024)
        std = 0.02
        return {'x': jax.random.normal(ks[0], (B, S, D), dtype=jnp.float32), 'wq_a': jax.random.normal(ks[1], (256, D), dtype=jnp.float32) * std, 'q_a_ln_w': jnp.ones((256,), dtype=jnp.float32), 'wq_b': jax.random.normal(ks[2], (H * QHD, 256), dtype=jnp.float32) * std, 'wkv_a': jax.random.normal(ks[3], (KVR + ROPE, D), dtype=jnp.float32) * std, 'kv_a_ln_w': jnp.ones((KVR,), dtype=jnp.float32), 'wkv_b': jax.random.normal(ks[4], (H * (NOPE + VD), KVR), dtype=jnp.float32) * std, 'wo': jax.random.normal(ks[5], (D, H * VD), dtype=jnp.float32) * std}
    _L0_attn_in = _L0_attn_setup()

    def _L0_ffn_setup():
        import jax, jax.numpy as jnp
        import numpy as np
        LORA_RANK = 16
        LORA_ALPHA = 16
        LORA_SCALE = LORA_ALPHA / LORA_RANK
        key = jax.random.key(seed)
        k1, k2, k3, k4, k5 = jax.random.split(key, 5)
        B, S, D_IN, D_OUT, N_LORA, R = (8, 512, 1024, 1024, 3, LORA_RANK)
        std = 1.0 / np.sqrt(D_IN)
        x = jax.random.normal(k1, (B, S, D_IN), dtype=jnp.float32)
        weight = jax.random.truncated_normal(k2, -3.0, 3.0, (D_OUT, D_IN), dtype=jnp.float32) * std
        bias = jax.random.normal(k3, (D_OUT,), dtype=jnp.float32) * 0.01
        lora_A = jax.random.normal(k4, (N_LORA, R, D_IN), dtype=jnp.float32) * std
        lora_B = jax.random.normal(k5, (N_LORA, D_OUT, R), dtype=jnp.float32) * 0.02
        lora_start_indices = jnp.arange(4, dtype=jnp.int64) * 2
        return {'x': x, 'weight': weight, 'bias': bias, 'lora_A': lora_A, 'lora_B': lora_B, 'lora_start_indices': lora_start_indices}
    _L0_ffn_in = _L0_ffn_setup()
    _d = {'L0_attn_x': _L0_attn_in['x'], 'L0_attn_wq_a': _L0_attn_in['wq_a'], 'L0_attn_q_a_ln_w': _L0_attn_in['q_a_ln_w'], 'L0_attn_wq_b': _L0_attn_in['wq_b'], 'L0_attn_wkv_a': _L0_attn_in['wkv_a'], 'L0_attn_kv_a_ln_w': _L0_attn_in['kv_a_ln_w'], 'L0_attn_wkv_b': _L0_attn_in['wkv_b'], 'L0_attn_wo': _L0_attn_in['wo'], 'L0_ffn_weight': _L0_ffn_in['weight'], 'L0_ffn_bias': _L0_ffn_in['bias'], 'L0_ffn_lora_A': _L0_ffn_in['lora_A'], 'L0_ffn_lora_B': _L0_ffn_in['lora_B'], 'L0_ffn_lora_start_indices': _L0_ffn_in['lora_start_indices']}
    _x0 = _d['L0_attn_x']
    _d['L0_attn_x'] = jax.random.normal(jax.random.fold_in(jax.random.key(seed), 1), (2, 1024, 1024), dtype=_x0.dtype)
    del _x0
    return _d

def reference(L0_attn_x, L0_attn_wq_a, L0_attn_q_a_ln_w, L0_attn_wq_b, L0_attn_wkv_a, L0_attn_kv_a_ln_w, L0_attn_wkv_b, L0_attn_wo, L0_ffn_weight, L0_ffn_bias, L0_ffn_lora_A, L0_ffn_lora_B, L0_ffn_lora_start_indices):

    def _L0_attn_ref(x, wq_a, q_a_ln_w, wq_b, wkv_a, kv_a_ln_w, wkv_b, wo):
        import math
        import jax, jax.numpy as jnp
        import numpy as np
        H = 32
        NOPE = 64
        ROPE = 64
        VD = 128
        QHD = NOPE + ROPE
        KVR = 64
        EPS = 1e-06

        def _yarn_cos_sin(seq_len, dim=ROPE, base=10000.0, factor=128.0, beta_fast=32.0, beta_slow=1.0, orig_max=2048, mscale=1.0, mscale_all_dim=1.0):

            def corr_dim(r):
                return dim * math.log(orig_max / (r * 2 * math.pi)) / (2 * math.log(base))
            low = max(math.floor(corr_dim(beta_fast)), 0)
            high = min(math.ceil(corr_dim(beta_slow)), dim - 1)
            hi = high + 0.001 if low == high else float(high)
            ramp = np.clip((np.arange(dim // 2, dtype=np.float32) - low) / (hi - low), 0.0, 1.0)
            inv_freq_mask = 1.0 - ramp
            freq_extra = 1.0 / base ** (np.arange(0, dim, 2, dtype=np.float32) / dim)
            freq_inter = freq_extra / factor
            inv_freq = freq_inter * (1.0 - inv_freq_mask) + freq_extra * inv_freq_mask
            t = np.arange(seq_len, dtype=np.float32)
            freqs = np.outer(t, inv_freq)
            emb = np.concatenate([freqs, freqs], axis=-1)

            def gm(s, m):
                return 1.0 if s <= 1 else 0.1 * m * math.log(s) + 1.0
            ms = gm(factor, mscale) / gm(factor, mscale_all_dim)
            return (jnp.asarray(np.cos(emb) * ms), jnp.asarray(np.sin(emb) * ms))

        def _rmsnorm(x, w, eps=EPS):
            var = jnp.mean(jnp.square(x), axis=-1, keepdims=True)
            return x * jax.lax.rsqrt(var + eps) * w

        def _deinterleave(x):
            d = x.shape[-1]
            x = x.reshape(*x.shape[:-1], d // 2, 2)
            return jnp.concatenate([x[..., 0], x[..., 1]], axis=-1)

        def _rotate_half(x):
            d = x.shape[-1] // 2
            return jnp.concatenate([-x[..., d:], x[..., :d]], axis=-1)

        def _apply_rope(x, cos, sin):
            return x * cos + _rotate_half(x) * sin
        B, S, D = x.shape
        m = 0.1 * 1.0 * math.log(128.0) + 1.0
        softmax_scale = QHD ** (-0.5) * m * m
        q = _rmsnorm(x @ wq_a.T, q_a_ln_w) @ wq_b.T
        q = q.reshape(B, S, H, QHD)
        q_nope, q_pe = (q[..., :NOPE], q[..., NOPE:])
        ckv_kpe = x @ wkv_a.T
        ckv, k_pe = (ckv_kpe[..., :KVR], ckv_kpe[..., KVR:])
        kv = _rmsnorm(ckv, kv_a_ln_w) @ wkv_b.T
        kv = kv.reshape(B, S, H, NOPE + VD)
        k_nope, v = (kv[..., :NOPE], kv[..., NOPE:])
        cos, sin = _yarn_cos_sin(S)
        q_pe = _apply_rope(_deinterleave(q_pe), cos[None, :, None, :], sin[None, :, None, :])
        k_pe = _apply_rope(_deinterleave(k_pe), cos[None, :, :], sin[None, :, :])
        q_full = jnp.concatenate([q_nope, q_pe], axis=-1)
        k_full = jnp.concatenate([k_nope, jnp.broadcast_to(k_pe[:, :, None, :], (B, S, H, ROPE))], axis=-1)
        scores = jnp.einsum('bqhd,bkhd->bhqk', q_full, k_full) * softmax_scale
        causal = jnp.tril(jnp.ones((S, S), dtype=bool))
        scores = jnp.where(causal[None, None], scores, jnp.finfo(scores.dtype).min)
        attn = jax.nn.softmax(scores, axis=-1)
        out = jnp.einsum('bhqk,bkhd->bqhd', attn, v).reshape(B, S, H * VD)
        return out @ wo.T

    def _L0_ffn_ref(x, weight, bias, lora_A, lora_B, lora_start_indices):
        import jax, jax.numpy as jnp
        import numpy as np
        LORA_RANK = 16
        LORA_ALPHA = 16
        LORA_SCALE = LORA_ALPHA / LORA_RANK
        y = jnp.einsum('bsd,od->bso', x, weight) + bias
        B = x.shape[0]
        seg = jnp.searchsorted(lora_start_indices, jnp.arange(B), side='right') - 1
        adapter_idx = jnp.clip(seg - 1, 0, lora_A.shape[0] - 1)
        A = lora_A[adapter_idx]
        Bw = lora_B[adapter_idx]
        lo = jnp.einsum('bsr,bor->bso', jnp.einsum('bsd,brd->bsr', x, A), Bw) * LORA_SCALE
        use_lora = (seg > 0)[:, None, None]
        return y + jnp.where(use_lora, lo, jnp.zeros((), dtype=y.dtype))
    x = L0_attn_x
    x = x + 0.5 * _L0_ffn_ref(_layernorm(x, axis=-1), L0_ffn_weight, L0_ffn_bias, L0_ffn_lora_A, L0_ffn_lora_B, L0_ffn_lora_start_indices)
    x = x + _L0_attn_ref(_layernorm(x, axis=-1), L0_attn_wq_a, L0_attn_q_a_ln_w, L0_attn_wq_b, L0_attn_wkv_a, L0_attn_kv_a_ln_w, L0_attn_wkv_b, L0_attn_wo)
    x = x + 0.5 * _L0_ffn_ref(_layernorm(x, axis=-1), L0_ffn_weight, L0_ffn_bias, L0_ffn_lora_A, L0_ffn_lora_B, L0_ffn_lora_start_indices)
    return x

_drawn_inputs = setup_inputs


def setup_inputs(seed=0):
    import zlib

    import numpy as np

    out = dict(_drawn_inputs(seed))
    spreads = {'L0_attn_q_a_ln_w': (1.0, 0.6), 'L0_attn_kv_a_ln_w': (1.0, 0.6)}
    factors = {'L0_attn_wq_a': 8.0,
     'L0_attn_wq_b': 8.0,
     'L0_attn_wkv_a': 4.153,
     'L0_attn_wkv_b': 4.23,
     'L0_attn_wo': 4.31,
     'L0_ffn_bias': 8.0}
    for name, (base, spread) in spreads.items():
        noise = np.random.default_rng([zlib.crc32(name.encode()), seed]).standard_normal(out[name].shape)
        drawn = base * np.exp(spread * noise) if base else spread * noise
        out[name] = jnp.asarray(drawn.astype(out[name].dtype))
    for name, factor in factors.items():
        out[name] = (out[name] * factor).astype(out[name].dtype)
    return out
```

```python
from contextlib import ExitStack

import numpy as np

import concourse.bass as bass
from concourse import mybir

ALU = mybir.AluOpType
ACT = mybir.ActivationFunctionType
AX_X = mybir.AxisListType.X
F32 = mybir.dt.float32
F32R = mybir.dt.float32r
BF16 = mybir.dt.bfloat16
I32 = mybir.dt.int32

P = 128
BANK = 512
B, S, D = 2, 1024, 1024
T = B * S
NT = T // P
DT = D // P
H = 32
PAIRS = H // 2
NOPE, ROPE, VD = 64, 64, 128
QHD = NOPE + ROPE
KVR = 64
QR = 256
QRT = QR // P
LAT = QR + KVR + ROPE
RANK = 16
ADAPTERS = 3
STARTS = 4
QT = S // P
CHUNK = 512
MSCALE = 0.1 * 1.0 * float(np.log(128.0)) + 1.0
SCALE = QHD ** -0.5 * MSCALE * MSCALE
LN_EPS = 1e-5
RMS_EPS = 1e-6
MASKED = -3.0e38

HI, LO = 0, 1
PASSES = ((HI, HI), (LO, HI), (HI, LO))


class Ctx:

    def __init__(self, nc, stack):
        self.nc, self.stack = nc, stack

    def sb(self, name, shape, dt=F32):
        return self.stack.enter_context(self.nc.sbuf_tensor(name, shape, dt))

    def ps(self, name, shape, dt=F32):
        return self.stack.enter_context(self.nc.psum_tensor(name, shape, dt))

    def sem(self, name):
        return self.stack.enter_context(self.nc.semaphore(name))


def steady(eng, body, steps, lead, lag=0, start=None):
    first = 4
    rounds = (steps - lead) // 2
    for n in range(-lead if start is None else start, first):
        body(n, n % 2, lambda m, n=n: 0 <= n + m < steps)
    with eng.Fori(first // 2, rounds) as r:
        for j in range(2):
            body(r * 2 + j, j, lambda m: True)
    for n in range(2 * rounds, steps + lag):
        body(n, n % 2, lambda m, n=n: 0 <= n + m < steps)


def later(n, least):
    return not isinstance(n, int) or n >= least



def constants_phase(nc, k):
    with ExitStack() as stack:
        c = Ctx(nc, stack)
        cleared, made = c.sem("c_cleared"), c.sem("c_made")
        block = stack.enter_context(nc.Block())

        @block.gpsimd
        def _(pool):
            nc.gpsimd.memset(k.ident[:], 0.0).then_inc(cleared, 1)
            nc.gpsimd.memset(k.ident_bf[:], 0.0).then_inc(cleared, 1)
            nc.gpsimd.memset(k.mask_bf[:], 0.0).then_inc(cleared, 1)
            nc.gpsimd.memset(k.eps_ln[:], LN_EPS)
            nc.gpsimd.memset(k.eps_rms[:], RMS_EPS)
            pool.wait_ge(cleared, 3)
            for m in (k.ident, k.ident_bf):
                nc.gpsimd.affine_select(out=m[:], in_=m[:], compare_op=ALU.not_equal, fill=1.0, base=0,
                                        pattern=[[-1, P]], channel_multiplier=1).then_inc(made, 1)
            nc.gpsimd.affine_select(out=k.mask_bf[:], in_=k.mask_bf[:], compare_op=ALU.is_ge, fill=MASKED, base=0,
                                    pattern=[[-1, P]], channel_multiplier=1).then_inc(made, 1)
            pool.wait_ge(made, 3)



def ffn_weights_phase(nc, tag, w, lora, weff, bias_half, args):
    w_d, bias_d, a_d, b_d, starts_d = args
    with ExitStack() as stack:
        c = Ctx(nc, stack)
        a_all = c.sb(tag + "a_all", [P, ADAPTERS, D])
        b_all = c.sb(tag + "b_all", [P, ADAPTERS, D])
        starts = c.sb(tag + "starts", [P, STARTS], I32)
        startf = c.sb(tag + "startf", [P, STARTS])
        hit = c.sb(tag + "hit", [P, B, STARTS])
        count = c.sb(tag + "count", [P, B])
        chosen = c.sb(tag + "chosen", [P, B, ADAPTERS], I32)
        sel = c.sb(tag + "sel", [P, 2, D])
        rounded = c.sb(tag + "rounded", [P, 2, D], F32R)
        a_st = c.sb(tag + "a_st", [P, B, D], F32R)
        b_st = c.sb(tag + "b_st", [P, B, D], F32R)
        w_in = c.sb(tag + "w_in", [P, 2, D])
        w_sum = c.sb(tag + "w_sum", [P, 2, D])
        ps = c.ps(tag + "ps_w", [P, 2, 2, BANK])
        cleared, lora_in, small_in = c.sem(tag + "cleared"), c.sem(tag + "lora_in"), c.sem(tag + "small_in")
        w_loaded = [c.sem(tag + f"w_loaded{j}") for j in range(2)]
        chain = c.sem(tag + "chain")
        stacked, outer, summed = c.sem(tag + "stacked"), c.sem(tag + "outer"), c.sem(tag + "summed")
        hi_done, lo_pool, lo_dve = c.sem(tag + "hi_done"), c.sem(tag + "lo_pool"), c.sem(tag + "lo_dve")
        block = stack.enter_context(nc.Block())

        @block.sync
        def _(sp):
            sp.dma_start(starts[:], starts_d.rearrange("(a n) -> a n", a=1).to_broadcast([P, STARTS])).then_inc(small_in, 16)
            sp.dma_start(bias_half[:], bias_d.rearrange("(a n) -> a n", a=1).to_broadcast([P, D])).then_inc(small_in, 16)
            sp.wait_ge(cleared, 2)
            for g in range(4):
                for tile, src in ((a_all, a_d), (b_all, b_d)):
                    sp.dma_start(tile[32 * g:32 * g + RANK, :, :], src.rearrange("a r d -> r a d")).then_inc(lora_in, 16)
            for dt in range(DT):
                if dt >= 2:
                    sp.wait_ge(summed, B * (dt - 1))
                sp.dma_start(w_in[:, dt % 2, :], w_d[:, dt * D:(dt + 1) * D]).then_inc(w_loaded[dt % 2], 16)

        @block.gpsimd
        def _(pool):
            nc.gpsimd.memset(a_all[:], 0.0).then_inc(cleared, 1)
            nc.gpsimd.memset(b_all[:], 0.0).then_inc(cleared, 1)
            for dt in range(DT):
                pool.wait_ge(hi_done, B * dt + 1)
                nc.gpsimd.tensor_tensor(weff[:, 0, LO, dt, :], w_sum[:, 0, :], weff[:, 0, HI, dt, :].bitcast(F32),
                                        ALU.subtract).then_inc(lo_pool, 1)

        @block.tensor
        def _(pe):
            pe.wait_ge(stacked, 2 * B)
            for dt in range(DT):
                for b in range(B):
                    if dt >= 1:
                        pe.wait_ge(summed, B * (dt - 1) + b + 1)
                    for half in range(2):
                        nc.tensor.matmul(ps[:, b, half, :], a_st[:, b, dt * P:(dt + 1) * P],
                                         b_st[:, b, half * BANK:(half + 1) * BANK], start=True, stop=True).then_inc(outer, 1)

        @block.scalar
        def _(act):
            for dt in range(DT):
                for b in range(B):
                    act.wait_ge(summed, B * dt + b + 1)
                    nc.scalar.activation(weff[:, b, HI, dt, :], w_sum[:, b, :], ACT.Copy).then_inc(hi_done, 1)

        @block.vector
        def _(dve):
            links = [0]

            def link(ins):
                links[0] += 1
                ins.then_inc(chain, 1)
                dve.wait_ge(chain, links[0])

            dve.wait_ge(small_in, 32)
            link(nc.vector.tensor_copy(startf[:], starts[:]))
            link(nc.vector.tensor_scalar(bias_half[:], bias_half[:], 0.5, None, ALU.mult))
            for b in range(B):
                link(nc.vector.tensor_scalar(hit[:, b, :], startf[:], float(b), None, ALU.is_le))
                link(nc.vector.reduce_sum(count[:, b:b + 1], hit[:, b, :], AX_X))
                for a in range(ADAPTERS):
                    op = ALU.is_ge if a == ADAPTERS - 1 else ALU.is_equal
                    link(nc.vector.tensor_scalar(chosen[:, b, a:a + 1], count[:, b:b + 1], float(a + 2), None, op))
            dve.wait_ge(lora_in, 16 * 8)
            for b in range(B):
                link(nc.vector.memset(sel[:], 0.0))
                for a in range(ADAPTERS):
                    m = chosen[:, b, a:a + 1].to_broadcast([P, D])
                    link(nc.vector.copy_predicated(sel[:, 0, :], m, a_all[:, a, :]))
                    link(nc.vector.copy_predicated(sel[:, 1, :], m, b_all[:, a, :]))
                link(nc.vector.tensor_copy(rounded[:], sel[:]))
                link(nc.vector.tensor_copy(a_st[0:64, b, :], sel[0:64, 0, :]))
                link(nc.vector.tensor_tensor(a_st[64:128, b, :], sel[64:128, 0, :], rounded[64:128, 0, :].bitcast(F32), ALU.subtract))
                for g in range(4):
                    r = slice(32 * g, 32 * g + 32)
                    if g % 2 == 0:
                        ins = nc.vector.tensor_copy(b_st[r, b, :], sel[r, 1, :])
                    else:
                        ins = nc.vector.tensor_tensor(b_st[r, b, :], sel[r, 1, :], rounded[r, 1, :].bitcast(F32), ALU.subtract)
                    if g < 3:
                        link(ins)
                ins.then_inc(stacked, 2)
                dve.wait_ge(stacked, 2 * b + 2)
            for dt in range(DT):
                dve.wait_ge(w_loaded[dt % 2], 16 * (dt // 2 + 1))
                for b in range(B):
                    if dt >= 1:
                        dve.wait_ge(hi_done, B * (dt - 1) + b + 1)
                        if b == 0:
                            dve.wait_ge(lo_pool, dt)
                        else:
                            dve.wait_ge(lo_dve, dt)
                    dve.wait_ge(outer, 2 * (B * dt + b) + 2)
                    nc.vector.tensor_tensor(w_sum[:, b, :], ps[:, b, :, :].rearrange("p a n -> p (a n)"),
                                            w_in[:, dt % 2, :], ALU.add).then_inc(summed, 1)
                dve.wait_ge(hi_done, B * dt + 2)
                nc.vector.tensor_tensor(weff[:, 1, LO, dt, :], w_sum[:, 1, :], weff[:, 1, HI, dt, :].bitcast(F32),
                                        ALU.subtract).then_inc(lo_dve, 1)


class Front:

    def __init__(self, c, tag):
        self.xt = c.sb(tag + "xt", [P, 2, D])
        self.xn = c.sb(tag + "xn", [P, 2, D])
        self.xT = c.sb(tag + "xT", [P, 2, 2, DT, P], F32R)
        self.st = c.sb(tag + "st", [P, 2, 12])
        self.mv = c.sb(tag + "mv", [P, 2, 2])
        self.std = c.sb(tag + "std", [P, 2, 1])
        self.rstd = c.sb(tag + "rstd", [P, 2, 1])
        self.ps = c.ps(tag + "ps_xT", [P, 2, BANK])
        self.x_in = [c.sem(tag + f"x_in{j}") for j in range(2)]
        self.stats, self.var, self.root = c.sem(tag + "stats"), c.sem(tag + "var"), c.sem(tag + "root")
        self.passed = c.sem(tag + "passed")
        self.inv, self.normed = c.sem(tag + "inv"), c.sem(tag + "normed")
        self.turned, self.hi, self.lo = c.sem(tag + "turned"), c.sem(tag + "hi"), c.sem(tag + "lo")

    def stats_of(self, nc, dve, n, j, loads):
        dve.wait_ge(self.x_in[j], loads)
        nc.vector.bn_stats(self.st[:, j, 0:6], self.xt[:, j, 0:512])
        nc.vector.bn_stats(self.st[:, j, 6:12], self.xt[:, j, 512:1024]).then_inc(self.stats, 1)
        dve.wait_ge(self.stats, n + 1)
        dve.sem_inc(self.passed, 1)
        nc.vector.bn_aggr(self.mv[:, j, :], self.st[:, j, :]).then_inc(self.var, 1)

    def root_of(self, nc, act, eps, n, j):
        act.wait_ge(self.var, n + 1)
        nc.scalar.activation(self.std[:, j, :], self.mv[:, j, 1:2], ACT.Sqrt, bias=eps, scale=1.0).then_inc(self.root, 1)

    def normalise(self, nc, dve, n, j):
        dve.wait_ge(self.root, n + 1)
        nc.vector.reciprocal(self.rstd[:, j, :], self.std[:, j, :]).then_inc(self.inv, 1)
        dve.wait_ge(self.inv, n + 1)
        nc.vector.tensor_scalar(self.xn[:, j, :], self.xt[:, j, :], self.mv[:, j, 0:1], self.rstd[:, j, :],
                                ALU.subtract, ALU.mult).then_inc(self.normed, 1)

    def turn(self, nc, pe, ident, n, j):
        pe.wait_ge(self.normed, n + 1)
        for g in range(2):
            if later(n, 1):
                pe.wait_ge(self.lo, n * 2 + g - 1)
            for q in range(4):
                ins = nc.tensor.transpose(self.ps[:, g, q * P:(q + 1) * P],
                                          self.xn[:, j, (4 * g + q) * P:(4 * g + q + 1) * P], ident[:])
            ins.then_inc(self.turned, 1)

    def split_hi(self, nc, act, n, j, product, per_tile):
        if later(n, 2):
            act.wait_ge(product, (n - 1) * per_tile)
        for g in range(2):
            act.wait_ge(self.turned, n * 2 + g + 1)
            nc.scalar.activation(self.xT[:, j, HI, 4 * g:4 * g + 4, :], self.ps[:, g, :].rearrange("p (a b) -> p a b", a=4),
                                 ACT.Copy).then_inc(self.hi, 1)

    def split_lo(self, nc, dve, n, j):
        for g in range(2):
            dve.wait_ge(self.hi, n * 2 + g + 1)
            nc.vector.tensor_tensor(self.xT[:, j, LO, 4 * g:4 * g + 4, :].rearrange("p a b -> p (a b)"), self.ps[:, g, :],
                                    self.xT[:, j, HI, 4 * g:4 * g + 4, :].rearrange("p a b -> p (a b)").bitcast(F32),
                                    ALU.subtract).then_inc(self.lo, 1)


def loads_of(n, j):
    return (n - j) * 8 + 16


def ffn_phase(nc, tag, k, src_d, dst_d, weff, bias_half):
    with ExitStack() as stack:
        c = Ctx(nc, stack)
        f = Front(c, tag)
        xb = c.sb(tag + "xb", [P, 2, D])
        xo = c.sb(tag + "xo", [P, 2, D])
        psy = c.ps(tag + "psy", [P, 2, 2, BANK])
        with_bias, product, result = c.sem(tag + "with_bias"), c.sem(tag + "product"), c.sem(tag + "result")
        stored = [c.sem(tag + f"stored{j}") for j in range(2)]
        block = stack.enter_context(nc.Block())

        def rows(n, j):
            return (n - j) * (P // 2) + j * S

        @block.sync
        def _(sp):
            def step(n, j, has):
                if has(3):
                    m, jm = n + 3, (j + 1) % 2
                    if later(m, 2):
                        sp.wait_ge(f.normed, m - 1)
                        sp.wait_ge(with_bias, m - 1)
                    sp.dma_start(f.xt[:, jm, :], src_d[bass.ds(rows(m, jm), P), :]).then_inc(f.x_in[jm], 16)
                if has(0):
                    sp.wait_ge(result, n * 2 + 2)
                    sp.dma_start(dst_d[bass.ds(rows(n, j), P), :], xo[:, j, :]).then_inc(stored[j], 16)
            steady(sp, step, NT, 3)
            for j in range(2):
                sp.wait_ge(stored[j], 16 * NT // 2)

        @block.gpsimd
        def _(pool):
            def step(n, j, has):
                pool.wait_ge(f.x_in[j], loads_of(n, j))
                if later(n, 2):
                    pool.wait_ge(result, n * 2 - 2)
                nc.gpsimd.tensor_tensor(xb[:, j, :], f.xt[:, j, :], bias_half[:], ALU.add).then_inc(with_bias, 1)
            steady(pool, step, NT, 0)

        @block.scalar
        def _(act):
            def step(n, j, has):
                if has(2):
                    f.root_of(nc, act, k.eps_ln[:], n + 2, j)
                if has(1):
                    f.split_hi(nc, act, n + 1, (j + 1) % 2, product, 2)
            steady(act, step, NT, 2)

        @block.tensor
        def _(pe):
            def step(n, j, has):
                if has(1):
                    f.turn(nc, pe, k.ident, n + 1, (j + 1) % 2)
                if has(0):
                    pe.wait_ge(f.lo, n * 2 + 2)
                    if later(n, 2):
                        pe.wait_ge(result, n * 2 - 2)
                    for half in range(2):
                        for i, (a, m) in enumerate(PASSES):
                            for dt in range(DT):
                                ins = nc.tensor.matmul(psy[:, j, half, :], f.xT[:, j, a, dt, :],
                                                       weff[:, j, m, dt, half * BANK:(half + 1) * BANK],
                                                       start=(i == 0 and dt == 0), stop=(i == 2 and dt == DT - 1))
                        ins.then_inc(product, 1)
            steady(pe, step, NT, 2)

        @block.vector
        def _(dve):
            def step(n, j, has):
                if has(2):
                    f.stats_of(nc, dve, n + 2, j, loads_of(n + 2, j))
                if has(1):
                    f.split_lo(nc, dve, n + 1, (j + 1) % 2)
                if has(2):
                    if later(n, 0):
                        dve.wait_ge(f.turned, n * 2 + 2)
                    f.normalise(nc, dve, n + 2, j)
                if has(0):
                    if later(n, 2):
                        dve.wait_ge(stored[j], (n - j) * 8)
                    dve.wait_ge(with_bias, n + 1)
                    for half in range(2):
                        dve.wait_ge(product, n * 2 + half + 1)
                        w = slice(half * BANK, (half + 1) * BANK)
                        nc.vector.scalar_tensor_tensor(out=xo[:, j, w], in0=psy[:, j, half, :], scalar=0.5,
                                                             in1=xb[:, j, w], op0=ALU.mult, op1=ALU.add).then_inc(result, 1)
            steady(dve, step, NT, 2)



def latents_phase(nc, k, src_d, args):
    wa_d, lnw_d, cos_d, sin_d = args
    tag = "l_"
    with ExitStack() as stack:
        c = Ctx(nc, stack)
        f = Front(c, tag)
        wa_in = c.sb("wa_in", [P, DT, LAT])
        wa = c.sb("wa", [P, 2, DT, LAT], F32R)
        lnw = c.sb("lnw", [P, QR + KVR])
        cos = c.sb("l_cos", [P, NT, ROPE])
        sin = c.sb("l_sin", [P, NT, ROPE])
        squares = c.sb("squares", [P, 2, QR + KVR])
        ss = c.sb("ss", [P, 2, 2])
        rms = c.sb("rms", [P, 2, 2])
        inv = c.sb("l_invs", [P, 2, 2])
        lat = c.sb("lat", [P, 2, LAT])
        rot = c.sb("rot", [P, 2, 2, ROPE])
        psl = c.ps("psl", [P, 2, BANK])
        ps2 = c.ps("ps2", [P, 2, BANK])
        w_loaded, w_hi, w_lo = c.sem("l_w_loaded"), c.sem("l_w_hi"), c.sem("l_w_lo")
        small_in, scaled = c.sem("l_small_in"), c.sem("l_scaled")
        product, rooted, inverted = c.sem("l_product"), c.sem("l_rooted"), c.sem("l_inverted")
        squared = c.sem("l_squared")
        partial, latent = c.sem("l_partial"), c.sem("l_latent")
        turned2, hi2, lo2 = c.sem("l_turned2"), c.sem("l_hi2"), c.sem("l_lo2")
        block = stack.enter_context(nc.Block())

        @block.sync
        def _(sp):
            sp.dma_start(wa_in[:], wa_d.rearrange("p (a n) -> p a n", a=DT)).then_inc(w_loaded, 16)
            sp.dma_start(lnw[:], lnw_d.rearrange("(a n) -> a n", a=1).to_broadcast([P, QR + KVR])).then_inc(small_in, 16)
            sp.dma_start(cos[:], cos_d.rearrange("(t p) n -> p t n", p=P)).then_inc(small_in, 16)
            sp.dma_start(sin[:], sin_d.rearrange("(t p) n -> p t n", p=P)).then_inc(small_in, 16)

            def step(n, j, has):
                if has(2):
                    if later(n, 0):
                        sp.wait_ge(f.normed, n + 1)
                    sp.dma_start(f.xt[:, j, :], src_d[bass.ds((n + 2) * P, P), :]).then_inc(f.x_in[j], 16)
            steady(sp, step, NT, 2)

        @block.gpsimd
        def _(pool):
            pool.wait_ge(w_hi, 1)
            nc.gpsimd.tensor_tensor(wa[:, LO, :, :], wa_in[:], wa[:, HI, :, :].bitcast(F32), ALU.subtract).then_inc(w_lo, 1)

        @block.scalar
        def _(act):
            act.wait_ge(w_loaded, 16)
            nc.scalar.activation(wa[:, HI, :, :], wa_in[:], ACT.Copy).then_inc(w_hi, 1)

            def step(n, j, has):
                if has(2):
                    f.root_of(nc, act, k.eps_ln[:], n + 2, j)
                if has(1):
                    f.split_hi(nc, act, n + 1, (j + 1) % 2, product, 1)
                if has(0):
                    act.wait_ge(product, n + 1)
                    if later(n, 2):
                        act.wait_ge(inverted, n - 1)
                        act.wait_ge(squared, n - 1)
                    nc.scalar.activation(squares[:, j, 0:QR], psl[:, j, 0:QR], ACT.Square,
                                         accum_out=ss[:, j, 0:1])
                    nc.scalar.activation(squares[:, j, QR:QR + KVR], psl[:, j, QR:QR + KVR], ACT.Square,
                                         accum_out=ss[:, j, 1:2]).then_inc(squared, 1)
                    act.wait_ge(squared, n + 1)
                    nc.scalar.activation(rms[:, j, 0:1], ss[:, j, 0:1], ACT.Sqrt, bias=k.eps_rms[:], scale=1.0 / QR)
                    nc.scalar.activation(rms[:, j, 1:2], ss[:, j, 1:2], ACT.Sqrt, bias=k.eps_rms[:], scale=1.0 / KVR).then_inc(rooted, 1)
                if has(-1):
                    m, jm = n - 1, (j + 1) % 2
                    act.wait_ge(turned2, n)
                    for r in range(QRT):
                        nc.scalar.activation(k.qnT[:, HI, r, bass.ds(m * P, P)], ps2[:, jm, r * P:(r + 1) * P], ACT.Copy)
                    nc.scalar.activation(k.keyT[:, HI, bass.ds(m * P, P)], ps2[:, jm, QR:LAT], ACT.Copy)
                    nc.scalar.activation(k.val[:, bass.ds(m, 1), 0:KVR], lat[:, jm:jm + 1, QR:QR + KVR], ACT.Copy).then_inc(hi2, 1)
            steady(act, step, NT, 2, 1)

        @block.tensor
        def _(pe):
            def step(n, j, has):
                if has(1):
                    f.turn(nc, pe, k.ident, n + 1, (j + 1) % 2)
                if has(0):
                    if not later(n, 1):
                        pe.wait_ge(w_lo, 1)
                    pe.wait_ge(f.lo, n * 2 + 2)
                    if later(n, 2):
                        pe.wait_ge(latent, n - 1)
                    for i, (a, m) in enumerate(PASSES):
                        for dt in range(DT):
                            ins = nc.tensor.matmul(psl[:, j, 0:LAT], f.xT[:, j, a, dt, :], wa[:, m, dt, :],
                                                   start=(i == 0 and dt == 0), stop=(i == 2 and dt == DT - 1))
                    ins.then_inc(product, 1)
                if has(-1):
                    jm = (j + 1) % 2
                    pe.wait_ge(latent, n)
                    if later(n, 3):
                        pe.wait_ge(lo2, n - 2)
                    for r in range(LAT // P):
                        ins = nc.tensor.transpose(ps2[:, jm, r * P:(r + 1) * P], lat[:, jm, r * P:(r + 1) * P], k.ident[:])
                    ins.then_inc(turned2, 1)
            steady(pe, step, NT, 2, 1)

        @block.vector
        def _(dve):
            dve.wait_ge(small_in, 48)
            nc.vector.tensor_scalar(lnw[:, 0:QR], lnw[:, 0:QR], SCALE, None, ALU.mult).then_inc(scaled, 1)
            dve.wait_ge(scaled, 1)

            def step(n, j, has):
                if has(2):
                    f.stats_of(nc, dve, n + 2, j, loads_of(n + 2, j))
                if has(1):
                    f.split_lo(nc, dve, n + 1, (j + 1) % 2)
                if has(2):
                    if later(n, 0):
                        dve.wait_ge(f.turned, n * 2 + 2)
                    f.normalise(nc, dve, n + 2, j)
                if has(0):
                    dve.wait_ge(rooted, n + 1)
                    nc.vector.reciprocal(inv[:, j, :], rms[:, j, :]).then_inc(inverted, 1)
                    pe_cols = psl[:, j, QR + KVR:LAT]
                    half = ROPE // 2
                    if later(n, 2):
                        dve.wait_ge(turned2, n - 1)
                        dve.wait_ge(hi2, n - 1)
                    nc.vector.tensor_tensor(rot[:, j, 0, :], pe_cols, cos[:, bass.ds(n, 1), :].rearrange("p a n -> p (a n)"), ALU.mult)
                    nc.vector.tensor_tensor(rot[:, j, 1, 0:half], pe_cols[:, half:ROPE],
                                            sin[:, bass.ds(n, 1), 0:half].rearrange("p a n -> p (a n)"), ALU.mult)
                    nc.vector.tensor_tensor(rot[:, j, 1, half:ROPE], pe_cols[:, 0:half],
                                            sin[:, bass.ds(n, 1), half:ROPE].rearrange("p a n -> p (a n)"), ALU.mult).then_inc(partial, 1)
                    dve.wait_ge(inverted, n + 1)
                    nc.vector.scalar_tensor_tensor(out=lat[:, j, 0:QR], in0=psl[:, j, 0:QR], scalar=inv[:, j, 0:1],
                                                   in1=lnw[:, 0:QR], op0=ALU.mult, op1=ALU.mult)
                    nc.vector.scalar_tensor_tensor(out=lat[:, j, QR:QR + KVR], in0=psl[:, j, QR:QR + KVR], scalar=inv[:, j, 1:2],
                                                   in1=lnw[:, QR:QR + KVR], op0=ALU.mult, op1=ALU.mult)
                    dve.wait_ge(partial, n + 1)
                    nc.vector.tensor_tensor(lat[:, j, QR + KVR:LAT], rot[:, j, 0, :], rot[:, j, 1, :], ALU.add).then_inc(latent, 1)
                if has(-1):
                    m, jm = n - 1, (j + 1) % 2
                    dve.wait_ge(hi2, n)
                    for r in range(QRT):
                        nc.vector.tensor_tensor(k.qnT[:, LO, r, bass.ds(m * P, P)], ps2[:, jm, r * P:(r + 1) * P],
                                                k.qnT[:, HI, r, bass.ds(m * P, P)].bitcast(F32), ALU.subtract)
                    nc.vector.tensor_tensor(k.keyT[:, LO, bass.ds(m * P, P)], ps2[:, jm, QR:LAT],
                                            k.keyT[:, HI, bass.ds(m * P, P)].bitcast(F32), ALU.subtract)
                    nc.vector.tensor_tensor(k.val[:, bass.ds(m, 1), KVR:2 * KVR], lat[:, jm:jm + 1, QR:QR + KVR],
                                            k.val[:, bass.ds(m, 1), 0:KVR].bitcast(F32), ALU.subtract).then_inc(lo2, 1)
            steady(dve, step, NT, 2, 1)



TILES = 4 * QT
GROUPS = (1, 2, 3, 4, 6, 8, 10, 12)
SLOTS_M = (
    ("Q", 1, 0), ("N", -1, 1), ("Q", 1, 1), ("W", 0, 0),
    ("Q", 2, 0), ("Q", 2, 1), ("W", 0, 1), ("N", 1, 0),
    ("Q", 3, 0), ("N", 1, 1), ("Q", 3, 1), ("F", 0, 0), ("W", 1, 0),
    ("Q", 4, 0), ("Q", 4, 1), ("F", 1, 0), ("W", 1, 1), ("N", 3, 0),
)
PROLOGUE_M = 4


def groups_through(li):
    return 12 * (li // QT) + GROUPS[li % QT]


class Round:

    def __init__(self, it, first, last):
        self.it, self.first, self.last = it, first, last
        keys = list(SLOTS_M)
        if first:
            keys.remove(("N", -1, 1))
        if last:
            keys = [x for x in keys if x[0] != "F" and x[:2] != ("Q", 4)] + [("N", 3, 1)]
        self.keys = keys
        self.before = PROLOGUE_M if first else it * len(SLOTS_M) + PROLOGUE_M - 1

    def use(self, *key):
        return self.before + self.keys.index(key)


def rounds(eng, body):
    body(Round(0, True, False))
    with eng.Fori(1, PAIRS - 1) as it:
        body(Round(it, False, False))
    body(Round(PAIRS - 1, False, True))


def attention_phase(nc, k, args, oT_d, wvo_d):
    wn_d, wpe_d, wv_d, wo_d, cosT_d, sinT_d = args
    with ExitStack() as stack:
        c = Ctx(nc, stack)
        wn = c.sb("wn", [64, 2, QR + KVR])
        wpe = c.sb("wpe", [P, 2, QRT, ROPE])
        wv = c.sb("wv", [P, 2, KVR])
        wo = c.sb("wo", [P, 2, D])
        wvo = c.sb("wvo", [64, 2, BANK])
        wq = c.sb("wq", [P, 2, 2, QRT, QHD], F32R)
        cosT = c.sb("cosT", [P, S])
        sinT = c.sb("sinT", [P, S])
        qf = c.sb("qf", [P, 2, CHUNK])
        rot = c.sb("q_rot", [P, 2, CHUNK])
        q = c.sb("q", [P, 2, 2, S], F32R)
        prob = c.sb("prob", [P, 4, S])
        pT0 = c.sb("pT0", [P, 2, 4, CHUNK], F32R)
        pT1 = c.sb("pT1", [P, 2, 8, CHUNK], F32R)
        pT = (pT0, pT1)
        negmax = c.sb("negmax", [P, 8])
        rowsum = c.sb("rowsum", [P, 4, QT])
        rinv = c.sb("rinv", [P, 4, QT])
        spread = c.sb("spread", [P, 2, 4, 2, KVR])
        lower = c.sb("lower", [64, CHUNK])
        o_sum = c.sb("o_sum", [P, 2, CHUNK])
        o_norm = c.sb("o_norm", [P, 2, CHUNK])
        psS = c.ps("psS", [P, 2, 2 * BANK])
        psT = c.ps("psT", [P, 2, BANK])
        psV = c.ps("psV", [P, BANK])
        psM = c.ps("psM", [P, BANK])
        tab_in, wn_in, wo_in = c.sem("tab_in"), c.sem("wn_in"), c.sem("wo_in")
        zeroed = c.sem("zeroed")
        scored, maxed, exped = c.sem("scored"), c.sem("maxed"), c.sem("exped")
        turned, p_hi, p_lo = c.sem("p_turned"), c.sem("p_hi"), c.sem("p_lo")
        valued, lowered, joined = c.sem("valued"), c.sem("lowered"), c.sem("joined")
        m_done, m_free = c.sem("m_done"), c.sem("m_free")
        rope_parts, roped, q_hi, q_lo = c.sem("rope_parts"), c.sem("roped"), c.sem("q_hi"), c.sem("q_lo")
        recip, inverted, wq_hi = c.sem("recip"), c.sem("inverted"), c.sem("wq_hi")
        o_stored = [c.sem(f"o_stored{n}") for n in range(2)]
        w_stored = [c.sem(f"w_stored{n}") for n in range(2)]
        block = stack.enter_context(nc.Block())

        @block.sync
        def _(sp):
            def load_fold(pair):
                sp.dma_start(wn[:], wn_d[bass.ds(pair, 1), :, :].rearrange("a p n -> (a p) n").rearrange("p (e n) -> p e n", e=2)).then_inc(wn_in, 16)
                sp.dma_start(wpe[:].rearrange("p e r n -> p (e r n)"), wpe_d[bass.ds(pair, 1), :, :].rearrange("a p n -> (a p) n")).then_inc(wn_in, 16)

            def load_out(pair):
                sp.dma_start(wv[:].rearrange("p e n -> p (e n)"), wv_d[bass.ds(pair, 1), :, :].rearrange("a p n -> (a p) n")).then_inc(wo_in, 16)
                sp.dma_start(wo[:].rearrange("p e n -> p (e n)"), wo_d[bass.ds(pair, 1), :, :].rearrange("a p n -> (a p) n")).then_inc(wo_in, 16)

            load_fold(0)
            sp.dma_start(cosT[:], cosT_d[:, :]).then_inc(tab_in, 16)
            sp.dma_start(sinT[:], sinT_d[:, :]).then_inc(tab_in, 16)
            load_out(0)

            def body(r):
                it = r.it

                def store_o(key, pair, b, ch):
                    sp.wait_ge(m_free, r.use(*key) + 1)
                    sp.dma_start(oT_d[bass.ds(pair * P, P), b * S + ch * CHUNK:b * S + (ch + 1) * CHUNK],
                                 o_norm[:, ch, :]).then_inc(o_stored[ch], 16)

                def store_w(e, half):
                    sp.wait_ge(m_free, r.use("W", e, half) + 1)
                    sp.dma_start(wvo_d[bass.ds(it * P + e * KVR, KVR), half * BANK:(half + 1) * BANK],
                                 wvo[:, half, :]).then_inc(w_stored[half], 16)

                if not r.last:
                    sp.wait_ge(m_free, 2 if r.first else r.before - len(SLOTS_M) + SLOTS_M.index(("F", 1, 0)) + 1)
                    load_fold(it + 1)
                if not r.first:
                    store_o(("N", -1, 1), it - 1, 1, 1)
                store_w(0, 0)
                store_w(0, 1)
                store_o(("N", 1, 0), it, 0, 0)
                store_o(("N", 1, 1), it, 0, 1)
                store_w(1, 0)
                store_w(1, 1)
                if not r.last:
                    load_out(it + 1)
                store_o(("N", 3, 0), it, 1, 0)
                if r.last:
                    store_o(("N", 3, 1), it, 1, 1)
            rounds(sp, body)
            for n in range(2):
                sp.wait_ge(o_stored[n], 16 * 2 * PAIRS)
                sp.wait_ge(w_stored[n], 16 * 2 * PAIRS)

        @block.tensor
        def _(pe):
            def shared(count):
                if later(count, 1):
                    pe.wait_ge(m_free, count)

            def fold_queries(e, count):
                shared(count)
                for t in range(QRT):
                    ins = nc.tensor.matmul(psM[:, t * NOPE:(t + 1) * NOPE], wn[:, e, t * P:(t + 1) * P], wn[:, e, QR:QR + KVR],
                                           start=True, stop=True)
                ins.then_inc(m_done, 1)

            def queries(s, ch, count):
                e, b = s % 2, (s // 2) % 2
                shared(count)
                for n, (a, m) in enumerate(PASSES):
                    for t in range(QRT):
                        ins = nc.tensor.matmul(psM[:, :], wq[:, a, e, t, :], k.qnT[:, m, t, b * S + ch * CHUNK:b * S + (ch + 1) * CHUNK],
                                               start=(n == 0 and t == 0), stop=(n == 2 and t == QRT - 1))
                ins.then_inc(m_done, 1)

            def scores(it, li):
                s, t = (li // QT) % 4, li % QT
                b = s // 2
                if later(it, 1) or li >= 2:
                    pe.wait_ge(exped, it * TILES + li - 1)
                if t % 4 == 0:
                    pe.wait_ge(q_lo, it * 8 + 2 * (li // QT) + t // 4 + 1)
                width = max(2 * P, (t + 1) * P)
                pieces = [(0, min(width, BANK))] + ([(BANK, max(width, BANK + 2 * P))] if width > BANK else [])
                for x0, x1 in pieces:
                    diagonal = x0 <= t * P < x1
                    for n, (a, m) in enumerate(PASSES):
                        ins = nc.tensor.matmul(psS[:, li % 2, x0:x1], q[:, s % 2, a, t * P:(t + 1) * P],
                                               k.keyT[:, m, b * S + x0:b * S + x1], start=(n == 0), stop=(n == 2))
                        if n == 0 and diagonal:
                            nc.tensor.matmul(psS[:, li % 2, t * P:(t + 1) * P], k.ident_bf[:], k.mask_bf[:], start=False, stop=False)
                ins.then_inc(scored, 1)

            def transposes(it, li):
                t = li % QT
                g0 = groups_through(li - 1)
                pe.wait_ge(exped, it * TILES + li + 1)
                for g in range(1 if t < 4 else 2):
                    if later(it, 1) or g0 + g >= 2:
                        pe.wait_ge(p_lo, it * 48 + g0 + g - 1)
                    for kt in range(4 * g, min(4 * g + 4, t + 1)):
                        ins = nc.tensor.transpose(psT[:, (g0 + g) % 2, (kt % 4) * P:(kt % 4 + 1) * P],
                                                  prob[:, li % 4, kt * P:(kt + 1) * P], k.ident[:])
                    ins.then_inc(turned, 1)

            def values(it, s, ch):
                b = (s // 2) % 2
                pe.wait_ge(p_lo, it * 48 + groups_through(QT * s + 4 * ch + 3))
                if later(it, 1) or 2 * s + ch >= 1:
                    pe.wait_ge(joined, it * 8 + 2 * s + ch)
                last = 4 * ch + 3
                for kt in range(last + 1):
                    n0 = min(max(kt - 4 * ch, 0), 2) * P
                    for part in (HI, LO):
                        ins = nc.tensor.matmul(psV[:, n0:CHUNK], k.val[:, b * QT + kt, :], pT[ch][:, part, kt, n0:CHUNK],
                                               start=(kt == 0 and part == HI), stop=(kt == last and part == LO))
                ins.then_inc(valued, 1)

            def broadcast(it, s, ch, count):
                pe.wait_ge(inverted, it * 8 + 2 * s + ch + 1)
                shared(count)
                for t in range(4):
                    ins = nc.tensor.transpose(psM[:, t * P:(t + 1) * P],
                                              spread[:, ch, t, :, :].rearrange("p e n -> p (e n)"), k.ident[:])
                ins.then_inc(m_done, 1)

            def fold_output(e, half, count):
                shared(count)
                nc.tensor.matmul(psM[0:KVR, :], wv[:, e, :], wo[:, e, half * BANK:(half + 1) * BANK],
                                 start=True, stop=True).then_inc(m_done, 1)

            pe.wait_ge(wn_in, 32)
            for e in range(2):
                fold_queries(e, e)
            for ch in range(2):
                if ch == 0:
                    pe.wait_ge(m_free, 2)
                queries(0, ch, 2 + ch)
            pe.wait_ge(zeroed, 2)
            scores(0, 0)

            def body(r):
                it = r.it
                for s in range(4):
                    for t in range(QT):
                        li = QT * s + t
                        if not (r.last and li == TILES - 1):
                            scores(it, li + 1)
                        if not (r.first and li == 0):
                            transposes(it, li - 1)
                        if t in (1, 4) and not (r.last and s == 3):
                            queries(s + 1, t // 4, r.use("Q", s + 1, t // 4))
                        if t == 2 and not (r.first and s == 0):
                            values(it, s - 1, 1)
                        if t == 3 and s % 2 == 0 and not (r.first and s == 0):
                            broadcast(it, s - 1, 1, r.use("N", s - 1, 1))
                        if t == 5 and s >= 2 and not r.last:
                            if s == 2:
                                pe.wait_ge(wn_in, (it + 2) * 32)
                            fold_queries(s - 2, r.use("F", s - 2, 0))
                        if t == 6:
                            values(it, s, 0)
                            if s == 0:
                                pe.wait_ge(wo_in, (it + 1) * 32)
                            fold_output(s // 2, s % 2, r.use("W", s // 2, s % 2))
                        if t == 7 and s % 2 == 1:
                            broadcast(it, s, 0, r.use("N", s, 0))
                if r.last:
                    transposes(it, TILES - 1)
                    values(it, 3, 1)
                    broadcast(it, 3, 1, r.use("N", 3, 1))
            rounds(pe, body)

        @block.scalar
        def _(act):
            def split_queries_hi(e, count, folds):
                act.wait_ge(m_done, count + 1)
                nc.scalar.activation(wq[:, HI, e, :, 0:NOPE], psM[:, 0:QRT * NOPE].rearrange("p (t n) -> p t n", t=QRT), ACT.Copy)
                nc.scalar.activation(wq[:, HI, e, :, NOPE:QHD], wpe[:, e, :, :], ACT.Copy).then_inc(wq_hi, 1)

            def copy_queries(ch, number, count):
                act.wait_ge(m_done, count + 1)
                if later(number, 2):
                    act.wait_ge(q_lo, number - 1)
                nc.scalar.activation(qf[:, ch, :], psM[:, :], ACT.Copy).then_inc(m_free, 1)

            def exponentials(it, li):
                s, t = (li // QT) % 4, li % QT
                act.wait_ge(maxed, it * TILES + li + 1)
                nc.scalar.activation(prob[:, li % 4, 0:(t + 1) * P], psS[:, li % 2, 0:(t + 1) * P], ACT.Exp,
                                     bias=negmax[:, li % 8:li % 8 + 1], scale=1.0,
                                     accum_out=rowsum[:, s, t:t + 1]).then_inc(exped, 1)

            def split_hi(it, li):
                t = li % QT
                g0 = groups_through(li - 1)
                ch, x = t // 4, (t % 4) * P
                for g in range(1 if t < 4 else 2):
                    n = min(4, t + 1 - 4 * g)
                    act.wait_ge(turned, it * 48 + g0 + g + 1)
                    nc.scalar.activation(pT[ch][:, HI, 4 * g:4 * g + n, x:x + P],
                                         psT[:, (g0 + g) % 2, 0:n * P].rearrange("p (a b) -> p a b", a=n), ACT.Copy).then_inc(p_hi, 1)

            def lower_half(it, s, ch):
                act.wait_ge(valued, it * 8 + 2 * s + ch + 1)
                nc.scalar.activation(lower[:, :], psV[KVR:2 * KVR, :], ACT.Copy).then_inc(lowered, 1)

            for e in range(2):
                split_queries_hi(e, e, e)
            for ch in range(2):
                copy_queries(ch, ch, 2 + ch)
            exponentials(0, 0)

            def body(r):
                it = r.it
                for s in range(4):
                    for t in range(QT):
                        li = QT * s + t
                        if not (r.first and li == 0):
                            split_hi(it, li - 1)
                        if not (r.last and li == TILES - 1):
                            exponentials(it, li + 1)
                        if t in (1, 4) and not (r.last and s == 3):
                            copy_queries(t // 4, it * 8 + 2 * (s + 1) + t // 4, r.use("Q", s + 1, t // 4))
                        if t == 2 and not (r.first and s == 0):
                            lower_half(it, s - 1, 1)
                        if t == 5 and s >= 2 and not r.last:
                            split_queries_hi(s - 2, r.use("F", s - 2, 0), None)
                        if t == 6:
                            lower_half(it, s, 0)
                            e, half = s // 2, s % 2
                            act.wait_ge(m_done, r.use("W", e, half) + 1)
                            if not (r.first and e == 0):
                                act.wait_ge(w_stored[half], (it * 2 + e) * 16)
                            nc.scalar.activation(wvo[:, half, :], psM[0:KVR, :], ACT.Copy).then_inc(m_free, 1)
                if r.last:
                    split_hi(it, TILES - 1)
                    lower_half(it, 3, 1)
            rounds(act, body)

        @block.vector
        def _(dve):
            def split_queries_lo(e, count):
                dve.wait_ge(wq_hi, count)
                nc.vector.tensor_tensor(wq[:, LO, e, :, NOPE:QHD], wpe[:, e, :, :], wq[:, HI, e, :, NOPE:QHD].bitcast(F32), ALU.subtract)
                nc.vector.tensor_tensor(wq[:, LO, e, :, 0:NOPE], psM[:, 0:QRT * NOPE].rearrange("p (t n) -> p t n", t=QRT),
                                        wq[:, HI, e, :, 0:NOPE].bitcast(F32), ALU.subtract).then_inc(m_free, 1)

            def query_hi(s, ch, number):
                dve.wait_ge(roped, number + 1)
                nc.vector.tensor_copy(q[:, s % 2, HI, ch * CHUNK:(ch + 1) * CHUNK], qf[:, ch, :]).then_inc(q_hi, 1)

            def maxima(it, li):
                t = li % QT
                dve.wait_ge(scored, it * TILES + li + 1)
                nc.vector.tensor_reduce(negmax[:, li % 8:li % 8 + 1], psS[:, li % 2, 0:(t + 1) * P], AX_X, ALU.max,
                                        negate=True).then_inc(maxed, 1)

            def split_lo(it, li):
                t = li % QT
                g0 = groups_through(li - 1)
                ch, x = t // 4, (t % 4) * P
                for g in range(1 if t < 4 else 2):
                    n = min(4, t + 1 - 4 * g)
                    dve.wait_ge(p_hi, it * 48 + g0 + g + 1)
                    nc.vector.tensor_tensor(pT[ch][:, LO, 4 * g:4 * g + n, x:x + P],
                                            psT[:, (g0 + g) % 2, 0:n * P].rearrange("p (a b) -> p a b", a=n),
                                            pT[ch][:, HI, 4 * g:4 * g + n, x:x + P].bitcast(F32), ALU.subtract).then_inc(p_lo, 1)

            def invert(it, s, ch):
                dve.wait_ge(exped, it * TILES + QT * s + 4 * ch + 4)
                nc.vector.reciprocal(rinv[:, s, 4 * ch:4 * ch + 4], rowsum[:, s, 4 * ch:4 * ch + 4]).then_inc(recip, 1)
                dve.wait_ge(recip, it * 8 + 2 * s + ch + 1)
                nc.vector.tensor_copy(spread[:, ch, :, s % 2, :],
                                      rinv[:, s, 4 * ch:4 * ch + 4].rearrange("p (t a) -> p t a", a=1).to_broadcast([P, 4, KVR])).then_inc(inverted, 1)

            def join(it, s, ch):
                e = s % 2
                dve.wait_ge(lowered, it * 8 + 2 * s + ch + 1)
                nc.vector.tensor_tensor(o_sum[KVR * e:KVR * e + KVR, ch, :], psV[0:KVR, :], lower[:, :], ALU.add).then_inc(joined, 1)

            def normalise(it, s, ch, count):
                dve.wait_ge(m_done, count + 1)
                if later(it, 1) or s > 1:
                    dve.wait_ge(o_stored[ch], it * 32 + 16 * ((s - 1) // 2))
                dve.wait_ge(joined, it * 8 + 2 * s + ch + 1)
                nc.vector.tensor_tensor(o_norm[:, ch, :], psM[:, :], o_sum[:, ch, :], ALU.mult).then_inc(m_free, 1)

            nc.vector.memset(pT0[:, :, 3, 2 * P:3 * P].bitcast(F32), 0.0).then_inc(zeroed, 1)
            nc.vector.memset(pT1[:, :, 7, 2 * P:3 * P].bitcast(F32), 0.0).then_inc(zeroed, 1)
            for e in range(2):
                split_queries_lo(e, e + 1)
            for ch in range(2):
                query_hi(0, ch, ch)
            maxima(0, 0)

            def body(r):
                it = r.it
                for s in range(4):
                    for t in range(QT):
                        li = QT * s + t
                        if not (r.last and li == TILES - 1):
                            maxima(it, li + 1)
                        if not (r.first and li == 0):
                            split_lo(it, li - 1)
                        if t in (4, 7) and not (r.last and s == 3):
                            query_hi(s + 1, t // 7, it * 8 + 2 * (s + 1) + t // 7)
                        if t == 3 and not (r.first and s == 0):
                            join(it, s - 1, 1)
                            if s % 2 == 0:
                                normalise(it, s - 1, 1, r.use("N", s - 1, 1))
                        if t == 4:
                            invert(it, s, 0)
                        if t == 5 and s >= 2 and not r.last:
                            split_queries_lo(s - 2, it * 2 + 2 + s - 2 + 1)
                        if t == 7:
                            invert(it, s, 1)
                            join(it, s, 0)
                            if s % 2 == 1:
                                normalise(it, s, 0, r.use("N", s, 0))
                if r.last:
                    split_lo(it, TILES - 1)
                    join(it, 3, 1)
                    normalise(it, 3, 1, r.use("N", 3, 1))
            rounds(dve, body)

        @block.gpsimd
        def _(pool):
            def rope(s, ch, number, count):
                x = slice(ch * CHUNK, (ch + 1) * CHUNK)
                if later(number, 1):
                    pool.wait_ge(q_lo, number)
                pool.wait_ge(m_free, count + 1)
                nc.gpsimd.tensor_tensor(rot[64:128, 0, :], qf[64:128, ch, :], cosT[64:128, x], ALU.mult).then_inc(rope_parts, 1)
                pool.wait_ge(rope_parts, number * 3 + 1)
                nc.gpsimd.tensor_tensor(rot[64:96, 1, :], qf[96:128, ch, :], sinT[96:128, x], ALU.mult).then_inc(rope_parts, 1)
                pool.wait_ge(rope_parts, number * 3 + 2)
                nc.gpsimd.tensor_tensor(rot[96:128, 1, :], qf[64:96, ch, :], sinT[64:96, x], ALU.mult).then_inc(rope_parts, 1)
                pool.wait_ge(rope_parts, number * 3 + 3)
                nc.gpsimd.tensor_tensor(qf[64:128, ch, :], rot[64:128, 0, :], rot[64:128, 1, :], ALU.add).then_inc(roped, 1)
                pool.wait_ge(q_hi, number + 1)
                nc.gpsimd.tensor_tensor(q[:, s % 2, LO, x], qf[:, ch, :], q[:, s % 2, HI, x].bitcast(F32), ALU.subtract).then_inc(q_lo, 1)

            pool.wait_ge(tab_in, 32)
            for ch in range(2):
                rope(0, ch, ch, 2 + ch)

            def body(r):
                for s in range(3 if r.last else 4):
                    for ch in range(2):
                        rope(s + 1, ch, r.it * 8 + 2 * (s + 1) + ch, r.use("Q", s + 1, ch))
            rounds(pool, body)



def output_phase(nc, src_d, dst_d, oT_d, wvo_d):
    with ExitStack() as stack:
        c = Ctx(nc, stack)
        w_in = c.sb("o_w_in", [P, 2, D])
        w = c.sb("o_w", [P, 2, PAIRS, D], F32R)
        o_in = c.sb("o_in", [P, PAIRS, P])
        o = c.sb("o_o", [P, 2, 2, PAIRS, P], F32R)
        x_in = c.sb("o_x_in", [P, 2, D])
        y = c.sb("o_y", [P, 2, D])
        psy = c.ps("o_psy", [P, 2, 2, BANK])
        w_loaded = [c.sem(f"o_w_loaded{j}") for j in range(2)]
        w_hi, w_lo = c.sem("o_w_hi"), c.sem("o_w_lo")
        o_loaded, o_hi, o_lo = c.sem("o_loaded"), c.sem("o_hi"), c.sem("o_lo")
        x_loaded = [c.sem(f"o_x_loaded{j}") for j in range(2)]
        product, result = c.sem("o_product"), c.sem("o_result")
        stored = [c.sem(f"o_y_stored{j}") for j in range(2)]
        block = stack.enter_context(nc.Block())
        oT_v = oT_d.rearrange("(a p) t -> p a t", p=P)

        @block.sync
        def _(sp):
            for pair in range(PAIRS):
                if pair == 1:
                    sp.dma_start(o_in[:], oT_v[:, :, 0:P]).then_inc(o_loaded, 16)
                if pair >= 2:
                    sp.wait_ge(w_lo, pair - 1)
                sp.dma_start(w_in[:, pair % 2, :], wvo_d[pair * P:(pair + 1) * P, :]).then_inc(w_loaded[pair % 2], 16)

            def step(n, j, has):
                if has(1):
                    sp.wait_ge(o_lo, n + 1)
                    sp.dma_start(o_in[:], oT_v[:, :, bass.ds((n + 1) * P, P)]).then_inc(o_loaded, 16)
                if has(0):
                    if later(n, 2):
                        sp.wait_ge(result, n * 2 - 2)
                    sp.dma_start(x_in[:, j, :], src_d[bass.ds(n * P, P), :]).then_inc(x_loaded[j], 16)
                if has(-1):
                    sp.wait_ge(result, n * 2)
                    jm = (j + 1) % 2
                    sp.dma_start(dst_d[bass.ds((n - 1) * P, P), :], y[:, jm, :]).then_inc(stored[jm], 16)
            output_steps(sp, step)
            for j in range(2):
                sp.wait_ge(stored[j], 16 * NT // 2)

        @block.scalar
        def _(act):
            for pair in range(PAIRS):
                act.wait_ge(w_loaded[pair % 2], 16 * (pair // 2 + 1))
                nc.scalar.activation(w[:, HI, pair, :], w_in[:, pair % 2, :], ACT.Copy).then_inc(w_hi, 1)
                if pair == 1:
                    act.wait_ge(o_loaded, 16)
                    nc.scalar.activation(o[:, 0, HI, :, :], o_in[:], ACT.Copy).then_inc(o_hi, 1)

            def step(n, j, has):
                if has(1):
                    jm = (j + 1) % 2
                    act.wait_ge(o_loaded, (n + 2) * 16)
                    if later(n, 1):
                        act.wait_ge(product, n * 2)
                    nc.scalar.activation(o[:, jm, HI, :, :], o_in[:], ACT.Copy).then_inc(o_hi, 1)
            output_steps(act, step)

        @block.vector
        def _(dve):
            for pair in range(PAIRS):
                dve.wait_ge(w_hi, pair + 1)
                nc.vector.tensor_tensor(w[:, LO, pair, :], w_in[:, pair % 2, :], w[:, HI, pair, :].bitcast(F32), ALU.subtract).then_inc(w_lo, 1)
                if pair == 1:
                    dve.wait_ge(o_hi, 1)
                    nc.vector.tensor_tensor(o[:, 0, LO, :, :], o_in[:], o[:, 0, HI, :, :].bitcast(F32), ALU.subtract).then_inc(o_lo, 1)

            def step(n, j, has):
                if has(1):
                    jm = (j + 1) % 2
                    dve.wait_ge(o_hi, n + 2)
                    nc.vector.tensor_tensor(o[:, jm, LO, :, :], o_in[:], o[:, jm, HI, :, :].bitcast(F32), ALU.subtract).then_inc(o_lo, 1)
                if has(0):
                    dve.wait_ge(x_loaded[j], loads_of(n, j))
                    if later(n, 2):
                        dve.wait_ge(stored[j], (n - j) * 8)
                    for half in range(2):
                        x = slice(half * BANK, (half + 1) * BANK)
                        dve.wait_ge(product, n * 2 + half + 1)
                        nc.vector.tensor_tensor(y[:, j, x], psy[:, j, half, :], x_in[:, j, x], ALU.add).then_inc(result, 1)
            output_steps(dve, step)

        @block.tensor
        def _(pe):
            def step(n, j, has):
                if has(0):
                    pe.wait_ge(o_lo, n + 1)
                    if later(n, 2):
                        pe.wait_ge(result, n * 2 - 2)
                    for half in range(2):
                        for pair in range(PAIRS):
                            if not later(n, 1) and half == 0:
                                pe.wait_ge(w_lo, pair + 1)
                            for i, (a, m) in enumerate(PASSES):
                                ins = nc.tensor.matmul(psy[:, j, half, :], o[:, j, a, pair, :], w[:, m, pair, half * BANK:(half + 1) * BANK],
                                                       start=(pair == 0 and i == 0), stop=(pair == PAIRS - 1 and i == 2))
                        ins.then_inc(product, 1)
            output_steps(pe, step)


def output_steps(eng, step):
    steady(eng, step, NT, 1, 1, start=0)



def macaron_block(nc, x, wa, lnw, wn, wpe, wv, wo, cos, sin, cosT, sinT, w, bias, lora_a, lora_b, starts, out):
    x1_d = nc.dram_tensor("x1", (T, D), F32).ap()
    x2_d = nc.dram_tensor("x2", (T, D), F32).ap()
    oT_d = nc.dram_tensor("oT", (PAIRS * P, T), F32).ap()
    wvo_d = nc.dram_tensor("wvo_fold", (PAIRS * P, D), F32).ap()
    with ExitStack() as stack:
        c = Ctx(nc, stack)
        k = Shared()
        k.ident = c.sb("ident", [P, P])
        k.ident_bf = c.sb("ident_bf", [P, P], BF16)
        k.mask_bf = c.sb("mask_bf", [P, P], BF16)
        k.eps_ln = c.sb("eps_ln", [P, 1])
        k.eps_rms = c.sb("eps_rms", [P, 1])
        constants_phase(nc, k)
        ffn_args = (w, bias, lora_a, lora_b, starts)

        def feed_forward(tag, src_d, dst_d):
            with ExitStack() as inner:
                ci = Ctx(nc, inner)
                weff = ci.sb(tag + "weff", [P, B, 2, DT, D], F32R)
                bias_half = ci.sb(tag + "bias_half", [P, D])
                ffn_weights_phase(nc, tag + "w_", w, (lora_a, lora_b), weff, bias_half, ffn_args)
                ffn_phase(nc, tag, k, src_d, dst_d, weff, bias_half)

        feed_forward("f1_", x, x1_d)
        with ExitStack() as inner:
            ci = Ctx(nc, inner)
            k.qnT = ci.sb("qnT", [P, 2, QRT, T], F32R)
            k.keyT = ci.sb("keyT", [P, 2, T], F32R)
            k.val = ci.sb("val", [P, NT, 2 * KVR], F32R)
            latents_phase(nc, k, x1_d, (wa, lnw, cos, sin))
            attention_phase(nc, k, (wn, wpe, wv, wo, cosT, sinT), oT_d, wvo_d)
        output_phase(nc, x1_d, x2_d, oT_d, wvo_d)
        feed_forward("f2_", x2_d, out)


class Shared:
    pass


def rope_tables():
    import math
    dim, base, factor, beta_fast, beta_slow, orig_max = ROPE, 10000.0, 128.0, 32.0, 1.0, 2048

    def corr_dim(r):
        return dim * math.log(orig_max / (r * 2 * math.pi)) / (2 * math.log(base))
    low = max(math.floor(corr_dim(beta_fast)), 0)
    high = min(math.ceil(corr_dim(beta_slow)), dim - 1)
    hi = high + 0.001 if low == high else float(high)
    ramp = np.clip((np.arange(dim // 2, dtype=np.float32) - low) / (hi - low), 0.0, 1.0)
    keep = 1.0 - ramp
    freq_extra = 1.0 / base ** (np.arange(0, dim, 2, dtype=np.float32) / dim)
    freq_inter = freq_extra / factor
    inv_freq = freq_inter * (1.0 - keep) + freq_extra * keep
    freqs = np.outer(np.arange(S, dtype=np.float32), inv_freq)
    emb = np.concatenate([freqs, freqs], axis=-1)
    sign = np.where(np.arange(ROPE) < ROPE // 2, -1.0, 1.0)
    return np.cos(emb).astype(np.float32), (np.sin(emb) * sign).astype(np.float32)


def kernel(**inputs):
    import numpy as _np
    import concourse.bacc as _bacc
    from concourse import mybir as _mybir
    from concourse.bass_utils import run_bass_kernel_spmd as _run

    get = lambda name: _np.asarray(inputs[name])
    wq_b = get("L0_attn_wq_b").reshape(PAIRS, 2, QHD, QR)
    wkv_b = get("L0_attn_wkv_b").reshape(PAIRS, 2, NOPE + VD, KVR)
    wkv_a = get("L0_attn_wkv_a")
    halves = _np.concatenate([_np.arange(0, ROPE, 2), _np.arange(1, ROPE, 2)])
    cos, sin = rope_tables()
    blank = _np.zeros((NOPE, S), _np.float32)
    data = {
        "x": get("L0_attn_x").reshape(T, D),
        "wa": _np.concatenate([get("L0_attn_wq_a"), wkv_a[:KVR], wkv_a[KVR:][halves]], 0).T.reshape(DT, P, LAT).transpose(1, 0, 2).reshape(P, DT * LAT),
        "lnw": _np.concatenate([get("L0_attn_q_a_ln_w"), get("L0_attn_kv_a_ln_w")]),
        "wn": _np.concatenate([wq_b[:, :, :NOPE], wkv_b[:, :, :NOPE]], 3).transpose(0, 2, 1, 3).reshape(PAIRS, NOPE, 2 * (QR + KVR)),
        "wpe": wq_b[:, :, NOPE:][:, :, halves].reshape(PAIRS, 2, ROPE, QRT, P).transpose(0, 4, 1, 3, 2).reshape(PAIRS, P, 2 * QRT * ROPE),
        "wv": wkv_b[:, :, NOPE:].transpose(0, 2, 1, 3).reshape(PAIRS, VD, 2 * KVR),
        "wo": get("L0_attn_wo").T.reshape(PAIRS, 2, VD, D).transpose(0, 2, 1, 3).reshape(PAIRS, VD, 2 * D),
        "cos": _np.concatenate([cos, cos], 0), "sin": _np.concatenate([sin, sin], 0),
        "cosT": _np.concatenate([blank, cos.T], 0),
        "sinT": _np.concatenate([blank, sin.T[ROPE // 2:], sin.T[:ROPE // 2]], 0),
        "w": get("L0_ffn_weight").T.reshape(DT, P, D).transpose(1, 0, 2).reshape(P, DT * D),
        "bias": get("L0_ffn_bias"),
        "lora_a": get("L0_ffn_lora_A"),
        "lora_b": get("L0_ffn_lora_B").transpose(0, 2, 1),
        "starts": get("L0_ffn_lora_start_indices"),
    }
    nc = _bacc.Bacc("TRN2", target_bir_lowering=False, num_devices=1)
    arrays, args = {}, []
    for name, a in data.items():
        a = _np.ascontiguousarray(a)
        arrays[f"in_{name}"] = a
        args.append(nc.dram_tensor(f"in_{name}", a.shape, _mybir.dt.from_np(a.dtype), kind="ExternalInput").ap())
    args.append(nc.dram_tensor("out_0", (T, D), F32, kind="ExternalOutput").ap())
    macaron_block(nc, *args)
    r = _run(nc, [arrays], core_ids=[0])
    return r.results[0]["out_0"].reshape(B, S, D)
```

```python
from contextlib import ExitStack

import numpy as np

import concourse.bass as bass
from concourse import mybir

ALU = mybir.AluOpType
ACT = mybir.ActivationFunctionType
AX_X = mybir.AxisListType.X
F32 = mybir.dt.float32
F32R = mybir.dt.float32r
BF16 = mybir.dt.bfloat16
I32 = mybir.dt.int32

P = 128
BANK = 512
B, S, D = 2, 1024, 1024
T = B * S
NT = T // P
DT = D // P
H = 32
PAIRS = H // 2
NOPE, ROPE, VD = 64, 64, 128
QHD = NOPE + ROPE
KVR = 64
QR = 256
QRT = QR // P
LAT = QR + KVR + ROPE
RANK = 16
ADAPTERS = 3
STARTS = 4
QT = S // P
CHUNK = 512
MSCALE = 0.1 * 1.0 * float(np.log(128.0)) + 1.0
SCALE = QHD ** -0.5 * MSCALE * MSCALE
LN_EPS = 1e-5
RMS_EPS = 1e-6
MASKED = -3.0e38

HI, LO = 0, 1
PASSES = ((HI, HI), (LO, HI), (HI, LO))


class Ctx:

    def __init__(self, nc, stack):
        self.nc, self.stack = nc, stack

    def sb(self, name, shape, dt=F32):
        return self.stack.enter_context(self.nc.sbuf_tensor(name, shape, dt))

    def ps(self, name, shape, dt=F32):
        return self.stack.enter_context(self.nc.psum_tensor(name, shape, dt))

    def sem(self, name):
        return self.stack.enter_context(self.nc.semaphore(name))


def steady(eng, body, steps, lead, lag=0, start=None):
    first = 4
    rounds = (steps - lead) // 2
    for n in range(-lead if start is None else start, first):
        body(n, n % 2, lambda m, n=n: 0 <= n + m < steps)
    with eng.Fori(first // 2, rounds) as r:
        for j in range(2):
            body(r * 2 + j, j, lambda m: True)
    for n in range(2 * rounds, steps + lag):
        body(n, n % 2, lambda m, n=n: 0 <= n + m < steps)


def later(n, least):
    return not isinstance(n, int) or n >= least



def constants_phase(nc, k):
    with ExitStack() as stack:
        c = Ctx(nc, stack)
        cleared, made = c.sem("c_cleared"), c.sem("c_made")
        block = stack.enter_context(nc.Block())

        @block.gpsimd
        def _(pool):
            nc.gpsimd.memset(k.ident[:], 0.0).then_inc(cleared, 1)
            nc.gpsimd.memset(k.ident_bf[:], 0.0).then_inc(cleared, 1)
            nc.gpsimd.memset(k.mask_bf[:], 0.0).then_inc(cleared, 1)
            nc.gpsimd.memset(k.eps_ln[:], LN_EPS)
            nc.gpsimd.memset(k.eps_rms[:], RMS_EPS)
            pool.wait_ge(cleared, 3)
            for m in (k.ident, k.ident_bf):
                nc.gpsimd.affine_select(out=m[:], in_=m[:], compare_op=ALU.not_equal, fill=1.0, base=0,
                                        pattern=[[-1, P]], channel_multiplier=1).then_inc(made, 1)
            nc.gpsimd.affine_select(out=k.mask_bf[:], in_=k.mask_bf[:], compare_op=ALU.is_ge, fill=MASKED, base=0,
                                    pattern=[[-1, P]], channel_multiplier=1).then_inc(made, 1)
            pool.wait_ge(made, 3)



def ffn_weights_phase(nc, tag, w, lora, weff, bias_half, args):
    w_d, bias_d, a_d, b_d, starts_d = args
    with ExitStack() as stack:
        c = Ctx(nc, stack)
        a_all = c.sb(tag + "a_all", [P, ADAPTERS, D])
        b_all = c.sb(tag + "b_all", [P, ADAPTERS, D])
        starts = c.sb(tag + "starts", [P, STARTS], I32)
        startf = c.sb(tag + "startf", [P, STARTS])
        hit = c.sb(tag + "hit", [P, B, STARTS])
        count = c.sb(tag + "count", [P, B])
        chosen = c.sb(tag + "chosen", [P, B, ADAPTERS], I32)
        sel = c.sb(tag + "sel", [P, 2, D])
        rounded = c.sb(tag + "rounded", [P, 2, D], F32R)
        a_st = c.sb(tag + "a_st", [P, B, D], F32R)
        b_st = c.sb(tag + "b_st", [P, B, D], F32R)
        w_in = c.sb(tag + "w_in", [P, 2, D])
        w_sum = c.sb(tag + "w_sum", [P, 2, D])
        ps = c.ps(tag + "ps_w", [P, 2, 2, BANK])
        cleared, lora_in, small_in = c.sem(tag + "cleared"), c.sem(tag + "lora_in"), c.sem(tag + "small_in")
        w_loaded = [c.sem(tag + f"w_loaded{j}") for j in range(2)]
        chain = c.sem(tag + "chain")
        stacked, outer, summed = c.sem(tag + "stacked"), c.sem(tag + "outer"), c.sem(tag + "summed")
        hi_done, lo_pool, lo_dve = c.sem(tag + "hi_done"), c.sem(tag + "lo_pool"), c.sem(tag + "lo_dve")
        block = stack.enter_context(nc.Block())

        @block.sync
        def _(sp):
            sp.dma_start(starts[:], starts_d.rearrange("(a n) -> a n", a=1).to_broadcast([P, STARTS])).then_inc(small_in, 16)
            sp.dma_start(bias_half[:], bias_d.rearrange("(a n) -> a n", a=1).to_broadcast([P, D])).then_inc(small_in, 16)
            sp.wait_ge(cleared, 2)
            for g in range(4):
                for tile, src in ((a_all, a_d), (b_all, b_d)):
                    sp.dma_start(tile[32 * g:32 * g + RANK, :, :], src.rearrange("a r d -> r a d")).then_inc(lora_in, 16)
            for dt in range(DT):
                if dt >= 2:
                    sp.wait_ge(summed, B * (dt - 1))
                sp.dma_start(w_in[:, dt % 2, :], w_d[:, dt * D:(dt + 1) * D]).then_inc(w_loaded[dt % 2], 16)

        @block.gpsimd
        def _(pool):
            nc.gpsimd.memset(a_all[:], 0.0).then_inc(cleared, 1)
            nc.gpsimd.memset(b_all[:], 0.0).then_inc(cleared, 1)
            for dt in range(DT):
                pool.wait_ge(hi_done, B * dt + 1)
                nc.gpsimd.tensor_tensor(weff[:, 0, LO, dt, :], w_sum[:, 0, :], weff[:, 0, HI, dt, :].bitcast(F32),
                                        ALU.subtract).then_inc(lo_pool, 1)

        @block.tensor
        def _(pe):
            pe.wait_ge(stacked, 2 * B)
            for dt in range(DT):
                for b in range(B):
                    if dt >= 1:
                        pe.wait_ge(summed, B * (dt - 1) + b + 1)
                    for half in range(2):
                        nc.tensor.matmul(ps[:, b, half, :], a_st[:, b, dt * P:(dt + 1) * P],
                                         b_st[:, b, half * BANK:(half + 1) * BANK], start=True, stop=True).then_inc(outer, 1)

        @block.scalar
        def _(act):
            for dt in range(DT):
                for b in range(B):
                    act.wait_ge(summed, B * dt + b + 1)
                    nc.scalar.activation(weff[:, b, HI, dt, :], w_sum[:, b, :], ACT.Copy).then_inc(hi_done, 1)

        @block.vector
        def _(dve):
            links = [0]

            def link(ins):
                links[0] += 1
                ins.then_inc(chain, 1)
                dve.wait_ge(chain, links[0])

            dve.wait_ge(small_in, 32)
            link(nc.vector.tensor_copy(startf[:], starts[:]))
            link(nc.vector.tensor_scalar(bias_half[:], bias_half[:], 0.5, None, ALU.mult))
            for b in range(B):
                link(nc.vector.tensor_scalar(hit[:, b, :], startf[:], float(b), None, ALU.is_le))
                link(nc.vector.reduce_sum(count[:, b:b + 1], hit[:, b, :], AX_X))
                for a in range(ADAPTERS):
                    op = ALU.is_ge if a == ADAPTERS - 1 else ALU.is_equal
                    link(nc.vector.tensor_scalar(chosen[:, b, a:a + 1], count[:, b:b + 1], float(a + 2), None, op))
            dve.wait_ge(lora_in, 16 * 8)
            for b in range(B):
                link(nc.vector.memset(sel[:], 0.0))
                for a in range(ADAPTERS):
                    m = chosen[:, b, a:a + 1].to_broadcast([P, D])
                    link(nc.vector.copy_predicated(sel[:, 0, :], m, a_all[:, a, :]))
                    link(nc.vector.copy_predicated(sel[:, 1, :], m, b_all[:, a, :]))
                link(nc.vector.tensor_copy(rounded[:], sel[:]))
                link(nc.vector.tensor_copy(a_st[0:64, b, :], sel[0:64, 0, :]))
                link(nc.vector.tensor_tensor(a_st[64:128, b, :], sel[64:128, 0, :], rounded[64:128, 0, :].bitcast(F32), ALU.subtract))
                for g in range(4):
                    r = slice(32 * g, 32 * g + 32)
                    if g % 2 == 0:
                        ins = nc.vector.tensor_copy(b_st[r, b, :], sel[r, 1, :])
                    else:
                        ins = nc.vector.tensor_tensor(b_st[r, b, :], sel[r, 1, :], rounded[r, 1, :].bitcast(F32), ALU.subtract)
                    if g < 3:
                        link(ins)
                ins.then_inc(stacked, 2)
                dve.wait_ge(stacked, 2 * b + 2)
            for dt in range(DT):
                dve.wait_ge(w_loaded[dt % 2], 16 * (dt // 2 + 1))
                for b in range(B):
                    if dt >= 1:
                        dve.wait_ge(hi_done, B * (dt - 1) + b + 1)
                        if b == 0:
                            dve.wait_ge(lo_pool, dt)
                        else:
                            dve.wait_ge(lo_dve, dt)
                    dve.wait_ge(outer, 2 * (B * dt + b) + 2)
                    nc.vector.tensor_tensor(w_sum[:, b, :], ps[:, b, :, :].rearrange("p a n -> p (a n)"),
                                            w_in[:, dt % 2, :], ALU.add).then_inc(summed, 1)
                dve.wait_ge(hi_done, B * dt + 2)
                nc.vector.tensor_tensor(weff[:, 1, LO, dt, :], w_sum[:, 1, :], weff[:, 1, HI, dt, :].bitcast(F32),
                                        ALU.subtract).then_inc(lo_dve, 1)


class Front:

    def __init__(self, c, tag):
        self.xt = c.sb(tag + "xt", [P, 2, D])
        self.xn = c.sb(tag + "xn", [P, 2, D])
        self.xT = c.sb(tag + "xT", [P, 2, 2, DT, P], F32R)
        self.st = c.sb(tag + "st", [P, 2, 12])
        self.mv = c.sb(tag + "mv", [P, 2, 2])
        self.std = c.sb(tag + "std", [P, 2, 1])
        self.rstd = c.sb(tag + "rstd", [P, 2, 1])
        self.ps = c.ps(tag + "ps_xT", [P, 2, BANK])
        self.x_in = [c.sem(tag + f"x_in{j}") for j in range(2)]
        self.stats, self.var, self.root = c.sem(tag + "stats"), c.sem(tag + "var"), c.sem(tag + "root")
        self.passed = c.sem(tag + "passed")
        self.inv, self.normed = c.sem(tag + "inv"), c.sem(tag + "normed")
        self.turned, self.hi, self.lo = c.sem(tag + "turned"), c.sem(tag + "hi"), c.sem(tag + "lo")

    def stats_of(self, nc, dve, n, j, loads):
        dve.wait_ge(self.x_in[j], loads)
        nc.vector.bn_stats(self.st[:, j, 0:6], self.xt[:, j, 0:512])
        nc.vector.bn_stats(self.st[:, j, 6:12], self.xt[:, j, 512:1024]).then_inc(self.stats, 1)
        dve.wait_ge(self.stats, n + 1)
        dve.sem_inc(self.passed, 1)
        nc.vector.bn_aggr(self.mv[:, j, :], self.st[:, j, :]).then_inc(self.var, 1)

    def root_of(self, nc, act, eps, n, j):
        act.wait_ge(self.var, n + 1)
        nc.scalar.activation(self.std[:, j, :], self.mv[:, j, 1:2], ACT.Sqrt, bias=eps, scale=1.0).then_inc(self.root, 1)

    def normalise(self, nc, dve, n, j):
        dve.wait_ge(self.root, n + 1)
        nc.vector.reciprocal(self.rstd[:, j, :], self.std[:, j, :]).then_inc(self.inv, 1)
        dve.wait_ge(self.inv, n + 1)
        nc.vector.tensor_scalar(self.xn[:, j, :], self.xt[:, j, :], self.mv[:, j, 0:1], self.rstd[:, j, :],
                                ALU.subtract, ALU.mult).then_inc(self.normed, 1)

    def turn(self, nc, pe, ident, n, j):
        pe.wait_ge(self.normed, n + 1)
        for g in range(2):
            if later(n, 1):
                pe.wait_ge(self.lo, n * 2 + g - 1)
            for q in range(4):
                ins = nc.tensor.transpose(self.ps[:, g, q * P:(q + 1) * P],
                                          self.xn[:, j, (4 * g + q) * P:(4 * g + q + 1) * P], ident[:])
            ins.then_inc(self.turned, 1)

    def split_hi(self, nc, act, n, j, product, per_tile):
        if later(n, 2):
            act.wait_ge(product, (n - 1) * per_tile)
        for g in range(2):
            act.wait_ge(self.turned, n * 2 + g + 1)
            nc.scalar.activation(self.xT[:, j, HI, 4 * g:4 * g + 4, :], self.ps[:, g, :].rearrange("p (a b) -> p a b", a=4),
                                 ACT.Copy).then_inc(self.hi, 1)

    def split_lo(self, nc, dve, n, j):
        for g in range(2):
            dve.wait_ge(self.hi, n * 2 + g + 1)
            nc.vector.tensor_tensor(self.xT[:, j, LO, 4 * g:4 * g + 4, :].rearrange("p a b -> p (a b)"), self.ps[:, g, :],
                                    self.xT[:, j, HI, 4 * g:4 * g + 4, :].rearrange("p a b -> p (a b)").bitcast(F32),
                                    ALU.subtract).then_inc(self.lo, 1)


def loads_of(n, j):
    return (n - j) * 8 + 16


def ffn_phase(nc, tag, k, src_d, dst_d, weff, bias_half):
    with ExitStack() as stack:
        c = Ctx(nc, stack)
        f = Front(c, tag)
        xb = c.sb(tag + "xb", [P, 2, D])
        xo = c.sb(tag + "xo", [P, 2, D])
        psy = c.ps(tag + "psy", [P, 2, 2, BANK])
        with_bias, product, result = c.sem(tag + "with_bias"), c.sem(tag + "product"), c.sem(tag + "result")
        stored = [c.sem(tag + f"stored{j}") for j in range(2)]
        block = stack.enter_context(nc.Block())

        def rows(n, j):
            return (n - j) * (P // 2) + j * S

        @block.sync
        def _(sp):
            def step(n, j, has):
                if has(3):
                    m, jm = n + 3, (j + 1) % 2
                    if later(m, 2):
                        sp.wait_ge(f.normed, m - 1)
                        sp.wait_ge(with_bias, m - 1)
                    sp.dma_start(f.xt[:, jm, :], src_d[bass.ds(rows(m, jm), P), :]).then_inc(f.x_in[jm], 16)
                if has(0):
                    sp.wait_ge(result, n * 2 + 2)
                    sp.dma_start(dst_d[bass.ds(rows(n, j), P), :], xo[:, j, :]).then_inc(stored[j], 16)
            steady(sp, step, NT, 3)
            for j in range(2):
                sp.wait_ge(stored[j], 16 * NT // 2)

        @block.gpsimd
        def _(pool):
            def step(n, j, has):
                pool.wait_ge(f.x_in[j], loads_of(n, j))
                if later(n, 2):
                    pool.wait_ge(result, n * 2 - 2)
                nc.gpsimd.tensor_tensor(xb[:, j, :], f.xt[:, j, :], bias_half[:], ALU.add).then_inc(with_bias, 1)
            steady(pool, step, NT, 0)

        @block.scalar
        def _(act):
            def step(n, j, has):
                if has(2):
                    f.root_of(nc, act, k.eps_ln[:], n + 2, j)
                if has(1):
                    f.split_hi(nc, act, n + 1, (j + 1) % 2, product, 2)
            steady(act, step, NT, 2)

        @block.tensor
        def _(pe):
            def step(n, j, has):
                if has(1):
                    f.turn(nc, pe, k.ident, n + 1, (j + 1) % 2)
                if has(0):
                    pe.wait_ge(f.lo, n * 2 + 2)
                    if later(n, 2):
                        pe.wait_ge(result, n * 2 - 2)
                    for half in range(2):
                        for i, (a, m) in enumerate(PASSES):
                            for dt in range(DT):
                                ins = nc.tensor.matmul(psy[:, j, half, :], f.xT[:, j, a, dt, :],
                                                       weff[:, j, m, dt, half * BANK:(half + 1) * BANK],
                                                       start=(i == 0 and dt == 0), stop=(i == 2 and dt == DT - 1))
                        ins.then_inc(product, 1)
            steady(pe, step, NT, 2)

        @block.vector
        def _(dve):
            def step(n, j, has):
                if has(2):
                    f.stats_of(nc, dve, n + 2, j, loads_of(n + 2, j))
                if has(1):
                    f.split_lo(nc, dve, n + 1, (j + 1) % 2)
                if has(2):
                    if later(n, 0):
                        dve.wait_ge(f.turned, n * 2 + 2)
                    f.normalise(nc, dve, n + 2, j)
                if has(0):
                    if later(n, 2):
                        dve.wait_ge(stored[j], (n - j) * 8)
                    dve.wait_ge(with_bias, n + 1)
                    for half in range(2):
                        dve.wait_ge(product, n * 2 + half + 1)
                        w = slice(half * BANK, (half + 1) * BANK)
                        nc.vector.scalar_tensor_tensor(out=xo[:, j, w], in0=psy[:, j, half, :], scalar=0.5,
                                                             in1=xb[:, j, w], op0=ALU.mult, op1=ALU.add).then_inc(result, 1)
            steady(dve, step, NT, 2)



def latents_phase(nc, k, src_d, args):
    wa_d, lnw_d, cos_d, sin_d = args
    tag = "l_"
    with ExitStack() as stack:
        c = Ctx(nc, stack)
        f = Front(c, tag)
        wa_in = c.sb("wa_in", [P, DT, LAT])
        wa = c.sb("wa", [P, 2, DT, LAT], F32R)
        lnw = c.sb("lnw", [P, QR + KVR])
        cos = c.sb("l_cos", [P, NT, ROPE])
        sin = c.sb("l_sin", [P, NT, ROPE])
        squares = c.sb("squares", [P, 2, QR + KVR])
        ss = c.sb("ss", [P, 2, 2])
        rms = c.sb("rms", [P, 2, 2])
        inv = c.sb("l_invs", [P, 2, 2])
        lat = c.sb("lat", [P, 2, LAT])
        rot = c.sb("rot", [P, 2, 2, ROPE])
        psl = c.ps("psl", [P, 2, BANK])
        ps2 = c.ps("ps2", [P, 2, BANK])
        w_loaded, w_hi, w_lo = c.sem("l_w_loaded"), c.sem("l_w_hi"), c.sem("l_w_lo")
        small_in, scaled = c.sem("l_small_in"), c.sem("l_scaled")
        product, rooted, inverted = c.sem("l_product"), c.sem("l_rooted"), c.sem("l_inverted")
        squared = c.sem("l_squared")
        partial, latent = c.sem("l_partial"), c.sem("l_latent")
        turned2, hi2, lo2 = c.sem("l_turned2"), c.sem("l_hi2"), c.sem("l_lo2")
        block = stack.enter_context(nc.Block())

        @block.sync
        def _(sp):
            sp.dma_start(wa_in[:], wa_d.rearrange("p (a n) -> p a n", a=DT)).then_inc(w_loaded, 16)
            sp.dma_start(lnw[:], lnw_d.rearrange("(a n) -> a n", a=1).to_broadcast([P, QR + KVR])).then_inc(small_in, 16)
            sp.dma_start(cos[:], cos_d.rearrange("(t p) n -> p t n", p=P)).then_inc(small_in, 16)
            sp.dma_start(sin[:], sin_d.rearrange("(t p) n -> p t n", p=P)).then_inc(small_in, 16)

            def step(n, j, has):
                if has(2):
                    if later(n, 0):
                        sp.wait_ge(f.normed, n + 1)
                    sp.dma_start(f.xt[:, j, :], src_d[bass.ds((n + 2) * P, P), :]).then_inc(f.x_in[j], 16)
            steady(sp, step, NT, 2)

        @block.gpsimd
        def _(pool):
            pool.wait_ge(w_hi, 1)
            nc.gpsimd.tensor_tensor(wa[:, LO, :, :], wa_in[:], wa[:, HI, :, :].bitcast(F32), ALU.subtract).then_inc(w_lo, 1)

        @block.scalar
        def _(act):
            act.wait_ge(w_loaded, 16)
            nc.scalar.activation(wa[:, HI, :, :], wa_in[:], ACT.Copy).then_inc(w_hi, 1)

            def step(n, j, has):
                if has(2):
                    f.root_of(nc, act, k.eps_ln[:], n + 2, j)
                if has(1):
                    f.split_hi(nc, act, n + 1, (j + 1) % 2, product, 1)
                if has(0):
                    act.wait_ge(product, n + 1)
                    if later(n, 2):
                        act.wait_ge(inverted, n - 1)
                        act.wait_ge(squared, n - 1)
                    nc.scalar.activation(squares[:, j, 0:QR], psl[:, j, 0:QR], ACT.Square,
                                         accum_out=ss[:, j, 0:1])
                    nc.scalar.activation(squares[:, j, QR:QR + KVR], psl[:, j, QR:QR + KVR], ACT.Square,
                                         accum_out=ss[:, j, 1:2]).then_inc(squared, 1)
                    act.wait_ge(squared, n + 1)
                    nc.scalar.activation(rms[:, j, 0:1], ss[:, j, 0:1], ACT.Sqrt, bias=k.eps_rms[:], scale=1.0 / QR)
                    nc.scalar.activation(rms[:, j, 1:2], ss[:, j, 1:2], ACT.Sqrt, bias=k.eps_rms[:], scale=1.0 / KVR).then_inc(rooted, 1)
                if has(-1):
                    m, jm = n - 1, (j + 1) % 2
                    act.wait_ge(turned2, n)
                    for r in range(QRT):
                        nc.scalar.activation(k.qnT[:, HI, r, bass.ds(m * P, P)], ps2[:, jm, r * P:(r + 1) * P], ACT.Copy)
                    nc.scalar.activation(k.keyT[:, HI, bass.ds(m * P, P)], ps2[:, jm, QR:LAT], ACT.Copy)
                    nc.scalar.activation(k.val[:, bass.ds(m, 1), 0:KVR], lat[:, jm:jm + 1, QR:QR + KVR], ACT.Copy).then_inc(hi2, 1)
            steady(act, step, NT, 2, 1)

        @block.tensor
        def _(pe):
            def step(n, j, has):
                if has(1):
                    f.turn(nc, pe, k.ident, n + 1, (j + 1) % 2)
                if has(0):
                    if not later(n, 1):
                        pe.wait_ge(w_lo, 1)
                    pe.wait_ge(f.lo, n * 2 + 2)
                    if later(n, 2):
                        pe.wait_ge(latent, n - 1)
                    for i, (a, m) in enumerate(PASSES):
                        for dt in range(DT):
                            ins = nc.tensor.matmul(psl[:, j, 0:LAT], f.xT[:, j, a, dt, :], wa[:, m, dt, :],
                                                   start=(i == 0 and dt == 0), stop=(i == 2 and dt == DT - 1))
                    ins.then_inc(product, 1)
                if has(-1):
                    jm = (j + 1) % 2
                    pe.wait_ge(latent, n)
                    if later(n, 3):
                        pe.wait_ge(lo2, n - 2)
                    for r in range(LAT // P):
                        ins = nc.tensor.transpose(ps2[:, jm, r * P:(r + 1) * P], lat[:, jm, r * P:(r + 1) * P], k.ident[:])
                    ins.then_inc(turned2, 1)
            steady(pe, step, NT, 2, 1)

        @block.vector
        def _(dve):
            dve.wait_ge(small_in, 48)
            nc.vector.tensor_scalar(lnw[:, 0:QR], lnw[:, 0:QR], SCALE, None, ALU.mult).then_inc(scaled, 1)
            dve.wait_ge(scaled, 1)

            def step(n, j, has):
                if has(2):
                    f.stats_of(nc, dve, n + 2, j, loads_of(n + 2, j))
                if has(1):
                    f.split_lo(nc, dve, n + 1, (j + 1) % 2)
                if has(2):
                    if later(n, 0):
                        dve.wait_ge(f.turned, n * 2 + 2)
                    f.normalise(nc, dve, n + 2, j)
                if has(0):
                    dve.wait_ge(rooted, n + 1)
                    nc.vector.reciprocal(inv[:, j, :], rms[:, j, :]).then_inc(inverted, 1)
                    pe_cols = psl[:, j, QR + KVR:LAT]
                    half = ROPE // 2
                    if later(n, 2):
                        dve.wait_ge(turned2, n - 1)
                        dve.wait_ge(hi2, n - 1)
                    nc.vector.tensor_tensor(rot[:, j, 0, :], pe_cols, cos[:, bass.ds(n, 1), :].rearrange("p a n -> p (a n)"), ALU.mult)
                    nc.vector.tensor_tensor(rot[:, j, 1, 0:half], pe_cols[:, half:ROPE],
                                            sin[:, bass.ds(n, 1), 0:half].rearrange("p a n -> p (a n)"), ALU.mult)
                    nc.vector.tensor_tensor(rot[:, j, 1, half:ROPE], pe_cols[:, 0:half],
                                            sin[:, bass.ds(n, 1), half:ROPE].rearrange("p a n -> p (a n)"), ALU.mult).then_inc(partial, 1)
                    dve.wait_ge(inverted, n + 1)
                    nc.vector.scalar_tensor_tensor(out=lat[:, j, 0:QR], in0=psl[:, j, 0:QR], scalar=inv[:, j, 0:1],
                                                   in1=lnw[:, 0:QR], op0=ALU.mult, op1=ALU.mult)
                    nc.vector.scalar_tensor_tensor(out=lat[:, j, QR:QR + KVR], in0=psl[:, j, QR:QR + KVR], scalar=inv[:, j, 1:2],
                                                   in1=lnw[:, QR:QR + KVR], op0=ALU.mult, op1=ALU.mult)
                    dve.wait_ge(partial, n + 1)
                    nc.vector.tensor_tensor(lat[:, j, QR + KVR:LAT], rot[:, j, 0, :], rot[:, j, 1, :], ALU.add).then_inc(latent, 1)
                if has(-1):
                    m, jm = n - 1, (j + 1) % 2
                    dve.wait_ge(hi2, n)
                    for r in range(QRT):
                        nc.vector.tensor_tensor(k.qnT[:, LO, r, bass.ds(m * P, P)], ps2[:, jm, r * P:(r + 1) * P],
                                                k.qnT[:, HI, r, bass.ds(m * P, P)].bitcast(F32), ALU.subtract)
                    nc.vector.tensor_tensor(k.keyT[:, LO, bass.ds(m * P, P)], ps2[:, jm, QR:LAT],
                                            k.keyT[:, HI, bass.ds(m * P, P)].bitcast(F32), ALU.subtract)
                    nc.vector.tensor_tensor(k.val[:, bass.ds(m, 1), KVR:2 * KVR], lat[:, jm:jm + 1, QR:QR + KVR],
                                            k.val[:, bass.ds(m, 1), 0:KVR].bitcast(F32), ALU.subtract).then_inc(lo2, 1)
            steady(dve, step, NT, 2, 1)



TILES = 4 * QT
GROUPS = tuple((t, kt, min(4, t + 1 - kt)) for t in range(QT) for kt in range(0, t + 1, 4))
NG = len(GROUPS)
PE_STEP = ("S0+0 T6-1 T7-1 Q0+1 S1+0 S2+0 T8-1 T9-1 Q1+1 S3+0 T10-1 T11-1 F0+0 S4+0 S5+0 T0+0 T1+0 V1-1 "
             "T2+0 S6+0 T3+0 S7+0 T4+0 W0+0 T5+0 V0+0")
ACT_STEP = ("E0+0 T7-1 V0-1 Q0+1 E1+0 T8-1 T9-1 E2+0 Q1+1 T10-1 E3+0 T11-1 T0+0 F0+0 T1+0 E4+0 E5+0 T2+0 "
             "V1-1 T3+0 E6+0 T4+0 W0+0 T5+0 E7+0 T6+0")
DVE_STEP = ("T11-1 M4+0 M5+0 P2+0 P3+0 H0+1 T0+0 P4+0 T1+0 P5+0 F0+0 T2+0 M6+0 V1-1 T3+0 M7+0 T4+0 T5+0 "
             "P6+0 M0+1 H1+1 T6+0 T7+0 M1+1 P7+0 M2+1 T8+0 T9+0 P0+1 M3+1 P1+1 V0+0 T10+0")
POOL_STEP = "Q0+1 Q1+1"


def parse(table):
    return [(job[0], int(job[1:-2]), int(job[-2:])) for job in table.split()]


class Round:

    def __init__(self, it, first=False, last=False):
        self.it, self.first, self.last = it, first, last
        self.keys = [job for job in self.jobs(PE_STEP) if job[0] in "QFW"]
        self.before = 2 if first else it * len(STEADY.keys) + 2 + len(FIRST.keys) - len(STEADY.keys)

    def jobs(self, table):
        for step in range(-1 if self.first else 0, 6 if self.last else 4):
            for job, n, shift in parse(table):
                s = step + shift
                absent = job == "F" and (s % 4 < 2 or self.last)
                if not absent and not (self.first and s < 0) and not (self.last and s > 3) and (shift > 0 or step >= 0) \
                        and (shift < 0 or step < 4):
                    yield job, n, s

    def use(self, *key):
        if key in self.keys:
            return self.before + self.keys.index(key)
        job, n, s = key
        return self.before - len(STEADY.keys) + STEADY.keys.index((job, n, s + 4))


class _Plain(Round):
    def __init__(self, first):
        self.first, self.last = first, False
        self.keys = [job for job in self.jobs(PE_STEP) if job[0] in "QFW"]


STEADY, FIRST = _Plain(False), _Plain(True)


def rounds(eng, body):
    body(Round(0, first=True))
    with eng.Fori(1, PAIRS - 1) as it:
        body(Round(it))
    body(Round(PAIRS - 1, last=True))


def attention_phase(nc, k, args, oT_d, wvo_d):
    wn_d, wpe_d, wv_d, wo_d, cosT_d, sinT_d = args
    with ExitStack() as stack:
        c = Ctx(nc, stack)
        wn = c.sb("wn", [64, 2, QR + KVR])
        wpe = c.sb("wpe", [P, 2, QRT, ROPE])
        wv = c.sb("wv", [P, 2, KVR])
        wo = c.sb("wo", [P, 2, D])
        wvo = c.sb("wvo", [64, 2, BANK])
        wq = c.sb("wq", [P, 2, 2, QRT, QHD], F32R)
        cosT = c.sb("cosT", [P, S])
        sinT = c.sb("sinT", [P, S])
        qf = c.sb("qf", [P, 2, CHUNK])
        rot = c.sb("q_rot", [P, 2, CHUNK])
        q = c.sb("q", [P, 2, 2, S], F32R)
        prob = c.sb("prob", [P, 4, S])
        pT0 = c.sb("pT0", [P, 2, 4, CHUNK], F32R)
        pT1 = c.sb("pT1", [P, 2, 8, CHUNK], F32R)
        pT = (pT0, pT1)
        negmax = c.sb("negmax", [P, 8])
        rowsum = c.sb("rowsum", [P, 8])
        rinv = c.sb("rinv", [P, 8])
        lower = c.sb("lower", [64, CHUNK])
        o_sum = c.sb("o_sum", [P, 2, CHUNK])
        psS = c.ps("psS", [P, 2, 2 * BANK])
        psT = c.ps("psT", [P, 2, BANK])
        psV = c.ps("psV", [P, BANK])
        psM = c.ps("psM", [P, BANK])
        tab_in, wn_in, wo_in = c.sem("tab_in"), c.sem("wn_in"), c.sem("wo_in")
        zeroed = c.sem("zeroed")
        scored, maxed, exped, recip, scaled = c.sem("scored"), c.sem("maxed"), c.sem("exped"), c.sem("recip"), c.sem("scaled")
        turned, p_hi, p_lo = c.sem("p_turned"), c.sem("p_hi"), c.sem("p_lo")
        valued, lowered, joined = c.sem("valued"), c.sem("lowered"), c.sem("joined")
        m_done, m_free = c.sem("m_done"), c.sem("m_free")
        rope_parts, roped, q_hi, q_lo = c.sem("rope_parts"), c.sem("roped"), c.sem("q_hi"), c.sem("q_lo")
        wq_hi = c.sem("wq_hi")
        o_stored = [[c.sem(f"o_stored{e}{ch}") for ch in range(2)] for e in range(2)]
        w_stored = [c.sem(f"w_stored{n}") for n in range(2)]
        block = stack.enter_context(nc.Block())

        def place(s, t):
            x = P if t == 4 else 0
            return psS[:, (QT * s + t) % 2, x:x + (t + 1) * P]

        @block.sync
        def _(sp):
            def load_fold(pair):
                sp.dma_start(wn[:], wn_d[bass.ds(pair, 1), :, :].rearrange("a p n -> (a p) n").rearrange("p (e n) -> p e n", e=2)).then_inc(wn_in, 16)
                sp.dma_start(wpe[:].rearrange("p e r n -> p (e r n)"), wpe_d[bass.ds(pair, 1), :, :].rearrange("a p n -> (a p) n")).then_inc(wn_in, 16)

            def load_out(pair):
                sp.dma_start(wv[:].rearrange("p e n -> p (e n)"), wv_d[bass.ds(pair, 1), :, :].rearrange("a p n -> (a p) n")).then_inc(wo_in, 16)
                sp.dma_start(wo[:].rearrange("p e n -> p (e n)"), wo_d[bass.ds(pair, 1), :, :].rearrange("a p n -> (a p) n")).then_inc(wo_in, 16)

            load_fold(0)
            sp.dma_start(cosT[:], cosT_d[:, :]).then_inc(tab_in, 16)
            sp.dma_start(sinT[:], sinT_d[:, :]).then_inc(tab_in, 16)
            load_out(0)

            def body(r):
                def store_o(pair, s, ch):
                    e, b = s % 2, (s // 2) % 2
                    sp.wait_ge(joined, r.it * 8 + 2 * s + ch + 1)
                    sp.dma_start(oT_d[bass.ds(pair * P + e * KVR, KVR), b * S + ch * CHUNK:b * S + (ch + 1) * CHUNK],
                                 o_sum[e * KVR:(e + 1) * KVR, ch, :]).then_inc(o_stored[e][ch], 16)

                def store_w(s):
                    e, half = s // 2, s % 2
                    sp.wait_ge(m_free, r.use("W", 0, s) + 1)
                    sp.dma_start(wvo_d[bass.ds(r.it * P + e * KVR, KVR), half * BANK:(half + 1) * BANK],
                                 wvo[:, half, :]).then_inc(w_stored[half], 16)

                if not r.last:
                    sp.wait_ge(m_free, 2 if r.first else r.use("F", 0, -1) + 1)
                    load_fold(r.it + 1)
                for s in range(4):
                    if s > 0:
                        store_o(r.it, s - 1, 1)
                    elif not r.first:
                        store_o(r.it - 1, -1, 1)
                    store_w(s)
                    store_o(r.it, s, 0)
                if r.last:
                    store_o(r.it, 3, 1)
                else:
                    load_out(r.it + 1)
            rounds(sp, body)
            for n in range(2):
                for e in range(2):
                    sp.wait_ge(o_stored[e][n], 16 * 2 * PAIRS)
                sp.wait_ge(w_stored[n], 16 * 2 * PAIRS)

        @block.tensor
        def _(pe):
            def fold_queries(e, count):
                if count >= 1 if isinstance(count, int) else True:
                    pe.wait_ge(m_free, count)
                for t in range(QRT):
                    ins = nc.tensor.matmul(psM[:, t * NOPE:(t + 1) * NOPE], wn[:, e, t * P:(t + 1) * P], wn[:, e, QR:QR + KVR],
                                           start=True, stop=True)
                ins.then_inc(m_done, 1)

            def queries(s, ch, count):
                e, b = s % 2, (s // 2) % 2
                pe.wait_ge(m_free, count)
                for n, (a, m) in enumerate(PASSES):
                    for t in range(QRT):
                        ins = nc.tensor.matmul(psM[:, :], wq[:, a, e, t, :], k.qnT[:, m, t, b * S + ch * CHUNK:b * S + (ch + 1) * CHUNK],
                                               start=(n == 0 and t == 0), stop=(n == 2 and t == QRT - 1))
                ins.then_inc(m_done, 1)

            def scores(it, s, t):
                li, b = QT * s + t, (s // 2) % 2
                if later(it * TILES + li - 1, 1):
                    pe.wait_ge(exped, it * TILES + li - 1)
                if t % 4 == 0:
                    pe.wait_ge(q_lo, it * 8 + 2 * s + t // 4 + 1)
                width = max(2 * P, (t + 1) * P)
                shift, cut = (P, BANK - P) if t == 4 else (0, BANK)
                pieces = [(0, min(width, cut))] + ([(cut, width)] if width > cut else [])
                for x0, x1 in pieces:
                    x1 = max(x1, x0 + 2 * P)
                    for n, (a, m) in enumerate(PASSES):
                        ins = nc.tensor.matmul(psS[:, li % 2, shift + x0:shift + x1], q[:, s % 2, a, t * P:(t + 1) * P],
                                               k.keyT[:, m, b * S + x0:b * S + x1], start=(n == 0), stop=(n == 2))
                        if n == 0 and x0 <= t * P < x1:
                            nc.tensor.matmul(psS[:, li % 2, shift + t * P:shift + (t + 1) * P], k.ident_bf[:], k.mask_bf[:],
                                             start=False, stop=False)
                ins.then_inc(scored, 1)

            def transposes(it, s, g):
                t, k0, blocks = GROUPS[g]
                if k0 == 0:
                    pe.wait_ge(scaled, it * TILES + QT * s + t + 1)
                if later(it * 4 * NG + NG * s + g - 1, 1):
                    pe.wait_ge(p_lo, it * 4 * NG + NG * s + g - 1)
                for kt in range(blocks):
                    ins = nc.tensor.transpose(psT[:, (NG * s + g) % 2, kt * P:(kt + 1) * P],
                                              prob[:, (QT * s + t) % 4, (k0 + kt) * P:(k0 + kt + 1) * P], k.ident[:])
                ins.then_inc(turned, 1)

            def values(it, s, ch):
                b, last = (s // 2) % 2, 4 * ch + 3
                groups = sum(t <= last for t, _, _ in GROUPS)
                pe.wait_ge(p_lo, it * 4 * NG + NG * s + groups)
                if later(it * 8 + 2 * s + ch, 1):
                    pe.wait_ge(joined, it * 8 + 2 * s + ch)
                for kt in range(last + 1):
                    n0 = min(max(kt - 4 * ch, 0), 2) * P
                    for part in (HI, LO):
                        ins = nc.tensor.matmul(psV[:, n0:CHUNK], k.val[:, b * QT + kt, :], pT[ch][:, part, kt, n0:CHUNK],
                                               start=(kt == 0 and part == HI), stop=(kt == last and part == LO))
                ins.then_inc(valued, 1)

            def fold_output(it, s, count):
                e, half = s // 2, s % 2
                if s == 0:
                    pe.wait_ge(wo_in, (it + 1) * 32)
                pe.wait_ge(m_free, count)
                nc.tensor.matmul(psM[0:KVR, :], wv[:, e, :], wo[:, e, half * BANK:(half + 1) * BANK],
                                 start=True, stop=True).then_inc(m_done, 1)

            pe.wait_ge(wn_in, 32)
            for e in range(2):
                fold_queries(e, e)
            pe.wait_ge(zeroed, 2)

            def body(r):
                for job, n, s in r.jobs(PE_STEP):
                    if job == "S":
                        scores(r.it, s, n)
                    elif job == "T":
                        transposes(r.it, s, n)
                    elif job == "V":
                        values(r.it, s, n)
                    elif job == "Q":
                        queries(s, n, r.use(job, n, s))
                    elif job == "W":
                        fold_output(r.it, s, r.use(job, n, s))
                    elif job == "F":
                        if s == 2:
                            pe.wait_ge(wn_in, (r.it + 2) * 32)
                        fold_queries(s - 2, r.use(job, n, s))
            rounds(pe, body)

        @block.scalar
        def _(act):
            def split_queries_hi(e, count):
                act.wait_ge(m_done, count + 1)
                nc.scalar.activation(wq[:, HI, e, :, 0:NOPE], psM[:, 0:QRT * NOPE].rearrange("p (t n) -> p t n", t=QRT), ACT.Copy)
                nc.scalar.activation(wq[:, HI, e, :, NOPE:QHD], wpe[:, e, :, :], ACT.Copy).then_inc(wq_hi, 1)

            def copy_queries(ch, number, count):
                act.wait_ge(m_done, count + 1)
                if later(number, 2):
                    act.wait_ge(q_lo, number - 1)
                nc.scalar.activation(qf[:, ch, :], psM[:, :], ACT.Copy).then_inc(m_free, 1)

            def exponentials(it, s, t):
                li = QT * s + t
                act.wait_ge(maxed, it * TILES + li + 1)
                groups = NG * ((li - 4) // QT) + sum(g[0] <= (li - 4) % QT for g in GROUPS)
                if later(it * 4 * NG + groups, 1):
                    act.wait_ge(turned, it * 4 * NG + groups)
                nc.scalar.activation(prob[:, li % 4, 0:(t + 1) * P], place(s, t), ACT.Exp,
                                     bias=negmax[:, li % 8:li % 8 + 1], scale=1.0,
                                     accum_out=rowsum[:, li % 8:li % 8 + 1]).then_inc(exped, 1)

            def split_hi(it, s, g):
                t, k0, blocks = GROUPS[g]
                ch, x = t // 4, (t % 4) * P
                act.wait_ge(turned, it * 4 * NG + NG * s + g + 1)
                nc.scalar.activation(pT[ch][:, HI, k0:k0 + blocks, x:x + P],
                                     psT[:, (NG * s + g) % 2, 0:blocks * P].rearrange("p (a b) -> p a b", a=blocks), ACT.Copy).then_inc(p_hi, 1)

            def lower_half(it, s, ch):
                act.wait_ge(valued, it * 8 + 2 * s + ch + 1)
                nc.scalar.activation(lower[:, :], psV[KVR:2 * KVR, :], ACT.Copy).then_inc(lowered, 1)

            def copy_output_weights(it, s, count):
                act.wait_ge(m_done, count + 1)
                if later(it * 4 + s, 2):
                    act.wait_ge(w_stored[s % 2], (it * 2 + s // 2) * 16)
                nc.scalar.activation(wvo[:, s % 2, :], psM[0:KVR, :], ACT.Copy).then_inc(m_free, 1)

            for e in range(2):
                split_queries_hi(e, e)

            def body(r):
                for job, n, s in r.jobs(ACT_STEP):
                    if job == "E":
                        exponentials(r.it, s, n)
                    elif job == "T":
                        split_hi(r.it, s, n)
                    elif job == "V":
                        lower_half(r.it, s, n)
                    elif job == "Q":
                        copy_queries(n, r.it * 8 + 2 * s + n, r.use(job, n, s))
                    elif job == "W":
                        copy_output_weights(r.it, s, r.use(job, n, s))
                    elif job == "F":
                        split_queries_hi(s - 2, r.use(job, n, s))
            rounds(act, body)

        @block.vector
        def _(dve):
            def split_queries_lo(e, count):
                dve.wait_ge(wq_hi, count)
                nc.vector.tensor_tensor(wq[:, LO, e, :, NOPE:QHD], wpe[:, e, :, :], wq[:, HI, e, :, NOPE:QHD].bitcast(F32), ALU.subtract)
                nc.vector.tensor_tensor(wq[:, LO, e, :, 0:NOPE], psM[:, 0:QRT * NOPE].rearrange("p (t n) -> p t n", t=QRT),
                                        wq[:, HI, e, :, 0:NOPE].bitcast(F32), ALU.subtract).then_inc(m_free, 1)

            def query_hi(s, ch, number):
                dve.wait_ge(roped, number + 1)
                nc.vector.tensor_copy(q[:, s % 2, HI, ch * CHUNK:(ch + 1) * CHUNK], qf[:, ch, :]).then_inc(q_hi, 1)

            def maxima(it, s, t):
                li = QT * s + t
                dve.wait_ge(scored, it * TILES + li + 1)
                nc.vector.tensor_reduce(negmax[:, li % 8:li % 8 + 1], place(s, t), AX_X, ALU.max, negate=True).then_inc(maxed, 1)

            def divide(it, s, t):
                li = QT * s + t
                dve.wait_ge(exped, it * TILES + li + 1)
                nc.vector.reciprocal(rinv[:, li % 8:li % 8 + 1], rowsum[:, li % 8:li % 8 + 1]).then_inc(recip, 1)
                dve.wait_ge(recip, it * TILES + li + 1)
                nc.vector.tensor_scalar(prob[:, li % 4, 0:(t + 1) * P], prob[:, li % 4, 0:(t + 1) * P],
                                        rinv[:, li % 8:li % 8 + 1], None, ALU.mult).then_inc(scaled, 1)

            def split_lo(it, s, g):
                t, k0, blocks = GROUPS[g]
                ch, x = t // 4, (t % 4) * P
                dve.wait_ge(p_hi, it * 4 * NG + NG * s + g + 1)
                nc.vector.tensor_tensor(pT[ch][:, LO, k0:k0 + blocks, x:x + P],
                                        psT[:, (NG * s + g) % 2, 0:blocks * P].rearrange("p (a b) -> p a b", a=blocks),
                                        pT[ch][:, HI, k0:k0 + blocks, x:x + P].bitcast(F32), ALU.subtract).then_inc(p_lo, 1)

            def join(it, s, ch):
                e = s % 2
                dve.wait_ge(lowered, it * 8 + 2 * s + ch + 1)
                if later(it * 4 + s, 2):
                    dve.wait_ge(o_stored[e][ch], it * 32 + 16 * (s // 2))
                nc.vector.tensor_tensor(o_sum[KVR * e:KVR * e + KVR, ch, :], psV[0:KVR, :], lower[:, :], ALU.add).then_inc(joined, 1)

            nc.vector.memset(pT0[:, :, 3, 2 * P:3 * P].bitcast(F32), 0.0).then_inc(zeroed, 1)
            nc.vector.memset(pT1[:, :, 7, 2 * P:3 * P].bitcast(F32), 0.0).then_inc(zeroed, 1)
            for e in range(2):
                split_queries_lo(e, e + 1)

            def body(r):
                for job, n, s in r.jobs(DVE_STEP):
                    if job == "M":
                        maxima(r.it, s, n)
                    elif job == "P":
                        divide(r.it, s, n)
                    elif job == "T":
                        split_lo(r.it, s, n)
                    elif job == "V":
                        join(r.it, s, n)
                    elif job == "H":
                        query_hi(s, n, r.it * 8 + 2 * s + n)
                    elif job == "F":
                        split_queries_lo(s - 2, r.it * 2 + 2 + s - 1)
            rounds(dve, body)

        @block.gpsimd
        def _(pool):
            def rope(s, ch, number, count):
                x = slice(ch * CHUNK, (ch + 1) * CHUNK)
                if later(number, 1):
                    pool.wait_ge(q_lo, number)
                pool.wait_ge(m_free, count + 1)
                nc.gpsimd.tensor_tensor(rot[64:128, 0, :], qf[64:128, ch, :], cosT[64:128, x], ALU.mult).then_inc(rope_parts, 1)
                pool.wait_ge(rope_parts, number * 3 + 1)
                nc.gpsimd.tensor_tensor(rot[64:96, 1, :], qf[96:128, ch, :], sinT[96:128, x], ALU.mult).then_inc(rope_parts, 1)
                pool.wait_ge(rope_parts, number * 3 + 2)
                nc.gpsimd.tensor_tensor(rot[96:128, 1, :], qf[64:96, ch, :], sinT[64:96, x], ALU.mult).then_inc(rope_parts, 1)
                pool.wait_ge(rope_parts, number * 3 + 3)
                nc.gpsimd.tensor_tensor(qf[64:128, ch, :], rot[64:128, 0, :], rot[64:128, 1, :], ALU.add).then_inc(roped, 1)
                pool.wait_ge(q_hi, number + 1)
                nc.gpsimd.tensor_tensor(q[:, s % 2, LO, x], qf[:, ch, :], q[:, s % 2, HI, x].bitcast(F32), ALU.subtract).then_inc(q_lo, 1)

            pool.wait_ge(tab_in, 32)

            def body(r):
                for job, n, s in r.jobs(POOL_STEP):
                    rope(s, n, r.it * 8 + 2 * s + n, r.use(job, n, s))
            rounds(pool, body)



def output_phase(nc, src_d, dst_d, oT_d, wvo_d):
    with ExitStack() as stack:
        c = Ctx(nc, stack)
        w_in = c.sb("o_w_in", [P, 2, D])
        w = c.sb("o_w", [P, 2, PAIRS, D], F32R)
        o_in = c.sb("o_in", [P, PAIRS, P])
        o = c.sb("o_o", [P, 2, 2, PAIRS, P], F32R)
        x_in = c.sb("o_x_in", [P, 2, D])
        y = c.sb("o_y", [P, 2, D])
        psy = c.ps("o_psy", [P, 2, 2, BANK])
        w_loaded = [c.sem(f"o_w_loaded{j}") for j in range(2)]
        w_hi, w_lo = c.sem("o_w_hi"), c.sem("o_w_lo")
        o_loaded, o_hi, o_lo = c.sem("o_loaded"), c.sem("o_hi"), c.sem("o_lo")
        x_loaded = [c.sem(f"o_x_loaded{j}") for j in range(2)]
        product, result = c.sem("o_product"), c.sem("o_result")
        stored = [c.sem(f"o_y_stored{j}") for j in range(2)]
        block = stack.enter_context(nc.Block())
        oT_v = oT_d.rearrange("(a p) t -> p a t", p=P)

        @block.sync
        def _(sp):
            for pair in range(PAIRS):
                if pair == 1:
                    sp.dma_start(o_in[:], oT_v[:, :, 0:P]).then_inc(o_loaded, 16)
                if pair >= 2:
                    sp.wait_ge(w_lo, pair - 1)
                sp.dma_start(w_in[:, pair % 2, :], wvo_d[pair * P:(pair + 1) * P, :]).then_inc(w_loaded[pair % 2], 16)

            def step(n, j, has):
                if has(1):
                    sp.wait_ge(o_lo, n + 1)
                    sp.dma_start(o_in[:], oT_v[:, :, bass.ds((n + 1) * P, P)]).then_inc(o_loaded, 16)
                if has(0):
                    if later(n, 2):
                        sp.wait_ge(result, n * 2 - 2)
                    sp.dma_start(x_in[:, j, :], src_d[bass.ds(n * P, P), :]).then_inc(x_loaded[j], 16)
                if has(-1):
                    sp.wait_ge(result, n * 2)
                    jm = (j + 1) % 2
                    sp.dma_start(dst_d[bass.ds((n - 1) * P, P), :], y[:, jm, :]).then_inc(stored[jm], 16)
            output_steps(sp, step)
            for j in range(2):
                sp.wait_ge(stored[j], 16 * NT // 2)

        @block.scalar
        def _(act):
            for pair in range(PAIRS):
                act.wait_ge(w_loaded[pair % 2], 16 * (pair // 2 + 1))
                nc.scalar.activation(w[:, HI, pair, :], w_in[:, pair % 2, :], ACT.Copy).then_inc(w_hi, 1)
                if pair == 1:
                    act.wait_ge(o_loaded, 16)
                    nc.scalar.activation(o[:, 0, HI, :, :], o_in[:], ACT.Copy).then_inc(o_hi, 1)

            def step(n, j, has):
                if has(1):
                    jm = (j + 1) % 2
                    act.wait_ge(o_loaded, (n + 2) * 16)
                    if later(n, 1):
                        act.wait_ge(product, n * 2)
                    nc.scalar.activation(o[:, jm, HI, :, :], o_in[:], ACT.Copy).then_inc(o_hi, 1)
            output_steps(act, step)

        @block.vector
        def _(dve):
            for pair in range(PAIRS):
                dve.wait_ge(w_hi, pair + 1)
                nc.vector.tensor_tensor(w[:, LO, pair, :], w_in[:, pair % 2, :], w[:, HI, pair, :].bitcast(F32), ALU.subtract).then_inc(w_lo, 1)
                if pair == 1:
                    dve.wait_ge(o_hi, 1)
                    nc.vector.tensor_tensor(o[:, 0, LO, :, :], o_in[:], o[:, 0, HI, :, :].bitcast(F32), ALU.subtract).then_inc(o_lo, 1)

            def step(n, j, has):
                if has(1):
                    jm = (j + 1) % 2
                    dve.wait_ge(o_hi, n + 2)
                    nc.vector.tensor_tensor(o[:, jm, LO, :, :], o_in[:], o[:, jm, HI, :, :].bitcast(F32), ALU.subtract).then_inc(o_lo, 1)
                if has(0):
                    dve.wait_ge(x_loaded[j], loads_of(n, j))
                    if later(n, 2):
                        dve.wait_ge(stored[j], (n - j) * 8)
                    for half in range(2):
                        x = slice(half * BANK, (half + 1) * BANK)
                        dve.wait_ge(product, n * 2 + half + 1)
                        nc.vector.tensor_tensor(y[:, j, x], psy[:, j, half, :], x_in[:, j, x], ALU.add).then_inc(result, 1)
            output_steps(dve, step)

        @block.tensor
        def _(pe):
            def step(n, j, has):
                if has(0):
                    pe.wait_ge(o_lo, n + 1)
                    if later(n, 2):
                        pe.wait_ge(result, n * 2 - 2)
                    for half in range(2):
                        for pair in range(PAIRS):
                            if not later(n, 1) and half == 0:
                                pe.wait_ge(w_lo, pair + 1)
                            for i, (a, m) in enumerate(PASSES):
                                ins = nc.tensor.matmul(psy[:, j, half, :], o[:, j, a, pair, :], w[:, m, pair, half * BANK:(half + 1) * BANK],
                                                       start=(pair == 0 and i == 0), stop=(pair == PAIRS - 1 and i == 2))
                        ins.then_inc(product, 1)
            output_steps(pe, step)


def output_steps(eng, step):
    steady(eng, step, NT, 1, 1, start=0)



def macaron_block(nc, x, wa, lnw, wn, wpe, wv, wo, cos, sin, cosT, sinT, w, bias, lora_a, lora_b, starts, out):
    x1_d = nc.dram_tensor("x1", (T, D), F32).ap()
    x2_d = nc.dram_tensor("x2", (T, D), F32).ap()
    oT_d = nc.dram_tensor("oT", (PAIRS * P, T), F32).ap()
    wvo_d = nc.dram_tensor("wvo_fold", (PAIRS * P, D), F32).ap()
    with ExitStack() as stack:
        c = Ctx(nc, stack)
        k = Shared()
        k.ident = c.sb("ident", [P, P])
        k.ident_bf = c.sb("ident_bf", [P, P], BF16)
        k.mask_bf = c.sb("mask_bf", [P, P], BF16)
        k.eps_ln = c.sb("eps_ln", [P, 1])
        k.eps_rms = c.sb("eps_rms", [P, 1])
        constants_phase(nc, k)
        ffn_args = (w, bias, lora_a, lora_b, starts)

        def feed_forward(tag, src_d, dst_d):
            with ExitStack() as inner:
                ci = Ctx(nc, inner)
                weff = ci.sb(tag + "weff", [P, B, 2, DT, D], F32R)
                bias_half = ci.sb(tag + "bias_half", [P, D])
                ffn_weights_phase(nc, tag + "w_", w, (lora_a, lora_b), weff, bias_half, ffn_args)
                ffn_phase(nc, tag, k, src_d, dst_d, weff, bias_half)

        feed_forward("f1_", x, x1_d)
        with ExitStack() as inner:
            ci = Ctx(nc, inner)
            k.qnT = ci.sb("qnT", [P, 2, QRT, T], F32R)
            k.keyT = ci.sb("keyT", [P, 2, T], F32R)
            k.val = ci.sb("val", [P, NT, 2 * KVR], F32R)
            latents_phase(nc, k, x1_d, (wa, lnw, cos, sin))
            attention_phase(nc, k, (wn, wpe, wv, wo, cosT, sinT), oT_d, wvo_d)
        output_phase(nc, x1_d, x2_d, oT_d, wvo_d)
        feed_forward("f2_", x2_d, out)


class Shared:
    pass


def rope_tables():
    import math
    dim, base, factor, beta_fast, beta_slow, orig_max = ROPE, 10000.0, 128.0, 32.0, 1.0, 2048

    def corr_dim(r):
        return dim * math.log(orig_max / (r * 2 * math.pi)) / (2 * math.log(base))
    low = max(math.floor(corr_dim(beta_fast)), 0)
    high = min(math.ceil(corr_dim(beta_slow)), dim - 1)
    hi = high + 0.001 if low == high else float(high)
    ramp = np.clip((np.arange(dim // 2, dtype=np.float32) - low) / (hi - low), 0.0, 1.0)
    keep = 1.0 - ramp
    freq_extra = 1.0 / base ** (np.arange(0, dim, 2, dtype=np.float32) / dim)
    freq_inter = freq_extra / factor
    inv_freq = freq_inter * (1.0 - keep) + freq_extra * keep
    freqs = np.outer(np.arange(S, dtype=np.float32), inv_freq)
    emb = np.concatenate([freqs, freqs], axis=-1)
    sign = np.where(np.arange(ROPE) < ROPE // 2, -1.0, 1.0)
    return np.cos(emb).astype(np.float32), (np.sin(emb) * sign).astype(np.float32)


def kernel(**inputs):
    import numpy as _np
    import concourse.bacc as _bacc
    from concourse import mybir as _mybir
    from concourse.bass_utils import run_bass_kernel_spmd as _run

    get = lambda name: _np.asarray(inputs[name])
    wq_b = get("L0_attn_wq_b").reshape(PAIRS, 2, QHD, QR)
    wkv_b = get("L0_attn_wkv_b").reshape(PAIRS, 2, NOPE + VD, KVR)
    wkv_a = get("L0_attn_wkv_a")
    halves = _np.concatenate([_np.arange(0, ROPE, 2), _np.arange(1, ROPE, 2)])
    cos, sin = rope_tables()
    blank = _np.zeros((NOPE, S), _np.float32)
    data = {
        "x": get("L0_attn_x").reshape(T, D),
        "wa": _np.concatenate([get("L0_attn_wq_a"), wkv_a[:KVR], wkv_a[KVR:][halves]], 0).T.reshape(DT, P, LAT).transpose(1, 0, 2).reshape(P, DT * LAT),
        "lnw": _np.concatenate([get("L0_attn_q_a_ln_w"), get("L0_attn_kv_a_ln_w")]),
        "wn": _np.concatenate([wq_b[:, :, :NOPE], wkv_b[:, :, :NOPE]], 3).transpose(0, 2, 1, 3).reshape(PAIRS, NOPE, 2 * (QR + KVR)),
        "wpe": wq_b[:, :, NOPE:][:, :, halves].reshape(PAIRS, 2, ROPE, QRT, P).transpose(0, 4, 1, 3, 2).reshape(PAIRS, P, 2 * QRT * ROPE),
        "wv": wkv_b[:, :, NOPE:].transpose(0, 2, 1, 3).reshape(PAIRS, VD, 2 * KVR),
        "wo": get("L0_attn_wo").T.reshape(PAIRS, 2, VD, D).transpose(0, 2, 1, 3).reshape(PAIRS, VD, 2 * D),
        "cos": _np.concatenate([cos, cos], 0), "sin": _np.concatenate([sin, sin], 0),
        "cosT": _np.concatenate([blank, cos.T], 0),
        "sinT": _np.concatenate([blank, sin.T[ROPE // 2:], sin.T[:ROPE // 2]], 0),
        "w": get("L0_ffn_weight").T.reshape(DT, P, D).transpose(1, 0, 2).reshape(P, DT * D),
        "bias": get("L0_ffn_bias"),
        "lora_a": get("L0_ffn_lora_A"),
        "lora_b": get("L0_ffn_lora_B").transpose(0, 2, 1),
        "starts": get("L0_ffn_lora_start_indices"),
    }
    nc = _bacc.Bacc("TRN2", target_bir_lowering=False, num_devices=1)
    arrays, args = {}, []
    for name, a in data.items():
        a = _np.ascontiguousarray(a)
        arrays[f"in_{name}"] = a
        args.append(nc.dram_tensor(f"in_{name}", a.shape, _mybir.dt.from_np(a.dtype), kind="ExternalInput").ap())
    args.append(nc.dram_tensor("out_0", (T, D), F32, kind="ExternalOutput").ap())
    macaron_block(nc, *args)
    r = _run(nc, [arrays], core_ids=[0])
    return r.results[0]["out_0"].reshape(B, S, D)
```

```python
from contextlib import ExitStack

import numpy as np

import concourse.bass as bass
from concourse import mybir

ALU = mybir.AluOpType
ACT = mybir.ActivationFunctionType
AX_X = mybir.AxisListType.X
F32 = mybir.dt.float32
F32R = mybir.dt.float32r
BF16 = mybir.dt.bfloat16
I32 = mybir.dt.int32

P = 128
BANK = 512
B, S, D = 2, 1024, 1024
T = B * S
NT = T // P
DT = D // P
H = 32
PAIRS = H // 2
NOPE, ROPE, VD = 64, 64, 128
QHD = NOPE + ROPE
KVR = 64
QR = 256
QRT = QR // P
LAT = QR + KVR + ROPE
RANK = 16
ADAPTERS = 3
STARTS = 4
QT = S // P
CHUNK = 512
MSCALE = 0.1 * 1.0 * float(np.log(128.0)) + 1.0
SCALE = QHD ** -0.5 * MSCALE * MSCALE
LN_EPS = 1e-5
RMS_EPS = 1e-6
MASKED = -3.0e38

HI, LO = 0, 1
PASSES = ((HI, HI), (LO, HI), (HI, LO))


class Ctx:

    def __init__(self, nc, stack):
        self.nc, self.stack = nc, stack

    def sb(self, name, shape, dt=F32):
        return self.stack.enter_context(self.nc.sbuf_tensor(name, shape, dt))

    def ps(self, name, shape, dt=F32):
        return self.stack.enter_context(self.nc.psum_tensor(name, shape, dt))

    def sem(self, name):
        return self.stack.enter_context(self.nc.semaphore(name))


def steady(eng, body, steps, lead, lag=0, start=None):
    first = 4
    rounds = (steps - lead) // 2
    for n in range(-lead if start is None else start, first):
        body(n, n % 2, lambda m, n=n: 0 <= n + m < steps)
    with eng.Fori(first // 2, rounds) as r:
        for j in range(2):
            body(r * 2 + j, j, lambda m: True)
    for n in range(2 * rounds, steps + lag):
        body(n, n % 2, lambda m, n=n: 0 <= n + m < steps)


def later(n, least):
    return not isinstance(n, int) or n >= least



def constants_phase(nc, k):
    with ExitStack() as stack:
        c = Ctx(nc, stack)
        cleared, made = c.sem("c_cleared"), c.sem("c_made")
        block = stack.enter_context(nc.Block())

        @block.gpsimd
        def _(pool):
            nc.gpsimd.memset(k.ident[:], 0.0).then_inc(cleared, 1)
            nc.gpsimd.memset(k.ident_bf[:], 0.0).then_inc(cleared, 1)
            nc.gpsimd.memset(k.mask_bf[:], 0.0).then_inc(cleared, 1)
            nc.gpsimd.memset(k.eps_ln[:], LN_EPS)
            nc.gpsimd.memset(k.eps_rms[:], RMS_EPS)
            pool.wait_ge(cleared, 3)
            for m in (k.ident, k.ident_bf):
                nc.gpsimd.affine_select(out=m[:], in_=m[:], compare_op=ALU.not_equal, fill=1.0, base=0,
                                        pattern=[[-1, P]], channel_multiplier=1).then_inc(made, 1)
            nc.gpsimd.affine_select(out=k.mask_bf[:], in_=k.mask_bf[:], compare_op=ALU.is_ge, fill=MASKED, base=0,
                                    pattern=[[-1, P]], channel_multiplier=1).then_inc(made, 1)
            pool.wait_ge(made, 3)



def adapters_phase(nc, a_st, b_st, args):
    a_d, b_d, starts_d = args
    with ExitStack() as stack:
        c = Ctx(nc, stack)
        a_all = c.sb("a_all", [P, ADAPTERS, D])
        b_all = c.sb("b_all", [P, ADAPTERS, D])
        starts = c.sb("starts", [P, STARTS], I32)
        startf = c.sb("startf", [P, STARTS])
        hit = c.sb("hit", [P, B, STARTS])
        count = c.sb("count", [P, B])
        chosen = c.sb("chosen", [P, B, ADAPTERS], I32)
        sel = c.sb("sel", [P, B, 2, D])
        rounded = c.sb("rounded", [P, B, 2, D], F32R)
        cleared, lora_in, small_in = c.sem("cleared"), c.sem("lora_in"), c.sem("small_in")
        chain, picked, made_round = c.sem("chain"), c.sem("picked"), c.sem("made_round")
        st_hi, st_lo = c.sem("st_hi"), c.sem("st_lo")
        block = stack.enter_context(nc.Block())

        @block.sync
        def _(sp):
            for tile, src in ((a_all, a_d), (b_all, b_d)):
                for g in range(4):
                    sp.dma_start(tile[32 * g:32 * g + 32, :, :], src).then_inc(lora_in, 16)
                if tile is a_all:
                    sp.dma_start(starts[:], starts_d.rearrange("(a n) -> a n", a=1).to_broadcast([P, STARTS])).then_inc(small_in, 16)

        @block.gpsimd
        def _(pool):
            for b in range(B):
                nc.gpsimd.memset(sel[:, b, :, :], 0.0).then_inc(cleared, 1)

        @block.scalar
        def _(act):
            for b in range(B):
                for x in range(2):
                    act.wait_ge(picked, 2 * b + x + 1)
                    nc.scalar.activation(rounded[:, b, x, :], sel[:, b, x, :], ACT.Copy).then_inc(made_round, 1)
                nc.scalar.activation(a_st[0:64, b, :], sel[0:64, b, 0, :], ACT.Copy)
                for g in (0, 2):
                    r = slice(32 * g, 32 * g + 32)
                    nc.scalar.activation(b_st[r, b, :], sel[r, b, 1, :], ACT.Copy).then_inc(st_hi, 1)
            act.wait_ge(st_hi, 2 * B)

        @block.vector
        def _(dve):
            links = [0]

            def link(ins):
                links[0] += 1
                ins.then_inc(chain, 1)
                dve.wait_ge(chain, links[0])

            def pick(b, x, tile):
                for a in range(ADAPTERS):
                    ins = nc.vector.copy_predicated(sel[:, b, x, :], chosen[:, b, a:a + 1].to_broadcast([P, D]), tile[:, a, :])
                    if a < ADAPTERS - 1:
                        link(ins)
                ins.then_inc(picked, 1)

            def low(b):
                dve.wait_ge(made_round, 2 * b + 2)
                nc.vector.tensor_tensor(a_st[64:128, b, :], sel[64:128, b, 0, :], rounded[64:128, b, 0, :].bitcast(F32), ALU.subtract)
                for g in (1, 3):
                    r = slice(32 * g, 32 * g + 32)
                    nc.vector.tensor_tensor(b_st[r, b, :], sel[r, b, 1, :], rounded[r, b, 1, :].bitcast(F32), ALU.subtract).then_inc(st_lo, 1)

            dve.wait_ge(small_in, 16)
            link(nc.vector.tensor_copy(startf[:], starts[:]))
            for b in range(B):
                link(nc.vector.tensor_scalar(hit[:, b, :], startf[:], float(b), None, ALU.is_le))
                link(nc.vector.reduce_sum(count[:, b:b + 1], hit[:, b, :], AX_X))
                for a in range(ADAPTERS):
                    op = ALU.is_ge if a == ADAPTERS - 1 else ALU.is_equal
                    link(nc.vector.tensor_scalar(chosen[:, b, a:a + 1], count[:, b:b + 1], float(a + 2), None, op))
            dve.wait_ge(cleared, B)
            dve.wait_ge(lora_in, 16 * 8)
            for b in range(B):
                pick(b, 0, a_all)
                pick(b, 1, b_all)
                if b == 1:
                    low(0)
            low(1)
            dve.wait_ge(st_lo, 2 * B)


class Front:

    def __init__(self, c, tag):
        self.xt = c.sb(tag + "xt", [P, 2, D])
        self.xn = c.sb(tag + "xn", [P, 2, D])
        self.xT = c.sb(tag + "xT", [P, 2, 2, DT, P], F32R)
        self.st = c.sb(tag + "st", [P, 2, 12])
        self.mv = c.sb(tag + "mv", [P, 2, 2])
        self.std = c.sb(tag + "std", [P, 2, 1])
        self.rstd = c.sb(tag + "rstd", [P, 2, 1])
        self.ps = c.ps(tag + "ps_xT", [P, 2, BANK])
        self.x_in = [c.sem(tag + f"x_in{j}") for j in range(2)]
        self.stats, self.var, self.root = c.sem(tag + "stats"), c.sem(tag + "var"), c.sem(tag + "root")
        self.passed = c.sem(tag + "passed")
        self.inv, self.normed = c.sem(tag + "inv"), c.sem(tag + "normed")
        self.turned, self.hi, self.lo = c.sem(tag + "turned"), c.sem(tag + "hi"), c.sem(tag + "lo")

    def stats_of(self, nc, dve, n, j, loads):
        dve.wait_ge(self.x_in[j], loads)
        nc.vector.bn_stats(self.st[:, j, 0:6], self.xt[:, j, 0:512])
        nc.vector.bn_stats(self.st[:, j, 6:12], self.xt[:, j, 512:1024]).then_inc(self.stats, 1)
        dve.wait_ge(self.stats, n + 1)
        dve.sem_inc(self.passed, 1)
        nc.vector.bn_aggr(self.mv[:, j, :], self.st[:, j, :]).then_inc(self.var, 1)

    def root_of(self, nc, act, eps, n, j):
        act.wait_ge(self.var, n + 1)
        nc.scalar.activation(self.std[:, j, :], self.mv[:, j, 1:2], ACT.Sqrt, bias=eps, scale=1.0).then_inc(self.root, 1)

    def invert(self, nc, dve, n, j):
        dve.wait_ge(self.root, n + 1)
        nc.vector.reciprocal(self.rstd[:, j, :], self.std[:, j, :]).then_inc(self.inv, 1)

    def normalise(self, nc, dve, n, j):
        self.invert(nc, dve, n, j)
        dve.wait_ge(self.inv, n + 1)
        nc.vector.tensor_scalar(self.xn[:, j, :], self.xt[:, j, :], self.mv[:, j, 0:1], self.rstd[:, j, :],
                                ALU.subtract, ALU.mult).then_inc(self.normed, 1)

    def turn(self, nc, pe, ident, n, j):
        pe.wait_ge(self.normed, n + 1)
        for g in range(2):
            if later(n, 1):
                pe.wait_ge(self.lo, n * 2 + g - 1)
            for q in range(4):
                ins = nc.tensor.transpose(self.ps[:, g, q * P:(q + 1) * P],
                                          self.xn[:, j, (4 * g + q) * P:(4 * g + q + 1) * P], ident[:])
            ins.then_inc(self.turned, 1)

    def split_hi(self, nc, act, n, j, product, per_tile):
        if later(n, 2):
            act.wait_ge(product, (n - 1) * per_tile)
        for g in range(2):
            act.wait_ge(self.turned, n * 2 + g + 1)
            nc.scalar.activation(self.xT[:, j, HI, 4 * g:4 * g + 4, :], self.ps[:, g, :].rearrange("p (a b) -> p a b", a=4),
                                 ACT.Copy).then_inc(self.hi, 1)

    def split_lo(self, nc, dve, n, j):
        for g in range(2):
            dve.wait_ge(self.hi, n * 2 + g + 1)
            nc.vector.tensor_tensor(self.xT[:, j, LO, 4 * g:4 * g + 4, :].rearrange("p a b -> p (a b)"), self.ps[:, g, :],
                                    self.xT[:, j, HI, 4 * g:4 * g + 4, :].rearrange("p a b -> p (a b)").bitcast(F32),
                                    ALU.subtract).then_inc(self.lo, 1)


def loads_of(n, j):
    return (n - j) * 8 + 16


SLOTS = 4
PIECES = B * DT
AHEAD = DT + 2


def ffn_steps(eng, step):
    def has(n):
        return lambda m: n + m < NT

    step(1, 1, 0, range(DT, AHEAD), has(1))
    for n in range(2, NT // 2):
        step(n, n % 2, 0, range(n + DT, n + DT + 1), has(n))
    with eng.Fori(NT // 4, NT // 2 - 2) as r:
        for j in range(2):
            step(r * 2 + j, j, 1, (), lambda m: True)
    for n in range(NT - 4, NT):
        step(n, n % 2, 1, (), has(n))


def ffn_phase(nc, tag, k, src_d, dst_d, bias_d, sum_d, w_d=None, a_st=None, b_st=None):
    with ExitStack() as stack:
        c = Ctx(nc, stack)
        weff = c.sb(tag + "weff", [P, B, 2, DT, D], F32R)
        bias_half = c.sb(tag + "bias_half", [P, D])
        w_in = c.sb(tag + "w_in", [P, SLOTS, D])
        f = Front(c, tag)
        xo = c.sb(tag + "xo", [P, 2, D])
        psy = c.ps(tag + "psy", [P, 2, 2, BANK])
        if w_d is not None:
            ps_w = c.ps(tag + "ps_w", [P, 2, BANK])
        bias_in, halved = c.sem(tag + "bias_in"), c.sem(tag + "halved")
        w_loaded = [c.sem(tag + f"w_loaded{j}") for j in range(SLOTS)]
        w_stored = [c.sem(tag + f"w_stored{j}") for j in range(SLOTS)]
        outer, summed, w_hi = c.sem(tag + "outer"), c.sem(tag + "summed"), c.sem(tag + "w_hi")
        w_lo = [c.sem(tag + f"w_lo{j}") for j in range(2)]
        with_bias, product, result = c.sem(tag + "with_bias"), c.sem(tag + "product"), c.sem(tag + "result")
        stored = [c.sem(tag + f"stored{j}") for j in range(2)]
        block = stack.enter_context(nc.Block())

        def piece_ready(eng, i):
            if w_d is None:
                eng.wait_ge(w_loaded[i % SLOTS], 16 * (i // SLOTS + 1))
            else:
                eng.wait_ge(summed, i + 1)

        def low(engine, i):
            b, dt = i // DT, i % DT
            engine.tensor_tensor(weff[:, b, LO, dt, :], w_in[:, i % SLOTS, :], weff[:, b, HI, dt, :].bitcast(F32),
                                 ALU.subtract).then_inc(w_lo[i % 2], 1)

        @block.sync
        def _(sp):
            def load_x(m, jm):
                sp.dma_start(f.xt[:, jm, :], src_d[bass.ds(m * P, P), :]).then_inc(f.x_in[jm], 16)

            def load_w(i):
                src = sum_d[i * P:(i + 1) * P, :] if w_d is None else w_d[:, (i % DT) * D:(i % DT + 1) * D]
                sp.dma_start(w_in[:, i % SLOTS, :], src).then_inc(w_loaded[i % SLOTS], 16)

            def renew(i):
                if w_d is not None:
                    sp.wait_ge(summed, i + 1)
                    sp.dma_start(sum_d[i * P:(i + 1) * P, :], w_in[:, i % SLOTS, :]).then_inc(w_stored[i % SLOTS], 16)
                i = i - 1
                if 0 <= i < PIECES - SLOTS:
                    sp.wait_ge(w_lo[i % 2], i // 2 + 1)
                    if w_d is not None:
                        sp.wait_ge(w_stored[i % SLOTS], 16 * (i // SLOTS + 1))
                    load_w(i + SLOTS)

            load_x(0, 0)
            load_w(0)
            load_x(1, 1)
            sp.dma_start(bias_half[:], bias_d.rearrange("(a n) -> a n", a=1).to_broadcast([P, D])).then_inc(bias_in, 16)
            for i in range(1, SLOTS):
                load_w(i)
            for i in range(DT):
                renew(i)
                if i in (1, 2):
                    sp.wait_ge(f.normed, i)
                    sp.wait_ge(with_bias, i)
                    load_x(i + 1, (i + 1) % 2)

            def step(n, j, b, pieces, has):
                if not later(n, 2):
                    sp.wait_ge(result, 2)
                    sp.dma_start(dst_d[0:P, :], xo[:, 0, :]).then_inc(stored[0], 16)
                if has(3):
                    sp.wait_ge(f.normed, n + 2)
                    sp.wait_ge(with_bias, n + 2)
                    load_x(n + 3, (j + 1) % 2)
                for i in pieces:
                    renew(i)
                sp.wait_ge(result, n * 2 + 2)
                sp.dma_start(dst_d[bass.ds(n * P, P), :], xo[:, j, :]).then_inc(stored[j], 16)
            ffn_steps(sp, step)
            for j in range(2):
                sp.wait_ge(stored[j], 16 * NT // 2)
            if w_d is not None:
                for j in range(SLOTS):
                    sp.wait_ge(w_stored[j], 16 * PIECES // SLOTS)

        @block.gpsimd
        def _(pool):
            def add_bias(n, j):
                pool.wait_ge(f.x_in[j], loads_of(n, j))
                if later(n, 2):
                    pool.wait_ge(stored[j], (n - j) * 8)
                nc.gpsimd.tensor_tensor(xo[:, j, :], f.xt[:, j, :], bias_half[:], ALU.add).then_inc(with_bias, 1)

            def pieces_low(pieces):
                for i in pieces:
                    if i % 2 == 0:
                        pool.wait_ge(w_hi, i + 1)
                        low(nc.gpsimd, i)

            pieces_low([0])
            pool.wait_ge(halved, 1)
            add_bias(0, 0)
            pieces_low([2])
            add_bias(1, 1)
            pieces_low(range(4, DT))

            def step(n, j, b, pieces, has):
                pieces_low(pieces)
                if has(1):
                    add_bias(n + 1, (j + 1) % 2)
            ffn_steps(pool, step)

        @block.scalar
        def _(act):
            def pieces_hi(pieces):
                for i in pieces:
                    piece_ready(act, i)
                    nc.scalar.activation(weff[:, i // DT, HI, i % DT, :], w_in[:, i % SLOTS, :], ACT.Copy).then_inc(w_hi, 1)

            f.root_of(nc, act, k.eps_ln[:], 0, 0)
            pieces_hi([0])
            f.root_of(nc, act, k.eps_ln[:], 1, 1)
            for n in range(2):
                f.split_hi(nc, act, n, n, product, 2)
            for i in range(1, DT):
                pieces_hi([i])
                if i in (4, 5):
                    f.root_of(nc, act, k.eps_ln[:], i - 2, i % 2)

            def step(n, j, b, pieces, has):
                if has(2) and later(n, 2):
                    f.root_of(nc, act, k.eps_ln[:], n + 2, j)
                if has(1):
                    f.split_hi(nc, act, n + 1, (j + 1) % 2, product, 2)
                pieces_hi(pieces)
            ffn_steps(act, step)

        @block.tensor
        def _(pe):
            def outer_products(i):
                if w_d is None:
                    return
                if i >= 1:
                    pe.wait_ge(summed, i)
                for half in range(2):
                    ins = nc.tensor.matmul(ps_w[:, half, :], a_st[:, i // DT, (i % DT) * P:(i % DT + 1) * P],
                                           b_st[:, i // DT, half * BANK:(half + 1) * BANK], start=True, stop=True)
                ins.then_inc(outer, 1)

            outer_products(0)
            f.turn(nc, pe, k.ident, 0, 0)
            outer_products(1)
            f.turn(nc, pe, k.ident, 1, 1)
            for i in range(DT):
                if i + 2 <= DT:
                    outer_products(i + 2)
                pe.wait_ge(w_hi, i + 1)
                pe.wait_ge(w_lo[i % 2], i // 2 + 1)
                for tile in range(2):
                    pe.wait_ge(f.lo, tile * 2 + 2)
                    for half in range(2):
                        for n, (a, m) in enumerate(PASSES):
                            ins = nc.tensor.matmul(psy[:, tile, half, :], f.xT[:, tile, a, i, :],
                                                   weff[:, 0, m, i, half * BANK:(half + 1) * BANK],
                                                   start=(i == 0 and n == 0), stop=(i == DT - 1 and n == 2))
                        if i == DT - 1:
                            ins.then_inc(product, 1)

            def step(n, j, b, pieces, has):
                if has(1):
                    f.turn(nc, pe, k.ident, n + 1, (j + 1) % 2)
                for i in pieces:
                    if i > DT:
                        outer_products(i)
                if later(n, 2):
                    pe.wait_ge(f.lo, n * 2 + 2)
                    pe.wait_ge(result, n * 2 - 2)
                    if b == 1:
                        pe.wait_ge(w_lo[0], PIECES // 2)
                        pe.wait_ge(w_lo[1], PIECES // 2)
                    for half in range(2):
                        for i, (a, m) in enumerate(PASSES):
                            for dt in range(DT):
                                ins = nc.tensor.matmul(psy[:, j, half, :], f.xT[:, j, a, dt, :],
                                                       weff[:, b, m, dt, half * BANK:(half + 1) * BANK],
                                                       start=(i == 0 and dt == 0), stop=(i == 2 and dt == DT - 1))
                        ins.then_inc(product, 1)
            ffn_steps(pe, step)

        @block.vector
        def _(dve):
            def make_pieces(pieces):
                for i in pieces:
                    if w_d is not None:
                        dve.wait_ge(w_loaded[i % SLOTS], 16 * (i // SLOTS + 1))
                        dve.wait_ge(outer, i + 1)
                        nc.vector.tensor_tensor(w_in[:, i % SLOTS, :], ps_w[:].rearrange("p a n -> p (a n)"),
                                                w_in[:, i % SLOTS, :], ALU.add).then_inc(summed, 1)
                    if i % 2 == 1:
                        dve.wait_ge(w_hi, i + 1)
                        low(nc.vector, i)

            def results(n, j):
                dve.wait_ge(with_bias, n + 1)
                for half in range(2):
                    dve.wait_ge(product, n * 2 + half + 1)
                    w = slice(half * BANK, (half + 1) * BANK)
                    nc.vector.scalar_tensor_tensor(out=xo[:, j, w], in0=psy[:, j, half, :], scalar=0.5,
                                                         in1=xo[:, j, w], op0=ALU.mult, op1=ALU.add).then_inc(result, 1)

            f.stats_of(nc, dve, 0, 0, loads_of(0, 0))
            make_pieces([0])
            f.normalise(nc, dve, 0, 0)
            f.stats_of(nc, dve, 1, 1, loads_of(1, 1))
            f.split_lo(nc, dve, 0, 0)
            f.normalise(nc, dve, 1, 1)
            make_pieces([1])
            f.split_lo(nc, dve, 1, 1)
            dve.wait_ge(bias_in, 16)
            nc.vector.tensor_scalar(bias_half[:], bias_half[:], 0.5, None, ALU.mult).then_inc(halved, 1)
            for i in range(2, DT):
                make_pieces([i])
                if i in (3, 4):
                    f.stats_of(nc, dve, i - 1, (i - 1) % 2, loads_of(i - 1, (i - 1) % 2))
                if i in (5, 6):
                    dve.wait_ge(f.turned, 2 * (i - 4))
                    f.normalise(nc, dve, i - 3, (i - 3) % 2)

            def step(n, j, b, pieces, has):
                if has(2) and later(n, 2):
                    f.stats_of(nc, dve, n + 2, j, loads_of(n + 2, j))
                if not later(n, 2):
                    results(0, 0)
                if has(1):
                    f.split_lo(nc, dve, n + 1, (j + 1) % 2)
                if has(2) and later(n, 2):
                    dve.wait_ge(f.turned, n * 2 + 2)
                    f.normalise(nc, dve, n + 2, j)
                make_pieces(pieces)
                results(n, j)
            ffn_steps(dve, step)



def latents_phase(nc, k, src_d, args):
    wa_d, lnw_d, cos_d, sin_d = args
    tag = "l_"
    with ExitStack() as stack:
        c = Ctx(nc, stack)
        f = Front(c, tag)
        wa_in = c.sb("wa_in", [P, DT, LAT])
        wa = c.sb("wa", [P, 2, DT, LAT], F32R)
        lnw = c.sb("lnw", [P, QR + KVR])
        cos = c.sb("l_cos", [P, NT, ROPE])
        sin = c.sb("l_sin", [P, NT, ROPE])
        squares = c.sb("squares", [P, 2, QR + KVR])
        ss = c.sb("ss", [P, 2, 2])
        rms = c.sb("rms", [P, 2, 2])
        inv = c.sb("l_invs", [P, 2, 2])
        lat = c.sb("lat", [P, 2, LAT])
        rot = c.sb("rot", [P, 2, 2, ROPE])
        shift = c.sb("l_shift", [P, 2, 1])
        shifted = c.sem("l_shifted")
        psl = c.ps("psl", [P, 2, BANK])
        ps2 = c.ps("ps2", [P, 2, BANK])
        w_loaded, w_hi, w_lo = c.sem("l_w_loaded"), c.sem("l_w_hi"), c.sem("l_w_lo")
        small_in, scaled = c.sem("l_small_in"), c.sem("l_scaled")
        product, rooted, inverted = c.sem("l_product"), c.sem("l_rooted"), c.sem("l_inverted")
        squared = c.sem("l_squared")
        partial, latent = c.sem("l_partial"), c.sem("l_latent")
        turned2, hi2, lo2 = c.sem("l_turned2"), c.sem("l_hi2"), c.sem("l_lo2")
        block = stack.enter_context(nc.Block())

        @block.sync
        def _(sp):
            sp.dma_start(wa_in[:], wa_d.rearrange("p (a n) -> p a n", a=DT)).then_inc(w_loaded, 16)
            sp.dma_start(lnw[:], lnw_d.rearrange("(a n) -> a n", a=1).to_broadcast([P, QR + KVR])).then_inc(small_in, 16)
            sp.dma_start(cos[:], cos_d.rearrange("(t p) n -> p t n", p=P)).then_inc(small_in, 16)
            sp.dma_start(sin[:], sin_d.rearrange("(t p) n -> p t n", p=P)).then_inc(small_in, 16)

            def step(n, j, has):
                if has(2):
                    if later(n, 0):
                        sp.wait_ge(f.normed, n + 1)
                    sp.dma_start(f.xt[:, j, :], src_d[bass.ds((n + 2) * P, P), :]).then_inc(f.x_in[j], 16)
            steady(sp, step, NT, 2)

        @block.gpsimd
        def _(pool):
            pool.wait_ge(w_hi, 1)
            nc.gpsimd.tensor_tensor(wa[:, LO, :, :], wa_in[:], wa[:, HI, :, :].bitcast(F32), ALU.subtract).then_inc(w_lo, 1)

        @block.scalar
        def _(act):
            act.wait_ge(w_loaded, 16)
            nc.scalar.activation(wa[:, HI, :, :], wa_in[:], ACT.Copy).then_inc(w_hi, 1)

            def step(n, j, has):
                jm = (j + 1) % 2
                if has(0):
                    act.wait_ge(product, n + 1)
                    if later(n, 2):
                        act.wait_ge(inverted, n - 1)
                        act.wait_ge(squared, n - 1)
                    nc.scalar.activation(squares[:, j, 0:QR], psl[:, j, 0:QR], ACT.Square,
                                         accum_out=ss[:, j, 0:1])
                    nc.scalar.activation(squares[:, j, QR:QR + KVR], psl[:, j, QR:QR + KVR], ACT.Square,
                                         accum_out=ss[:, j, 1:2]).then_inc(squared, 1)
                    act.wait_ge(squared, n + 1)
                    nc.scalar.activation(rms[:, j, 0:1], ss[:, j, 0:1], ACT.Sqrt, bias=k.eps_rms[:], scale=1.0 / QR)
                    nc.scalar.activation(rms[:, j, 1:2], ss[:, j, 1:2], ACT.Sqrt, bias=k.eps_rms[:], scale=1.0 / KVR).then_inc(rooted, 1)
                if has(3):
                    f.root_of(nc, act, k.eps_ln[:], n + 3, jm)
                if has(2):
                    f.split_hi(nc, act, n + 2, j, product, 1)
                if has(-1):
                    m = n - 1
                    act.wait_ge(turned2, n)
                    nc.scalar.activation(k.qnT[:, HI, :, bass.ds(m * P, P)], ps2[:, jm, 0:QR].rearrange("p (r n) -> p r n", r=QRT), ACT.Copy)
                    nc.scalar.activation(k.keyT[:, HI, bass.ds(m * P, P)], ps2[:, jm, QR:LAT], ACT.Copy)
                    nc.scalar.activation(k.val[:, bass.ds(m, 1), 0:KVR], lat[:, jm:jm + 1, QR:QR + KVR], ACT.Copy).then_inc(hi2, 1)
                if has(3):
                    if later(n, -1):
                        act.wait_ge(f.turned, n * 2 + 4)
                    act.wait_ge(shifted, n + 4)
                    nc.scalar.activation(f.xn[:, jm, :], f.xt[:, jm, :], ACT.Identity, bias=shift[:, jm, :],
                                         scale=f.rstd[:, jm, :]).then_inc(f.normed, 1)
            steady(act, step, NT, 3, 1)

        @block.tensor
        def _(pe):
            def step(n, j, has):
                if has(1):
                    f.turn(nc, pe, k.ident, n + 1, (j + 1) % 2)
                if has(0):
                    if not later(n, 1):
                        pe.wait_ge(w_lo, 1)
                    pe.wait_ge(f.lo, n * 2 + 2)
                    if later(n, 2):
                        pe.wait_ge(latent, n - 1)
                    for i, (a, m) in enumerate(PASSES):
                        for dt in range(DT):
                            ins = nc.tensor.matmul(psl[:, j, 0:LAT], f.xT[:, j, a, dt, :], wa[:, m, dt, :],
                                                   start=(i == 0 and dt == 0), stop=(i == 2 and dt == DT - 1))
                    ins.then_inc(product, 1)
                if has(-1):
                    jm = (j + 1) % 2
                    pe.wait_ge(latent, n)
                    if later(n, 3):
                        pe.wait_ge(lo2, n - 2)
                    for r in range(LAT // P):
                        ins = nc.tensor.transpose(ps2[:, jm, r * P:(r + 1) * P], lat[:, jm, r * P:(r + 1) * P], k.ident[:])
                    ins.then_inc(turned2, 1)
            steady(pe, step, NT, 2, 1)

        @block.vector
        def _(dve):
            dve.wait_ge(small_in, 48)
            nc.vector.tensor_scalar(lnw[:, 0:QR], lnw[:, 0:QR], SCALE, None, ALU.mult).then_inc(scaled, 1)
            dve.wait_ge(scaled, 1)

            def step(n, j, has):
                jm = (j + 1) % 2
                if has(3):
                    f.stats_of(nc, dve, n + 3, jm, loads_of(n + 3, jm))
                if has(0):
                    dve.wait_ge(rooted, n + 1)
                    nc.vector.reciprocal(inv[:, j, :], rms[:, j, :]).then_inc(inverted, 1)
                    pe_cols = psl[:, j, QR + KVR:LAT]
                    half = ROPE // 2
                    if later(n, 2):
                        dve.wait_ge(turned2, n - 1)
                        dve.wait_ge(hi2, n - 1)
                    nc.vector.tensor_tensor(rot[:, j, 0, :], pe_cols, cos[:, bass.ds(n, 1), :].rearrange("p a n -> p (a n)"), ALU.mult)
                    nc.vector.tensor_tensor(rot[:, j, 1, 0:half], pe_cols[:, half:ROPE],
                                            sin[:, bass.ds(n, 1), 0:half].rearrange("p a n -> p (a n)"), ALU.mult)
                    nc.vector.tensor_tensor(rot[:, j, 1, half:ROPE], pe_cols[:, 0:half],
                                            sin[:, bass.ds(n, 1), half:ROPE].rearrange("p a n -> p (a n)"), ALU.mult).then_inc(partial, 1)
                    dve.wait_ge(inverted, n + 1)
                    nc.vector.scalar_tensor_tensor(out=lat[:, j, 0:QR], in0=psl[:, j, 0:QR], scalar=inv[:, j, 0:1],
                                                   in1=lnw[:, 0:QR], op0=ALU.mult, op1=ALU.mult)
                    nc.vector.scalar_tensor_tensor(out=lat[:, j, QR:QR + KVR], in0=psl[:, j, QR:QR + KVR], scalar=inv[:, j, 1:2],
                                                   in1=lnw[:, QR:QR + KVR], op0=ALU.mult, op1=ALU.mult)
                    dve.wait_ge(partial, n + 1)
                    nc.vector.tensor_tensor(lat[:, j, QR + KVR:LAT], rot[:, j, 0, :], rot[:, j, 1, :], ALU.add).then_inc(latent, 1)
                if has(3):
                    if later(n, -1):
                        dve.wait_ge(f.normed, n + 2)
                    f.invert(nc, dve, n + 3, jm)
                    dve.wait_ge(f.inv, n + 4)
                    nc.vector.tensor_scalar(shift[:, jm, :], f.mv[:, jm, 0:1], f.rstd[:, jm, :], -1.0, ALU.mult, ALU.mult).then_inc(shifted, 1)
                if has(2):
                    f.split_lo(nc, dve, n + 2, j)
                if has(-1):
                    m = n - 1
                    dve.wait_ge(hi2, n)
                    nc.vector.tensor_tensor(k.qnT[:, LO, :, bass.ds(m * P, P)], ps2[:, jm, 0:QR].rearrange("p (r n) -> p r n", r=QRT),
                                            k.qnT[:, HI, :, bass.ds(m * P, P)].bitcast(F32), ALU.subtract)
                    nc.vector.tensor_tensor(k.keyT[:, LO, bass.ds(m * P, P)], ps2[:, jm, QR:LAT],
                                            k.keyT[:, HI, bass.ds(m * P, P)].bitcast(F32), ALU.subtract)
                    nc.vector.tensor_tensor(k.val[:, bass.ds(m, 1), KVR:2 * KVR], lat[:, jm:jm + 1, QR:QR + KVR],
                                            k.val[:, bass.ds(m, 1), 0:KVR].bitcast(F32), ALU.subtract).then_inc(lo2, 1)
            steady(dve, step, NT, 3, 1)



TILES = 4 * QT
GROUPS = tuple((t, kt, min(4, t + 1 - kt)) for t in range(QT) for kt in range(0, t + 1, 4))
NG = len(GROUPS)
PE_STEP = ("S0+0 T7-1 V0-1 T8-1 S1+0 S2+0 T9-1 Q0+1 S3+0 T10-1 T11-1 Q1+1 S4+0 T0+0 S5+0 F0+0 T1+0 T2+0 "
             "V1-1 T3+0 S6+0 T4+0 S7+0 T5+0 W0+0 T6+0")
ACT_STEP = ("E6-1 T5-1 T6-1 E7-1 T7-1 E0+0 W0-1 T8-1 E1+0 T9-1 E2+0 Q0+1 V0-1 T10-1 T11-1 E3+0 Q1+1 T0+0 "
             "F0+0 T1+0 E4+0 T2+0 E5+0 T3+0 T4+0 V1-1")
DVE_STEP = ("T1+0 F0+0 P4+0 T2+0 P5+0 H0+1 T3+0 M6+0 T4+0 M7+0 T5+0 P6+0 T6+0 M0+1 T7+0 P7+0 M1+1 M2+1 "
             "H1+1 T8+0 T9+0 P0+1 P1+1 M3+1 T10+0 P2+1 P3+1 T11+0 T0+1 M4+1 M5+1")
POOL_STEP = "Q0+1 Q1+1 V1-1 V0+0"


def parse(table):
    return [(job[0], int(job[1:-2]), int(job[-2:])) for job in table.split()]


class Round:

    def __init__(self, it, first=False, last=False):
        self.it, self.first, self.last = it, first, last
        self.keys = [job for job in self.jobs(PE_STEP) if job[0] in "QFW"]
        self.before = 2 if first else it * len(STEADY.keys) + 2 + len(FIRST.keys) - len(STEADY.keys)

    def jobs(self, table):
        for step in range(-1 if self.first else 0, 6 if self.last else 4):
            for job, n, shift in parse(table):
                s = step + shift
                absent = job == "F" and (s % 4 < 2 or self.last)
                if not absent and not (self.first and s < 0) and not (self.last and s > 3) and (shift > 0 or step >= 0) \
                        and (shift < 0 or step < 4):
                    yield job, n, s

    def use(self, *key):
        if key in self.keys:
            return self.before + self.keys.index(key)
        job, n, s = key
        return self.before - len(STEADY.keys) + STEADY.keys.index((job, n, s + 4))


class _Plain(Round):
    def __init__(self, first):
        self.first, self.last = first, False
        self.keys = [job for job in self.jobs(PE_STEP) if job[0] in "QFW"]


STEADY, FIRST = _Plain(False), _Plain(True)


def rounds(eng, body):
    body(Round(0, first=True))
    with eng.Fori(1, PAIRS - 1) as it:
        body(Round(it))
    body(Round(PAIRS - 1, last=True))


def attention_phase(nc, k, args, oT_d, wvo_d):
    wn_d, wpe_d, wv_d, wo_d, cosT_d, sinT_d = args
    with ExitStack() as stack:
        c = Ctx(nc, stack)
        wn = c.sb("wn", [64, 2, QR + KVR])
        wpe = c.sb("wpe", [P, 2, QRT, ROPE])
        wv = c.sb("wv", [P, 2, KVR])
        wo = c.sb("wo", [P, 2, D])
        wvo = c.sb("wvo", [64, 2, BANK])
        wq = c.sb("wq", [P, 2, 2, QRT, QHD], F32R)
        cosT = c.sb("cosT", [P, S])
        sinT = c.sb("sinT", [P, S])
        qf = c.sb("qf", [P, 2, CHUNK])
        rot = c.sb("q_rot", [P, 2, CHUNK])
        q = c.sb("q", [P, 2, 2, S], F32R)
        prob = c.sb("prob", [P, 4, S])
        pT0 = c.sb("pT0", [P, 2, 4, CHUNK], F32R)
        pT1 = c.sb("pT1", [P, 2, 8, CHUNK], F32R)
        pT = (pT0, pT1)
        negmax = c.sb("negmax", [P, 8])
        rowsum = c.sb("rowsum", [P, 8])
        rinv = c.sb("rinv", [P, 8])
        o_parts = c.sb("o_parts", [KVR, 2, 2, CHUNK])
        o_sum = c.sb("o_sum", [P, 2, CHUNK])
        psS = c.ps("psS", [P, 2, 2 * BANK])
        psT = c.ps("psT", [P, 2, BANK])
        psV = c.ps("psV", [P, BANK])
        psM = c.ps("psM", [P, BANK])
        tab_in, wn_in, wo_in = c.sem("tab_in"), c.sem("wn_in"), c.sem("wo_in")
        zeroed = c.sem("zeroed")
        scored, maxed, exped, recip, scaled = c.sem("scored"), c.sem("maxed"), c.sem("exped"), c.sem("recip"), c.sem("scaled")
        turned, p_hi, p_lo = c.sem("p_turned"), c.sem("p_hi"), c.sem("p_lo")
        valued, copied, joined = c.sem("valued"), c.sem("copied"), c.sem("joined")
        m_done, m_free = c.sem("m_done"), c.sem("m_free")
        rope_parts, roped, q_hi, q_lo = c.sem("rope_parts"), c.sem("roped"), c.sem("q_hi"), c.sem("q_lo")
        wq_hi = c.sem("wq_hi")
        o_stored = [[c.sem(f"o_stored{e}{ch}") for ch in range(2)] for e in range(2)]
        w_stored = [c.sem(f"w_stored{n}") for n in range(2)]
        block = stack.enter_context(nc.Block())

        def place(s, t):
            x = P if t == 4 else 0
            return psS[:, (QT * s + t) % 2, x:x + (t + 1) * P]

        @block.sync
        def _(sp):
            def load_fold(pair):
                sp.dma_start(wn[:], wn_d[bass.ds(pair, 1), :, :].rearrange("a p n -> (a p) n").rearrange("p (e n) -> p e n", e=2)).then_inc(wn_in, 16)
                sp.dma_start(wpe[:].rearrange("p e r n -> p (e r n)"), wpe_d[bass.ds(pair, 1), :, :].rearrange("a p n -> (a p) n")).then_inc(wn_in, 16)

            def load_out(pair):
                sp.dma_start(wv[:].rearrange("p e n -> p (e n)"), wv_d[bass.ds(pair, 1), :, :].rearrange("a p n -> (a p) n")).then_inc(wo_in, 16)
                sp.dma_start(wo[:].rearrange("p e n -> p (e n)"), wo_d[bass.ds(pair, 1), :, :].rearrange("a p n -> (a p) n")).then_inc(wo_in, 16)

            load_fold(0)
            sp.dma_start(cosT[:], cosT_d[:, :]).then_inc(tab_in, 16)
            sp.dma_start(sinT[:], sinT_d[:, :]).then_inc(tab_in, 16)
            load_out(0)

            def body(r):
                def store_o(pair, s, ch):
                    e, b = s % 2, (s // 2) % 2
                    sp.wait_ge(joined, r.it * 8 + 2 * s + ch + 1)
                    sp.dma_start(oT_d[bass.ds(pair * P + e * KVR, KVR), b * S + ch * CHUNK:b * S + (ch + 1) * CHUNK],
                                 o_sum[e * KVR:(e + 1) * KVR, ch, :]).then_inc(o_stored[e][ch], 16)

                def store_w(s):
                    e, half = s // 2, s % 2
                    sp.wait_ge(m_free, r.use("W", 0, s) + 1)
                    sp.dma_start(wvo_d[bass.ds(r.it * P + e * KVR, KVR), half * BANK:(half + 1) * BANK],
                                 wvo[:, half, :]).then_inc(w_stored[half], 16)

                if not r.last:
                    sp.wait_ge(m_free, 2 if r.first else r.use("F", 0, -1) + 1)
                    load_fold(r.it + 1)
                for s in range(4):
                    if s > 0:
                        store_o(r.it, s - 1, 1)
                    elif not r.first:
                        store_o(r.it - 1, -1, 1)
                    store_w(s)
                    store_o(r.it, s, 0)
                if r.last:
                    store_o(r.it, 3, 1)
                else:
                    load_out(r.it + 1)
            rounds(sp, body)
            for n in range(2):
                for e in range(2):
                    sp.wait_ge(o_stored[e][n], 16 * 2 * PAIRS)
                sp.wait_ge(w_stored[n], 16 * 2 * PAIRS)

        @block.tensor
        def _(pe):
            def fold_queries(e, count):
                if count >= 1 if isinstance(count, int) else True:
                    pe.wait_ge(m_free, count)
                for t in range(QRT):
                    ins = nc.tensor.matmul(psM[:, t * NOPE:(t + 1) * NOPE], wn[:, e, t * P:(t + 1) * P], wn[:, e, QR:QR + KVR],
                                           start=True, stop=True)
                ins.then_inc(m_done, 1)

            def queries(s, ch, count):
                e, b = s % 2, (s // 2) % 2
                pe.wait_ge(m_free, count)
                for n, (a, m) in enumerate(PASSES):
                    for t in range(QRT):
                        ins = nc.tensor.matmul(psM[:, :], wq[:, a, e, t, :], k.qnT[:, m, t, b * S + ch * CHUNK:b * S + (ch + 1) * CHUNK],
                                               start=(n == 0 and t == 0), stop=(n == 2 and t == QRT - 1))
                ins.then_inc(m_done, 1)

            def scores(it, s, t):
                li, b = QT * s + t, (s // 2) % 2
                if later(it * TILES + li - 1, 1):
                    pe.wait_ge(exped, it * TILES + li - 1)
                if t % 4 == 0:
                    pe.wait_ge(q_lo, it * 8 + 2 * s + t // 4 + 1)
                width = max(2 * P, (t + 1) * P)
                shift, cut = (P, BANK - P) if t == 4 else (0, BANK)
                pieces = [(0, min(width, cut))] + ([(cut, width)] if width > cut else [])
                for x0, x1 in pieces:
                    x1 = max(x1, x0 + 2 * P)
                    for n, (a, m) in enumerate(PASSES):
                        ins = nc.tensor.matmul(psS[:, li % 2, shift + x0:shift + x1], q[:, s % 2, a, t * P:(t + 1) * P],
                                               k.keyT[:, m, b * S + x0:b * S + x1], start=(n == 0), stop=(n == 2))
                        if n == 0 and x0 <= t * P < x1:
                            nc.tensor.matmul(psS[:, li % 2, shift + t * P:shift + (t + 1) * P], k.ident_bf[:], k.mask_bf[:],
                                             start=False, stop=False)
                ins.then_inc(scored, 1)

            def transposes(it, s, g):
                t, k0, blocks = GROUPS[g]
                if k0 == 0:
                    pe.wait_ge(scaled, it * TILES + QT * s + t + 1)
                if later(it * 4 * NG + NG * s + g - 1, 1):
                    pe.wait_ge(p_lo, it * 4 * NG + NG * s + g - 1)
                for kt in range(blocks):
                    ins = nc.tensor.transpose(psT[:, (NG * s + g) % 2, kt * P:(kt + 1) * P],
                                              prob[:, (QT * s + t) % 4, (k0 + kt) * P:(k0 + kt + 1) * P], k.ident[:])
                ins.then_inc(turned, 1)

            def values(it, s, ch):
                b, last = (s // 2) % 2, 4 * ch + 3
                groups = sum(t <= last for t, _, _ in GROUPS)
                pe.wait_ge(p_lo, it * 4 * NG + NG * s + groups)
                if later(it * 8 + 2 * s + ch, 1):
                    pe.wait_ge(copied, it * 8 + 2 * s + ch)
                for kt in range(last + 1):
                    n0 = min(max(kt - 4 * ch, 0), 2) * P
                    for part in (HI, LO):
                        ins = nc.tensor.matmul(psV[:, n0:CHUNK], k.val[:, b * QT + kt, :], pT[ch][:, part, kt, n0:CHUNK],
                                               start=(kt == 0 and part == HI), stop=(kt == last and part == LO))
                ins.then_inc(valued, 1)

            def fold_output(it, s, count):
                e, half = s // 2, s % 2
                if s == 0:
                    pe.wait_ge(wo_in, (it + 1) * 32)
                pe.wait_ge(m_free, count)
                nc.tensor.matmul(psM[0:KVR, :], wv[:, e, :], wo[:, e, half * BANK:(half + 1) * BANK],
                                 start=True, stop=True).then_inc(m_done, 1)

            pe.wait_ge(wn_in, 32)
            for e in range(2):
                fold_queries(e, e)
            pe.wait_ge(zeroed, 2)

            def body(r):
                for job, n, s in r.jobs(PE_STEP):
                    if job == "S":
                        scores(r.it, s, n)
                    elif job == "T":
                        transposes(r.it, s, n)
                    elif job == "V":
                        values(r.it, s, n)
                    elif job == "Q":
                        queries(s, n, r.use(job, n, s))
                    elif job == "W":
                        fold_output(r.it, s, r.use(job, n, s))
                    elif job == "F":
                        if s == 2:
                            pe.wait_ge(wn_in, (r.it + 2) * 32)
                        fold_queries(s - 2, r.use(job, n, s))
            rounds(pe, body)

        @block.scalar
        def _(act):
            def split_queries_hi(e, count):
                act.wait_ge(m_done, count + 1)
                nc.scalar.activation(wq[:, HI, e, :, 0:NOPE], psM[:, 0:QRT * NOPE].rearrange("p (t n) -> p t n", t=QRT), ACT.Copy)
                nc.scalar.activation(wq[:, HI, e, :, NOPE:QHD], wpe[:, e, :, :], ACT.Copy).then_inc(wq_hi, 1)

            def copy_queries(ch, number, count):
                act.wait_ge(m_done, count + 1)
                if later(number, 2):
                    act.wait_ge(q_lo, number - 1)
                nc.scalar.activation(qf[:, ch, :], psM[:, :], ACT.Copy).then_inc(m_free, 1)

            def exponentials(it, s, t):
                li = QT * s + t
                act.wait_ge(maxed, it * TILES + li + 1)
                groups = NG * ((li - 4) // QT) + sum(g[0] <= (li - 4) % QT for g in GROUPS)
                if later(it * 4 * NG + groups, 1):
                    act.wait_ge(turned, it * 4 * NG + groups)
                nc.scalar.activation(prob[:, li % 4, 0:(t + 1) * P], place(s, t), ACT.Exp,
                                     bias=negmax[:, li % 8:li % 8 + 1], scale=1.0,
                                     accum_out=rowsum[:, li % 8:li % 8 + 1]).then_inc(exped, 1)

            def split_hi(it, s, g):
                t, k0, blocks = GROUPS[g]
                ch, x = t // 4, (t % 4) * P
                act.wait_ge(turned, it * 4 * NG + NG * s + g + 1)
                nc.scalar.activation(pT[ch][:, HI, k0:k0 + blocks, x:x + P],
                                     psT[:, (NG * s + g) % 2, 0:blocks * P].rearrange("p (a b) -> p a b", a=blocks), ACT.Copy).then_inc(p_hi, 1)

            def copy_values(it, s, ch):
                act.wait_ge(valued, it * 8 + 2 * s + ch + 1)
                if later(it * 8 + 2 * s + ch, 2):
                    act.wait_ge(joined, it * 8 + 2 * s + ch - 1)
                nc.scalar.activation(o_parts[:, ch, 0, :], psV[0:KVR, :], ACT.Copy)
                nc.scalar.activation(o_parts[:, ch, 1, :], psV[KVR:2 * KVR, :], ACT.Copy).then_inc(copied, 1)

            def copy_output_weights(it, s, count):
                act.wait_ge(m_done, count + 1)
                if later(it * 4 + s, 2):
                    act.wait_ge(w_stored[s % 2], (it * 2 + s // 2) * 16)
                nc.scalar.activation(wvo[:, s % 2, :], psM[0:KVR, :], ACT.Copy).then_inc(m_free, 1)

            for e in range(2):
                split_queries_hi(e, e)

            def body(r):
                for job, n, s in r.jobs(ACT_STEP):
                    if job == "E":
                        exponentials(r.it, s, n)
                    elif job == "T":
                        split_hi(r.it, s, n)
                    elif job == "V":
                        copy_values(r.it, s, n)
                    elif job == "Q":
                        copy_queries(n, r.it * 8 + 2 * s + n, r.use(job, n, s))
                    elif job == "W":
                        copy_output_weights(r.it, s, r.use(job, n, s))
                    elif job == "F":
                        split_queries_hi(s - 2, r.use(job, n, s))
            rounds(act, body)

        @block.vector
        def _(dve):
            def split_queries_lo(e, count):
                dve.wait_ge(wq_hi, count)
                nc.vector.tensor_tensor(wq[:, LO, e, :, NOPE:QHD], wpe[:, e, :, :], wq[:, HI, e, :, NOPE:QHD].bitcast(F32), ALU.subtract)
                nc.vector.tensor_tensor(wq[:, LO, e, :, 0:NOPE], psM[:, 0:QRT * NOPE].rearrange("p (t n) -> p t n", t=QRT),
                                        wq[:, HI, e, :, 0:NOPE].bitcast(F32), ALU.subtract).then_inc(m_free, 1)

            def query_hi(s, ch, number):
                dve.wait_ge(roped, number + 1)
                nc.vector.tensor_copy(q[:, s % 2, HI, ch * CHUNK:(ch + 1) * CHUNK], qf[:, ch, :]).then_inc(q_hi, 1)

            def maxima(it, s, t):
                li = QT * s + t
                dve.wait_ge(scored, it * TILES + li + 1)
                nc.vector.tensor_reduce(negmax[:, li % 8:li % 8 + 1], place(s, t), AX_X, ALU.max, negate=True).then_inc(maxed, 1)

            def divide(it, s, t):
                li = QT * s + t
                dve.wait_ge(exped, it * TILES + li + 1)
                nc.vector.reciprocal(rinv[:, li % 8:li % 8 + 1], rowsum[:, li % 8:li % 8 + 1]).then_inc(recip, 1)
                dve.wait_ge(recip, it * TILES + li + 1)
                nc.vector.tensor_scalar(prob[:, li % 4, 0:(t + 1) * P], prob[:, li % 4, 0:(t + 1) * P],
                                        rinv[:, li % 8:li % 8 + 1], None, ALU.mult).then_inc(scaled, 1)

            def split_lo(it, s, g):
                t, k0, blocks = GROUPS[g]
                ch, x = t // 4, (t % 4) * P
                dve.wait_ge(p_hi, it * 4 * NG + NG * s + g + 1)
                nc.vector.tensor_tensor(pT[ch][:, LO, k0:k0 + blocks, x:x + P],
                                        psT[:, (NG * s + g) % 2, 0:blocks * P].rearrange("p (a b) -> p a b", a=blocks),
                                        pT[ch][:, HI, k0:k0 + blocks, x:x + P].bitcast(F32), ALU.subtract).then_inc(p_lo, 1)

            nc.vector.memset(pT0[:, :, 3, 2 * P:3 * P].bitcast(F32), 0.0).then_inc(zeroed, 1)
            nc.vector.memset(pT1[:, :, 7, 2 * P:3 * P].bitcast(F32), 0.0).then_inc(zeroed, 1)
            for e in range(2):
                split_queries_lo(e, e + 1)

            def body(r):
                for job, n, s in r.jobs(DVE_STEP):
                    if job == "M":
                        maxima(r.it, s, n)
                    elif job == "P":
                        divide(r.it, s, n)
                    elif job == "T":
                        split_lo(r.it, s, n)
                    elif job == "H":
                        query_hi(s, n, r.it * 8 + 2 * s + n)
                    elif job == "F":
                        split_queries_lo(s - 2, r.it * 2 + 2 + s - 1)
            rounds(dve, body)

        @block.gpsimd
        def _(pool):
            def rope(s, ch, number, count):
                x = slice(ch * CHUNK, (ch + 1) * CHUNK)
                pool.wait_ge(m_free, count + 1)
                nc.gpsimd.tensor_tensor(rot[64:128, 0, :], qf[64:128, ch, :], cosT[64:128, x], ALU.mult).then_inc(rope_parts, 1)
                pool.wait_ge(rope_parts, number * 3 + 1)
                nc.gpsimd.tensor_tensor(rot[64:96, 1, :], qf[96:128, ch, :], sinT[96:128, x], ALU.mult).then_inc(rope_parts, 1)
                pool.wait_ge(rope_parts, number * 3 + 2)
                nc.gpsimd.tensor_tensor(rot[96:128, 1, :], qf[64:96, ch, :], sinT[64:96, x], ALU.mult).then_inc(rope_parts, 1)
                pool.wait_ge(rope_parts, number * 3 + 3)
                nc.gpsimd.tensor_tensor(qf[64:128, ch, :], rot[64:128, 0, :], rot[64:128, 1, :], ALU.add).then_inc(roped, 1)
                pool.wait_ge(q_hi, number + 1)
                nc.gpsimd.tensor_tensor(q[:, s % 2, LO, x], qf[:, ch, :], q[:, s % 2, HI, x].bitcast(F32), ALU.subtract).then_inc(q_lo, 1)

            def join(it, s, ch):
                e = s % 2
                pool.wait_ge(copied, it * 8 + 2 * s + ch + 1)
                if later(it * 4 + s, 2):
                    pool.wait_ge(o_stored[e][ch], it * 32 + 16 * (s // 2))
                nc.gpsimd.tensor_tensor(o_sum[KVR * e:KVR * e + KVR, ch, :], o_parts[:, ch, 0, :], o_parts[:, ch, 1, :],
                                        ALU.add).then_inc(joined, 1)

            pool.wait_ge(tab_in, 32)

            def body(r):
                jobs = list(r.jobs(POOL_STEP))
                job, n, s = list(STEADY.jobs(POOL_STEP))[-1]
                before = None if r.first else (job, n, s - 4)
                for job, n, s in jobs:
                    if before:
                        pool.wait_ge(q_lo if before[0] == "Q" else joined, r.it * 8 + 2 * before[2] + before[1] + 1)
                    before = job, n, s
                    if job == "Q":
                        rope(s, n, r.it * 8 + 2 * s + n, r.use(job, n, s))
                    elif job == "V":
                        join(r.it, s, n)
            rounds(pool, body)



def output_phase(nc, src_d, dst_d, oT_d, wvo_d):
    with ExitStack() as stack:
        c = Ctx(nc, stack)
        w_in = c.sb("o_w_in", [P, SLOTS, D])
        w = c.sb("o_w", [P, 2, PAIRS, D], F32R)
        o_in = c.sb("o_in", [P, PAIRS, P])
        o = c.sb("o_o", [P, 2, 2, PAIRS, P], F32R)
        x_in = c.sb("o_x_in", [P, 2, D])
        y = c.sb("o_y", [P, 2, D])
        psy = c.ps("o_psy", [P, 2, 2, BANK])
        w_loaded = [c.sem(f"o_w_loaded{j}") for j in range(SLOTS)]
        w_hi, w_lo = c.sem("o_w_hi"), c.sem("o_w_lo")
        o_loaded, o_hi, o_lo = c.sem("o_loaded"), c.sem("o_hi"), c.sem("o_lo")
        x_loaded = [c.sem(f"o_x_loaded{j}") for j in range(2)]
        product, result = c.sem("o_product"), c.sem("o_result")
        stored = [c.sem(f"o_y_stored{j}") for j in range(2)]
        block = stack.enter_context(nc.Block())
        oT_v = oT_d.rearrange("(a p) t -> p a t", p=P)

        @block.sync
        def _(sp):
            sp.dma_start(o_in[:], oT_v[:, :, 0:P]).then_inc(o_loaded, 16)
            for pair in range(PAIRS):
                if pair >= SLOTS:
                    sp.wait_ge(w_lo, pair - SLOTS + 1)
                sp.dma_start(w_in[:, pair % SLOTS, :], wvo_d[pair * P:(pair + 1) * P, :]).then_inc(w_loaded[pair % SLOTS], 16)
                if pair == 1:
                    sp.wait_ge(o_lo, 1)
                    sp.dma_start(o_in[:], oT_v[:, :, P:2 * P]).then_inc(o_loaded, 16)

            def step(n, j, has):
                if has(1) and later(n, 1):
                    sp.wait_ge(o_lo, n + 1)
                    sp.dma_start(o_in[:], oT_v[:, :, bass.ds((n + 1) * P, P)]).then_inc(o_loaded, 16)
                if has(0):
                    if later(n, 2):
                        sp.wait_ge(result, n * 2 - 2)
                    sp.dma_start(x_in[:, j, :], src_d[bass.ds(n * P, P), :]).then_inc(x_loaded[j], 16)
                if has(-1):
                    sp.wait_ge(result, n * 2)
                    jm = (j + 1) % 2
                    sp.dma_start(dst_d[bass.ds((n - 1) * P, P), :], y[:, jm, :]).then_inc(stored[jm], 16)
            output_steps(sp, step)
            for j in range(2):
                sp.wait_ge(stored[j], 16 * NT // 2)

        @block.scalar
        def _(act):
            for pair in range(PAIRS):
                if pair in (0, 2):
                    tile = pair // 2
                    act.wait_ge(o_loaded, 16 * (tile + 1))
                    nc.scalar.activation(o[:, tile, HI, :, :], o_in[:], ACT.Copy).then_inc(o_hi, 1)
                act.wait_ge(w_loaded[pair % SLOTS], 16 * (pair // SLOTS + 1))
                nc.scalar.activation(w[:, HI, pair, :], w_in[:, pair % SLOTS, :], ACT.Copy).then_inc(w_hi, 1)

            def step(n, j, has):
                if has(1) and later(n, 1):
                    jm = (j + 1) % 2
                    act.wait_ge(o_loaded, (n + 2) * 16)
                    act.wait_ge(product, n * 2)
                    nc.scalar.activation(o[:, jm, HI, :, :], o_in[:], ACT.Copy).then_inc(o_hi, 1)
            output_steps(act, step)

        @block.vector
        def _(dve):
            for pair in range(PAIRS):
                if pair in (0, 2):
                    tile = pair // 2
                    dve.wait_ge(o_hi, tile + 1)
                    nc.vector.tensor_tensor(o[:, tile, LO, :, :], o_in[:], o[:, tile, HI, :, :].bitcast(F32), ALU.subtract).then_inc(o_lo, 1)
                dve.wait_ge(w_hi, pair + 1)
                nc.vector.tensor_tensor(w[:, LO, pair, :], w_in[:, pair % SLOTS, :], w[:, HI, pair, :].bitcast(F32), ALU.subtract).then_inc(w_lo, 1)

            def step(n, j, has):
                if has(1) and later(n, 1):
                    jm = (j + 1) % 2
                    dve.wait_ge(o_hi, n + 2)
                    nc.vector.tensor_tensor(o[:, jm, LO, :, :], o_in[:], o[:, jm, HI, :, :].bitcast(F32), ALU.subtract).then_inc(o_lo, 1)
                if has(0):
                    dve.wait_ge(x_loaded[j], loads_of(n, j))
                    if later(n, 2):
                        dve.wait_ge(stored[j], (n - j) * 8)
                    for half in range(2):
                        x = slice(half * BANK, (half + 1) * BANK)
                        dve.wait_ge(product, n * 2 + half + 1)
                        nc.vector.tensor_tensor(y[:, j, x], psy[:, j, half, :], x_in[:, j, x], ALU.add).then_inc(result, 1)
            output_steps(dve, step)

        @block.tensor
        def _(pe):
            for pair in range(PAIRS):
                for tile in range(2):
                    pe.wait_ge(o_lo, tile + 1)
                    pe.wait_ge(w_lo, pair + 1)
                    for half in range(2):
                        for i, (a, m) in enumerate(PASSES):
                            ins = nc.tensor.matmul(psy[:, tile, half, :], o[:, tile, a, pair, :], w[:, m, pair, half * BANK:(half + 1) * BANK],
                                                   start=(pair == 0 and i == 0), stop=(pair == PAIRS - 1 and i == 2))
                        if pair == PAIRS - 1:
                            ins.then_inc(product, 1)

            def step(n, j, has):
                if has(0) and later(n, 2):
                    pe.wait_ge(o_lo, n + 1)
                    pe.wait_ge(result, n * 2 - 2)
                    for half in range(2):
                        for pair in range(PAIRS):
                            for i, (a, m) in enumerate(PASSES):
                                ins = nc.tensor.matmul(psy[:, j, half, :], o[:, j, a, pair, :], w[:, m, pair, half * BANK:(half + 1) * BANK],
                                                       start=(pair == 0 and i == 0), stop=(pair == PAIRS - 1 and i == 2))
                        ins.then_inc(product, 1)
            output_steps(pe, step)


def output_steps(eng, step):
    steady(eng, step, NT, 1, 1, start=0)



def macaron_block(nc, x, wa, lnw, wn, wpe, wv, wo, cos, sin, cosT, sinT, w, bias, lora_a, lora_b, starts, out):
    x1_d = nc.dram_tensor("x1", (T, D), F32).ap()
    x2_d = nc.dram_tensor("x2", (T, D), F32).ap()
    oT_d = nc.dram_tensor("oT", (PAIRS * P, T), F32).ap()
    wvo_d = nc.dram_tensor("wvo_fold", (PAIRS * P, D), F32).ap()
    sum_d = nc.dram_tensor("w_sum", (PIECES * P, D), F32).ap()
    with ExitStack() as stack:
        c = Ctx(nc, stack)
        k = Shared()
        k.ident = c.sb("ident", [P, P])
        k.ident_bf = c.sb("ident_bf", [P, P], BF16)
        k.mask_bf = c.sb("mask_bf", [P, P], BF16)
        k.eps_ln = c.sb("eps_ln", [P, 1])
        k.eps_rms = c.sb("eps_rms", [P, 1])
        constants_phase(nc, k)
        with ExitStack() as inner:
            ci = Ctx(nc, inner)
            a_st = ci.sb("a_st", [P, B, D], F32R)
            b_st = ci.sb("b_st", [P, B, D], F32R)
            adapters_phase(nc, a_st, b_st, (lora_a, lora_b, starts))
            ffn_phase(nc, "f1_", k, x, x1_d, bias, sum_d, w, a_st, b_st)
        with ExitStack() as inner:
            ci = Ctx(nc, inner)
            k.qnT = ci.sb("qnT", [P, 2, QRT, T], F32R)
            k.keyT = ci.sb("keyT", [P, 2, T], F32R)
            k.val = ci.sb("val", [P, NT, 2 * KVR], F32R)
            latents_phase(nc, k, x1_d, (wa, lnw, cos, sin))
            attention_phase(nc, k, (wn, wpe, wv, wo, cosT, sinT), oT_d, wvo_d)
        output_phase(nc, x1_d, x2_d, oT_d, wvo_d)
        ffn_phase(nc, "f2_", k, x2_d, out, bias, sum_d)


class Shared:
    pass


def rope_tables():
    import math
    dim, base, factor, beta_fast, beta_slow, orig_max = ROPE, 10000.0, 128.0, 32.0, 1.0, 2048

    def corr_dim(r):
        return dim * math.log(orig_max / (r * 2 * math.pi)) / (2 * math.log(base))
    low = max(math.floor(corr_dim(beta_fast)), 0)
    high = min(math.ceil(corr_dim(beta_slow)), dim - 1)
    hi = high + 0.001 if low == high else float(high)
    ramp = np.clip((np.arange(dim // 2, dtype=np.float32) - low) / (hi - low), 0.0, 1.0)
    keep = 1.0 - ramp
    freq_extra = 1.0 / base ** (np.arange(0, dim, 2, dtype=np.float32) / dim)
    freq_inter = freq_extra / factor
    inv_freq = freq_inter * (1.0 - keep) + freq_extra * keep
    freqs = np.outer(np.arange(S, dtype=np.float32), inv_freq)
    emb = np.concatenate([freqs, freqs], axis=-1)
    sign = np.where(np.arange(ROPE) < ROPE // 2, -1.0, 1.0)
    return np.cos(emb).astype(np.float32), (np.sin(emb) * sign).astype(np.float32)


def kernel(**inputs):
    import numpy as _np
    import concourse.bacc as _bacc
    from concourse import mybir as _mybir
    from concourse.bass_utils import run_bass_kernel_spmd as _run

    get = lambda name: _np.asarray(inputs[name])
    wq_b = get("L0_attn_wq_b").reshape(PAIRS, 2, QHD, QR)
    wkv_b = get("L0_attn_wkv_b").reshape(PAIRS, 2, NOPE + VD, KVR)
    wkv_a = get("L0_attn_wkv_a")
    halves = _np.concatenate([_np.arange(0, ROPE, 2), _np.arange(1, ROPE, 2)])
    cos, sin = rope_tables()
    blank = _np.zeros((NOPE, S), _np.float32)
    blank_rows = _np.zeros((32 - RANK, ADAPTERS, D), _np.float32)
    data = {
        "x": get("L0_attn_x").reshape(T, D),
        "wa": _np.concatenate([get("L0_attn_wq_a"), wkv_a[:KVR], wkv_a[KVR:][halves]], 0).T.reshape(DT, P, LAT).transpose(1, 0, 2).reshape(P, DT * LAT),
        "lnw": _np.concatenate([get("L0_attn_q_a_ln_w"), get("L0_attn_kv_a_ln_w")]),
        "wn": _np.concatenate([wq_b[:, :, :NOPE], wkv_b[:, :, :NOPE]], 3).transpose(0, 2, 1, 3).reshape(PAIRS, NOPE, 2 * (QR + KVR)),
        "wpe": wq_b[:, :, NOPE:][:, :, halves].reshape(PAIRS, 2, ROPE, QRT, P).transpose(0, 4, 1, 3, 2).reshape(PAIRS, P, 2 * QRT * ROPE),
        "wv": wkv_b[:, :, NOPE:].transpose(0, 2, 1, 3).reshape(PAIRS, VD, 2 * KVR),
        "wo": get("L0_attn_wo").T.reshape(PAIRS, 2, VD, D).transpose(0, 2, 1, 3).reshape(PAIRS, VD, 2 * D),
        "cos": _np.concatenate([cos, cos], 0), "sin": _np.concatenate([sin, sin], 0),
        "cosT": _np.concatenate([blank, cos.T], 0),
        "sinT": _np.concatenate([blank, sin.T[ROPE // 2:], sin.T[:ROPE // 2]], 0),
        "w": get("L0_ffn_weight").T.reshape(DT, P, D).transpose(1, 0, 2).reshape(P, DT * D),
        "bias": get("L0_ffn_bias"),
        "lora_a": _np.concatenate([get("L0_ffn_lora_A").transpose(1, 0, 2), blank_rows], 0),
        "lora_b": _np.concatenate([get("L0_ffn_lora_B").transpose(2, 0, 1), blank_rows], 0),
        "starts": get("L0_ffn_lora_start_indices"),
    }
    nc = _bacc.Bacc("TRN2", target_bir_lowering=False, num_devices=1)
    arrays, args = {}, []
    for name, a in data.items():
        a = _np.ascontiguousarray(a)
        arrays[f"in_{name}"] = a
        args.append(nc.dram_tensor(f"in_{name}", a.shape, _mybir.dt.from_np(a.dtype), kind="ExternalInput").ap())
    args.append(nc.dram_tensor("out_0", (T, D), F32, kind="ExternalOutput").ap())
    macaron_block(nc, *args)
    r = _run(nc, [arrays], core_ids=[0])
    return r.results[0]["out_0"].reshape(B, S, D)
```
